# Optimizing a Trainium2 kernel written in Bass

```python
import numpy as np
import jax
import jax.numpy as jnp

def _softmax(x, axis=-1):
    return jax.nn.softmax(x, axis=axis)

def _gelu(x):
    return jax.nn.gelu(x, approximate=True)

def _silu(x):
    return jax.nn.silu(x)

def _sigmoid(x):
    return jax.nn.sigmoid(x)

def _layernorm(x, axis=-1, eps=1e-05):
    m = jnp.mean(x, axis=axis, keepdims=True)
    v = jnp.var(x, axis=axis, keepdims=True)
    return (x - m) / jnp.sqrt(v + eps)

def _scatter_add(tgt, idx, src, axis=0):
    return tgt.at[idx].add(src)

def _segment_sum(src, seg, n):
    return jax.ops.segment_sum(src, seg, n)
kernel_name = 'mk_gps_d1_gnn_r8_a7daae'

def setup_inputs(seed: int=0):
    np.random.seed(seed)
    _w = jnp.asarray

    def _rec_inputs():
        import jax
        import jax.numpy as jnp
        _gk = jax.random.key(seed)
        x = -0.0001126 + 1 * jax.random.normal(jax.random.fold_in(_gk, 1), (1250, 768), jnp.float32)
        src = jax.random.randint(jax.random.fold_in(_gk, 2), (20000,), 0, 1250, jnp.int32)
        dst = jax.random.randint(jax.random.fold_in(_gk, 3), (20000,), 0, 1250, jnp.int32)
        _o = jnp.argsort(dst, stable=True)
        src = src[_o]
        dst = dst[_o]
        return (x, src, dst)
    x, src, dst = _rec_inputs()

    def _L0_gnn_setup():
        import jax, jax.numpy as jnp
        import numpy as np
        N = 1250
        E = 20000
        D = 768
        H1, C1 = (4, 192)
        H2, C2 = (2, 96)
        EPS = 1e-05
        NEG_SLOPE = 0.2

        def layer_norm(x, g, b):
            mu = x.mean(-1, keepdims=True)
            var = ((x - mu) ** 2).mean(-1, keepdims=True)
            return (x - mu) * jax.lax.rsqrt(var + EPS) * g + b

        def gat_conv(x, src, dst, W, a_src, a_dst, bias, H, C, n):
            h = (x @ W).reshape(n, H, C)
            s_src = (h * a_src).sum(-1)
            s_dst = (h * a_dst).sum(-1)
            e = jax.nn.leaky_relu(s_src[src] + s_dst[dst], NEG_SLOPE)
            emax = jax.ops.segment_max(e, dst, num_segments=n)
            ee = jnp.exp(e - emax[dst])
            denom = jax.ops.segment_sum(ee, dst, num_segments=n)
            alpha = ee / denom[dst]
            out = jax.ops.segment_sum(alpha[:, :, None] * h[src], dst, num_segments=n)
            return out.reshape(n, H * C) + bias
        key = jax.random.key(seed)
        ks = jax.random.split(key, 16)
        sd = 1.0 / np.sqrt(D)
        inp = {'x': jax.random.normal(ks[0], (N, D), jnp.float32), 'edge_index': jax.random.randint(ks[1], (2, E), 0, N, jnp.int64), 'norm_g': jnp.ones((D,), jnp.float32), 'norm_b': jnp.zeros((D,), jnp.float32), 'W1': jax.random.normal(ks[2], (D, H1 * C1), jnp.float32) * sd, 'a_src1': jax.random.normal(ks[3], (H1, C1), jnp.float32) * sd, 'a_dst1': jax.random.normal(ks[4], (H1, C1), jnp.float32) * sd, 'b1': jnp.zeros((H1 * C1,), jnp.float32), 'W2': jax.random.normal(ks[5], (H1 * C1, H2 * C2), jnp.float32) * sd, 'a_src2': jax.random.normal(ks[6], (H2, C2), jnp.float32) * sd, 'a_dst2': jax.random.normal(ks[7], (H2, C2), jnp.float32) * sd, 'b2': jnp.zeros((H2 * C2,), jnp.float32), 'Wu': jax.random.normal(ks[8], (D + H2 * C2, D), jnp.float32) / np.sqrt(D + H2 * C2), 'bu': jnp.zeros((D,), jnp.float32)}
        return inp
    _L0_gnn_all = _L0_gnn_setup()
    _L0_gnn_in = {k: v for k, v in _L0_gnn_all.items() if k in ('norm_g', 'norm_b', 'W1', 'a_src1', 'a_dst1', 'b1', 'W2', 'a_src2', 'a_dst2', 'b2', 'Wu', 'bu')}
    del _L0_gnn_all

    def _L0_mix_setup():
        import jax, jax.numpy as jnp
        import numpy as np
        NUM_HEADS = 12

        def _reference_tuple_inner(x, w_qkv, w_proj, b_proj):
            B, S, E = x.shape
            H = NUM_HEADS
            D = E // H
            qkv = (x @ w_qkv).reshape(B, S, 3, H, D).transpose(2, 0, 3, 1, 4)
            q, k, v = (qkv[0], qkv[1], qkv[2])
            q = jax.nn.elu(q) + 1.0
            k = jax.nn.elu(k) + 1.0
            kv = jnp.einsum('bhsd,bhse->bhde', k, v)
            k_sum = jnp.sum(k, axis=-2)
            z = 1.0 / jnp.einsum('bhsd,bhd->bhs', q, k_sum)
            out = jnp.einsum('bhsd,bhde->bhse', q, kv) * z[..., None]
            out = out.transpose(0, 2, 1, 3).reshape(B, S, E)
            out = out @ w_proj + b_proj
            return (out, kv)
        key = jax.random.key(seed)
        k1, k2, k3 = jax.random.split(key, 3)
        B, S, E = (8, 512, 768)
        x = jax.random.normal(k1, (B, S, E), dtype=jnp.float32)
        w_qkv = jax.random.normal(k2, (E, 3 * E), dtype=jnp.float32) * 0.02
        w_proj = jax.random.normal(k3, (E, E), dtype=jnp.float32) * 0.02
        b_proj = jnp.zeros((E,), dtype=jnp.float32)
        return {'x': x, 'w_qkv': w_qkv, 'w_proj': w_proj, 'b_proj': b_proj}
    _L0_mix_all = _L0_mix_setup()
    _L0_mix_in = {k: v for k, v in _L0_mix_all.items() if k in ('w_qkv', 'w_proj', 'b_proj')}
    del _L0_mix_all

    def _L0_ffn_setup():
        import jax, jax.numpy as jnp
        import numpy as np
        B, S, D = (4, 1024, 768)
        E = 8
        H = 768
        HS = 384
        TOPK_ROUTED = 2
        key = jax.random.key(seed)
        ks = jax.random.split(key, 10)
        w = lambda k, shape: jax.random.normal(k, shape, dtype=jnp.float32) * 0.02
        return {'x': jax.random.normal(ks[0], (B, S, D), dtype=jnp.float32), 'router_w': w(ks[1], (D, E)), 'w_gate': w(ks[2], (E, D, H)), 'w_up': w(ks[3], (E, D, H)), 'w_down': w(ks[4], (E, H, D)), 'ws_gate': w(ks[5], (D, HS)), 'ws_up': w(ks[6], (D, HS)), 'ws_down': w(ks[7], (HS, D)), 'sg_w': w(ks[8], (D, 1)), 'sg_b': jnp.zeros((1,), jnp.float32)}
    _L0_ffn_all = _L0_ffn_setup()
    _L0_ffn_in = {k: v for k, v in _L0_ffn_all.items() if k in ('router_w', 'w_gate', 'w_up', 'w_down', 'ws_gate', 'ws_up', 'ws_down', 'sg_w', 'sg_b')}
    del _L0_ffn_all
    return {'x': x, 'src': src, 'dst': dst, 'L0_gnn_norm_g': _L0_gnn_in['norm_g'], 'L0_gnn_norm_b': _L0_gnn_in['norm_b'], 'L0_gnn_W1': _L0_gnn_in['W1'], 'L0_gnn_a_src1': _L0_gnn_in['a_src1'], 'L0_gnn_a_dst1': _L0_gnn_in['a_dst1'], 'L0_gnn_b1': _L0_gnn_in['b1'], 'L0_gnn_W2': _L0_gnn_in['W2'], 'L0_gnn_a_src2': _L0_gnn_in['a_src2'], 'L0_gnn_a_dst2': _L0_gnn_in['a_dst2'], 'L0_gnn_b2': _L0_gnn_in['b2'], 'L0_gnn_Wu': _L0_gnn_in['Wu'], 'L0_gnn_bu': _L0_gnn_in['bu'], 'L0_mix_w_qkv': _L0_mix_in['w_qkv'], 'L0_mix_w_proj': _L0_mix_in['w_proj'], 'L0_mix_b_proj': _L0_mix_in['b_proj'], 'L0_ffn_router_w': _L0_ffn_in['router_w'], 'L0_ffn_w_gate': _L0_ffn_in['w_gate'], 'L0_ffn_w_up': _L0_ffn_in['w_up'], 'L0_ffn_w_down': _L0_ffn_in['w_down'], 'L0_ffn_ws_gate': _L0_ffn_in['ws_gate'], 'L0_ffn_ws_up': _L0_ffn_in['ws_up'], 'L0_ffn_ws_down': _L0_ffn_in['ws_down'], 'L0_ffn_sg_w': _L0_ffn_in['sg_w'], 'L0_ffn_sg_b': _L0_ffn_in['sg_b']}

def reference(x, src, dst, L0_gnn_norm_g, L0_gnn_norm_b, L0_gnn_W1, L0_gnn_a_src1, L0_gnn_a_dst1, L0_gnn_b1, L0_gnn_W2, L0_gnn_a_src2, L0_gnn_a_dst2, L0_gnn_b2, L0_gnn_Wu, L0_gnn_bu, L0_mix_w_qkv, L0_mix_w_proj, L0_mix_b_proj, L0_ffn_router_w, L0_ffn_w_gate, L0_ffn_w_up, L0_ffn_w_down, L0_ffn_ws_gate, L0_ffn_ws_up, L0_ffn_ws_down, L0_ffn_sg_w, L0_ffn_sg_b):
    import jax
    import jax.numpy as jnp

    def _L0_gnn_ref(x, edge_index, norm_g, norm_b, W1, a_src1, a_dst1, b1, W2, a_src2, a_dst2, b2, Wu, bu):
        import jax, jax.numpy as jnp
        import numpy as np
        N = 1250
        E = 20000
        D = 768
        H1, C1 = (4, 192)
        H2, C2 = (2, 96)
        EPS = 1e-05
        NEG_SLOPE = 0.2

        def layer_norm(x, g, b):
            mu = x.mean(-1, keepdims=True)
            var = ((x - mu) ** 2).mean(-1, keepdims=True)
            return (x - mu) * jax.lax.rsqrt(var + EPS) * g + b

        def gat_conv(x, src, dst, W, a_src, a_dst, bias, H, C, n):
            h = (x @ W).reshape(n, H, C)
            s_src = (h * a_src).sum(-1)
            s_dst = (h * a_dst).sum(-1)
            e = jax.nn.leaky_relu(s_src[src] + s_dst[dst], NEG_SLOPE)
            emax = jax.ops.segment_max(e, dst, num_segments=n)
            ee = jnp.exp(e - emax[dst])
            denom = jax.ops.segment_sum(ee, dst, num_segments=n)
            alpha = ee / denom[dst]
            out = jax.ops.segment_sum(alpha[:, :, None] * h[src], dst, num_segments=n)
            return out.reshape(n, H * C) + bias
        loops = jnp.arange(N, dtype=edge_index.dtype)
        src = jnp.concatenate([edge_index[0], loops])
        dst = jnp.concatenate([edge_index[1], loops])
        x_norm = layer_norm(x, norm_g, norm_b)
        out1 = gat_conv(x_norm, src, dst, W1, a_src1, a_dst1, b1, H1, C1, N)
        out2 = gat_conv(out1, src, dst, W2, a_src2, a_dst2, b2, H2, C2, N)
        combined = jnp.concatenate([x, out2], axis=-1)
        return combined @ Wu + bu

    def _L0_mix_ref(x, w_qkv, w_proj, b_proj):
        import jax, jax.numpy as jnp
        import numpy as np
        NUM_HEADS = 12

        def _reference_tuple_inner(x, w_qkv, w_proj, b_proj):
            B, S, E = x.shape
            H = NUM_HEADS
            D = E // H
            qkv = (x @ w_qkv).reshape(B, S, 3, H, D).transpose(2, 0, 3, 1, 4)
            q, k, v = (qkv[0], qkv[1], qkv[2])
            q = jax.nn.elu(q) + 1.0
            k = jax.nn.elu(k) + 1.0
            kv = jnp.einsum('bhsd,bhse->bhde', k, v)
            k_sum = jnp.sum(k, axis=-2)
            z = 1.0 / jnp.einsum('bhsd,bhd->bhs', q, k_sum)
            out = jnp.einsum('bhsd,bhde->bhse', q, kv) * z[..., None]
            out = out.transpose(0, 2, 1, 3).reshape(B, S, E)
            out = out @ w_proj + b_proj
            return (out, kv)
        return _reference_tuple_inner(x, w_qkv, w_proj, b_proj)[0]

    def _L0_ffn_ref(x, router_w, w_gate, w_up, w_down, ws_gate, ws_up, ws_down, sg_w, sg_b):
        import jax, jax.numpy as jnp
        import numpy as np
        B, S, D = (4, 1024, 768)
        E = 8
        H = 768
        HS = 384
        TOPK_ROUTED = 2
        probs = jax.nn.softmax(x @ router_w, axis=-1)
        gates, idx = jax.lax.top_k(probs, TOPK_ROUTED)
        gates = gates / jnp.sum(gates, axis=-1, keepdims=True)
        n_exp = router_w.shape[1]
        dense_g = jnp.sum(jax.nn.one_hot(idx, n_exp, dtype=x.dtype) * gates[..., None], axis=-2)
        g = jax.nn.silu(jnp.einsum('bsd,edh->bseh', x, w_gate))
        u = jnp.einsum('bsd,edh->bseh', x, w_up)
        expert_out = jnp.einsum('bseh,ehd->bsed', g * u, w_down)
        routed = jnp.einsum('bse,bsed->bsd', dense_g, expert_out)
        shared = jax.nn.silu(x @ ws_gate) * (x @ ws_up) @ ws_down
        alpha = jax.nn.sigmoid(x @ sg_w + sg_b)
        return alpha * shared + (1.0 - alpha) * routed
    edge_index = jnp.stack([src, dst])
    xn = _layernorm(x, axis=-1)
    x = x + _L0_gnn_ref(xn, edge_index, L0_gnn_norm_g, L0_gnn_norm_b, L0_gnn_W1, L0_gnn_a_src1, L0_gnn_a_dst1, L0_gnn_b1, L0_gnn_W2, L0_gnn_a_src2, L0_gnn_a_dst2, L0_gnn_b2, L0_gnn_Wu, L0_gnn_bu) + _L0_mix_ref(xn[None], L0_mix_w_qkv, L0_mix_w_proj, L0_mix_b_proj)[0]
    x = x + _L0_ffn_ref(_layernorm(x, axis=-1)[None], L0_ffn_router_w, L0_ffn_w_gate, L0_ffn_w_up, L0_ffn_w_down, L0_ffn_ws_gate, L0_ffn_ws_up, L0_ffn_ws_down, L0_ffn_sg_w, L0_ffn_sg_b)[0]
    return x

_drawn_inputs = setup_inputs


def setup_inputs(seed=0):
    import zlib

    import numpy as np

    out = dict(_drawn_inputs(seed))
    spreads = {'L0_gnn_norm_g': (1.0, 0.6),
     'L0_gnn_norm_b': (0.0, 0.1),
     'L0_gnn_b1': (0.0, 0.1),
     'L0_gnn_b2': (0.0, 0.1),
     'L0_gnn_bu': (0.0, 0.1),
     'L0_mix_b_proj': (0.0, 0.1)}
    factors = {'L0_gnn_a_src1': 4.553,
     'L0_gnn_a_dst1': 8.0,
     'L0_gnn_a_src2': 8.0,
     'L0_gnn_a_dst2': 8.0,
     'L0_mix_w_qkv': 8.0,
     'L0_mix_w_proj': 8.0,
     'L0_ffn_sg_w': 6.052}
    for name, (base, spread) in spreads.items():
        noise = np.random.default_rng([zlib.crc32(name.encode()), seed]).standard_normal(out[name].shape)
        drawn = base * np.exp(spread * noise) if base else spread * noise
        out[name] = jnp.asarray(drawn.astype(out[name].dtype))
    for name, factor in factors.items():
        out[name] = (out[name] * factor).astype(out[name].dtype)
    return out
```

```python
from contextlib import ExitStack

import concourse.bass as bass
from concourse import mybir

F32 = mybir.dt.float32
BF16 = mybir.dt.bfloat16
F16 = mybir.dt.float16
I32 = mybir.dt.int32
U32 = mybir.dt.uint32
ALU = mybir.AluOpType
ACT = mybir.ActivationFunctionType
AX = mybir.AxisListType

P = 128
EPS = 1e-5
SLOPE = 0.2
MASKED = -1.0e30
ARENA = 52900
SMALL = 3420


class Handoff:

    def __init__(self, ready, freed, slots, first=0):
        self.ready, self.freed, self.slots, self.first = ready, freed, slots, first

    def after(self, jobs):
        assert jobs % 2 == 0
        return Handoff(self.ready, self.freed, self.slots, self.first + jobs)

    def wait_free(self, pe, q):
        if q >= self.slots:
            p = self.first + q - self.slots
            pe.wait_ge(self.freed[p % 2], p // 2 + 1)

    def filled(self, ins):
        ins.then_inc(self.ready, 1)

    def wait_filled(self, eng, q):
        eng.wait_ge(self.ready, self.first + q + 1)

    def taken(self, ins, q):
        ins.then_inc(self.freed[q % 2], 1)

    def wait_all_taken(self, eng, n):
        eng.wait_ge(self.freed[0], (self.first + n) // 2)
        eng.wait_ge(self.freed[1], (self.first + n) // 2)


class Chain:

    def __init__(self, eng, sem):
        self.eng, self.sem, self.n = eng, sem, 0

    def __call__(self, ins):
        ins.then_inc(self.sem, 1)
        self.n += 1
        return ins

    def wait(self, but=0):
        if self.n > but:
            self.eng.wait_ge(self.sem, self.n - but)


def gps_layer(nc, x, src, dst, norm_g, norm_b, W1, a_src1, a_dst1, b1, W2, a_src2, a_dst2, b2, Wu, bu,
              w_qkv, w_proj, b_proj, router_w, w_gate, w_up, w_down, ws_gate, ws_up, ws_down, sg_w, sg_b,
              out):
    N, D = x.shape
    KD = D // P
    NT = 10
    T = N // NT
    E = src.shape[0]
    EC = E // T
    H1, C1 = a_src1.shape
    H2, C2 = a_src2.shape
    NH = 12
    DG = 3
    G = -(-N // DG)
    NBK = NT * DG
    CW = DG * G
    NCH = (E + NBK * (P - 1)) // P
    NCH += NCH % 2
    SRS = 512
    NE = router_w.shape[1]
    HS = ws_gate.shape[1]
    NTM = (2 * N + NE * (P - 1)) // P
    assert T * NT == N and T * EC == E and T <= P and G <= 512 and NTM % 2 == 1
    NG = [(i * G, min(G, N - i * G)) for i in range(DG)]

    with ExitStack() as ctx:
        def sem(name):
            return ctx.enter_context(nc.semaphore(name))

        arena = ctx.enter_context(nc.sbuf_tensor("arena", [P, ARENA], F32))
        ps = [ctx.enter_context(nc.psum_tensor(f"bank{i}", [P, 512], F32)) for i in range(8)]

        def words(off, n, dt=F32):
            v = arena[:, off:off + n]
            return v if dt == F32 else v.bitcast(dt)

        small_at = [0]

        def small(n, dt=F32):
            w = n if dt in (F32, I32, U32) else (n + 1) // 2
            v = words(small_at[0], w, dt)
            small_at[0] += w
            assert small_at[0] <= SMALL, small_at
            return v

        ident = small(P)
        ones = small(P)
        route0 = small_at[0]
        zeros = small(D)
        iota_i = small(G, I32)
        route1 = small_at[0]
        ones_b = small(P, BF16)
        tri = small(P, BF16)
        triinc = small(P, BF16)
        later = small(EC, BF16)
        iota = small(G)
        iota_h = small(G + 1, F16)
        epst = small(1)
        stats = small(NT * 12).rearrange("p (t s) -> p t s", t=NT)
        mv = small(NT * 2).rearrange("p (t s) -> p t s", t=NT)
        std = small(NT)
        rstd = small(NT)
        gcol = small(KD)
        bcol = small(KD)
        b1col = small(KD)
        b2col = small(2)
        s1 = small(NT * 8).rearrange("p (t h s a) -> p t h s a", t=NT, h=2, s=2)
        s2 = small(NT * 4).rearrange("p (t s a) -> p t s a", t=NT, s=2)
        smax = small(NT)
        zt = small(NT)
        mt = small(NT)
        arow = small(NT)
        brow = small(NT)
        s02 = small(NT)
        rec = small(NT)
        slot_i = small(EC, I32)
        edge_v = small(EC, I32)
        bucket_row = small(NCH)
        offs_i = small(NCH, I32)
        junk8 = small(8)

        A0 = SMALL
        B0 = A0 + NT * D
        C0 = B0 + NT * D
        D0 = C0 + KD * N
        E0 = D0 + KD * N
        F0 = E0 + 776 * KD
        G0 = F0 + 4 * 193 * NT
        assert G0 + 6700 <= ARENA

        x_rows = x.rearrange("(t p) d -> p t d", p=T)
        out_rows = out.rearrange("(t p) d -> p t d", p=T)

        def scratch(name, shape, dt):
            return nc.dram_tensor(name, shape, dt, kind="Internal").ap()

        edge_table = scratch("edge_table", [P * NCH, 1], I32)
        mixed_dram = scratch("mixed_rows", [N, D], F32)
        xg_dram = scratch("expert_in", [NTM * P, D], F32)
        yg_dram = scratch("expert_out", [NTM * P, D], F32)

        s_const = sem("const_ready")
        s_iota = sem("iota_step")
        s_edges = sem("edges_in")
        s_gb = sem("gain_bias_in")
        s_x = [sem(f"x_in{g}") for g in range(5)]
        s_avec = sem("avec_in")
        s_w1 = sem("w1_in")
        s_stats = sem("ln_stats")
        s_std = sem("ln_std")
        s_xn = sem("xn_ready")
        s_oh = sem("edge_onehot")
        s_tot = sem("edge_totals")
        s_br = sem("edge_base_ready")
        s_cnt = sem("bucket_counts")
        s_chunks = sem("bucket_chunks")
        s_starts = sem("bucket_starts")
        s_startrow = sem("start_row")
        s_cmp = sem("chunk_cmp")
        s_bk = sem("chunk_bucket")
        s_rank = sem("rank_ready")
        s_rankfree = sem("rank_taken")
        s_slot = sem("slots_ready")
        s_inval = sem("table_invalid")
        s_invmem = sem("invalid_words")
        s_scat = sem("edges_scattered")
        s_tabin = sem("table_in")
        s_wa = sem("wa_ready")
        s_h1ones = sem("h1_ones")
        s_dve = sem("dve_step")
        s_act = sem("act_step")
        s_pool = sem("pool_step")
        s_offs = sem("chunk_offsets")
        s_fin_taken = sem("gnn_taken")
        s_zero = sem("slots_zeroed")
        XT = Handoff(sem("banks_filled"), [sem("banks_taken_act"), sem("banks_taken_dve")], 4)
        HH = XT.after(4 * NT)

        xs = words(A0, NT * D).rearrange("p (t d) -> p t d", t=NT)
        xm = words(B0, NT * D).rearrange("p (t d) -> p t d", t=NT)
        avec = words(B0, 2 * D)
        xnT = words(C0, KD * N).rearrange("p (k n) -> p k n", k=KD)
        xmT = words(D0, KD * N).rearrange("p (k n) -> p k n", k=KD)
        w1x = words(E0, 776 * KD).rearrange("p (k h n) -> p k h n", k=KD, h=2)
        h1 = words(F0, 772 * NT).rearrange("p (t h c) -> p t h c", t=NT, h=H1)
        ttr_junk = words(F0, 4 * C1).rearrange("p (b c) -> p b c", b=4)

        g = G0
        onehot = words(g, EC * NBK // 2, BF16).rearrange("p (c b) -> p c b", c=EC)
        g += EC * NBK // 2
        base0 = words(g, EC * NBK // 2, BF16).rearrange("p (c b) -> p c b", c=EC)
        g += EC * NBK // 2
        EC1 = EC - P
        base1 = words(g, EC1 * NBK // 2, BF16).rearrange("p (c b) -> p c b", c=EC1)
        g += EC1 * NBK // 2
        ef = words(g, 6 * EC).rearrange("p (i c) -> p i c", i=6)
        src_i, dst_i, src_f, dst_f, st_f, dg_f = [ef[:, i, :] for i in range(6)]
        g += 6 * EC
        tot0 = words(g, NBK // 2, BF16)
        g += NBK // 2
        tot1 = words(g, NBK // 2, BF16)
        g += NBK // 2
        chb = words(g, 4)
        g += 4
        startrow = words(g, NBK // 2, BF16)
        g += NBK // 2
        cmpb = words(g, NCH // 2, BF16)
        g += NCH // 2
        assert g <= ARENA, g
        rank_tmp = words(F0 + 768, 960).rearrange("p (i c b) -> p i c b", i=2, c=16)
        rank = words(F0 + 2048, EC)
        invalid = words(F0 + 2304, NCH, I32)
        RC = 16
        RJ = EC // RC

        wkv = words(A0, 2 * D * KD).rearrange("p (k n) -> p k n", k=KD)
        wq = words(A0 + 2 * D * KD, D * KD).rearrange("p (k n) -> p k n", k=KD)
        wout = words(A0, 2 * D * KD).rearrange("p (k n) -> p k n", k=2 * KD)
        mixT = words(D0, KD * N).rearrange("p (k n) -> p k n", k=KD)
        m = D0 + KD * N
        kbuf = words(m, 2 * D).rearrange("p (b n) -> p b n", b=2)
        m += 2 * D
        vbuf = words(m, 2 * KD * 129).rearrange("p (b k n) -> p b k n", b=2, k=KD)
        m += 2 * KD * 129
        mrow = words(m, 2 * D).rearrange("p (b n) -> p b n", b=2)
        m += 2 * D
        assert m <= F0, (m, F0)
        m = G0
        qbuf = words(m, 2 * G).rearrange("p (b n) -> p b n", b=2)
        m += 2 * G
        ebuf = words(m, 2 * G).rearrange("p (b n) -> p b n", b=2)
        m += 2 * G
        rbuf = words(m, 2 * G).rearrange("p (b n) -> p b n", b=2)
        m += 2 * G
        dbuf = words(m, G)
        m += G
        kvb = words(m, D).rearrange("p (k n) -> p k n", k=KD)
        m += D
        ksb = words(m, D).rearrange("p (k n) -> p k n", k=KD)
        m += D
        biasb = words(m, D)
        m += D
        assert m <= ARENA, m
        bias2 = kvb.rearrange("p k n -> p (k n)")

        s_wkv = sem("wkv_in")
        s_wq = sem("wq_in")
        s_wout = sem("wout_in")
        s_bias = sem("bias_in")
        s_biasum = sem("bias_sum")
        s_kready = sem("k_psum")
        s_kexp = sem("k_exp")
        s_kfeat = sem("k_feature")
        s_vready = sem("v_psum")
        s_vsb = sem("v_sb")
        s_kvused = sem("kv_used")
        s_vones = sem("v_ones")
        s_kvblk = sem("kv_blocks")
        s_kvzero = sem("kv_zero")
        s_qpsum = sem("q_psum")
        s_qexp = sem("q_exp")
        s_qfeat = sem("q_feature")
        s_den = sem("attn_psum")
        s_mixT = sem("mixT_ready")
        s_mixps = sem("mix_psum")
        s_mixrow = sem("mix_row")
        s_mixout = [sem(f"mix_out{i}") for i in range(2)]

        counts = words(A0, NT * CW).rearrange("p (t n) -> p t n", t=NT)
        counts_flat = words(A0, NT * CW)
        m = A0 + NT * CW
        mask = words(m, NT * N // 2, BF16).rearrange("p (t n) -> p t n", t=NT)
        m += NT * N // 2
        NPT = 3
        ptile = words(m, NPT * N).rearrange("p (b n) -> p b n", b=NPT)
        lat0 = m
        m += NPT * N
        ubuf = words(m, 2 * N).rearrange("p (b n) -> p b n", b=2)
        m += 2 * N
        tbuf = words(m, 2 * N).rearrange("p (b n) -> p b n", b=2)
        m += 2 * N
        rowbuf = words(m, 3 * N).rearrange("p (b n) -> p b n", b=3)
        m += 3 * N
        heads_end = m
        o3 = m
        m += NT * C1
        w2x = words(m, KD * 196).rearrange("p (k n) -> p k n", k=KD)
        m += KD * 196
        assert m <= F0, (m, F0)
        out1 = [words(G0 + h * NT * C1, NT * C1).rearrange("p (t c) -> p t c", t=NT) for h in range(3)]
        out1 += [words(o3, NT * C1).rearrange("p (t c) -> p t c", t=NT)]
        gm = G0 + 3 * NT * C1
        avec2 = words(gm, 2 * H2 * C2)
        gm += 2 * H2 * C2
        assert gm <= ARENA
        out1T = words(lat0, KD * N).rearrange("p (k n) -> p k n", k=KD)
        assert lat0 + KD * N <= heads_end
        h2 = words(F0, NT * H2 * (C2 + 1)).rearrange("p (t h c) -> p t h c", t=NT, h=H2)
        m = F0 + NT * H2 * (C2 + 1)
        out2 = words(m, NT * H2 * C2).rearrange("p (t h c) -> p t h c", t=NT, h=H2)
        m += NT * H2 * C2
        out2T = words(m, H2 * N).rearrange("p (h n) -> p h n", h=H2)
        m += H2 * N
        assert m <= G0
        wub = words(G0, H2 * D).rearrange("p (h n) -> p h n", h=H2)
        ohs = words(F0 - 2 * 64, 2 * 64, BF16).rearrange("p (b n) -> p b n", b=2)
        ohd = words(G0, 2 * 210, BF16).rearrange("p (b n) -> p b n", b=2)
        vtab = words(G0 + 420, NCH, I32)
        vtmp = words(G0 + 420 + NCH, NCH, I32)
        srow = words(G0 + 420 + 2 * NCH, NCH + 1)
        dcol = words(G0 + 420 + 3 * NCH + 1, NCH + 1)
        x2 = words(A0, NT * D).rearrange("p (t d) -> p t d", t=NT)
        m = A0 + NT * D
        mixin = words(lat0, 2 * D).rearrange("p (b n) -> p b n", b=2)
        xin = words(lat0 + 2 * D, 2 * D).rearrange("p (b n) -> p b n", b=2)

        s_cz = sem("counts_zero")
        s_tab = sem("table_split")
        s_ohb = sem("chunk_onehots")
        s_cps = sem("chunk_psum")
        s_acc = sem("chunk_counted")
        s_mskT = sem("mask_psum")
        s_mask = sem("mask_ready")
        s_w2 = sem("w2_in")
        s_wa2 = sem("wa2_ready")
        s_diag = sem("row_diag")
        s_rowps = sem("row_psum")
        s_row = sem("row_copied")
        s_smax = sem("head_max")
        s_u = sem("head_u")
        s_t = sem("head_t")
        s_e = sem("head_exp")
        s_pt = sem("head_p")
        s_ptused = sem("head_p_used")
        s_hacc = sem("head_acc")
        s_hout = sem("head_out")
        s_h2ones = sem("h2_ones")
        OT = HH.after(2 * NT)
        H2H = OT.after(2 * NT)
        O2 = H2H.after(NT)
        s_wub = sem("wub_in")
        s_b2 = sem("b2_in")
        s_res = [sem(f"residual_in{i}") for i in range(2)]
        s_fin = sem("gnn_psum")
        s_x2a = sem("x2_ready")
        s_resfree = sem("residual_used")

        xf = words(B0, NT * D).rearrange("p (t d) -> p t d", t=NT)
        xfT = words(C0, KD * N).rearrange("p (k n) -> p k n", k=KD)
        wsgu = words(D0, KD * 2 * HS).rearrange("p (k n) -> p k n", k=KD)
        m = D0 + KD * 2 * HS
        KS = HS // P
        wsd = words(m, KS * D).rearrange("p (k n) -> p k n", k=KS)
        m += KS * D
        rwx = words(m, KD * 9).rearrange("p (k n) -> p k n", k=KD)
        m += KD * 9
        sg_s = words(m, 2 * HS).rearrange("p (b n) -> p b n", b=2)
        m += 2 * HS
        sg_h = words(m, 2 * HS).rearrange("p (b n) -> p b n", b=2)
        m += 2 * HS
        sg_hT = words(m, 2 * KS * T).rearrange("p (b k n) -> p b k n", b=2, k=KS)
        m += 2 * KS * T
        assert m <= 36004, m
        m = 36004
        xgb = words(m, 2 * D).rearrange("p (b n) -> p b n", b=2)
        m += 2 * D
        xgT = words(m, 2 * D).rearrange("p (b k n) -> p b k n", b=2, k=KD)
        m += 2 * D
        WB = [ARENA - 3 * KD * D, B0]
        assert m <= WB[0], (m, WB)
        ew = [[words(w + i * KD * D, KD * D).rearrange("p (k n) -> p k n", k=KD) for i in range(3)] for w in WB]
        m = WB[1] + 3 * KD * D
        gs = words(m, 2 * D).rearrange("p (b n) -> p b n", b=2)
        m += 2 * D
        hh = words(m, 2 * D).rearrange("p (b n) -> p b n", b=2)
        m += 2 * D
        hT = words(m, 2 * D).rearrange("p (b k n) -> p b k n", b=2, k=KD)
        m += 2 * D
        yb = words(m, 2 * D).rearrange("p (b n) -> p b n", b=2)
        m += 2 * D
        assert m <= 36004, m
        NGB = 6
        gath = words(B0, NGB * D).rearrange("p (b n) -> p b n", b=NGB)
        route_at = [route0]

        def route(n, dt=F32):
            w = n if dt in (F32, I32, U32) else (n + 1) // 2
            v = words(route_at[0], w, dt)
            route_at[0] += w
            assert route_at[0] <= route1, (route_at, route1)
            return v

        lg = route(NT * 9).rearrange("p (t e) -> p t e", t=NT)
        mx8 = route(NT * 8).rearrange("p (t e) -> p t e", t=NT)
        ix8 = route(NT * 8, U32).rearrange("p (t e) -> p t e", t=NT)
        ixf = route(2 * NT).rearrange("p (k t) -> p k t", k=2)
        oh = route(2 * NT * NE).rearrange("p (k t e) -> p k t e", k=2, t=NT)
        picked = route(NT * NE, BF16).rearrange("p (t e) -> p t e", t=NT)
        ex = route(NT * NE).rearrange("p (t e) -> p t e", t=NT)
        ex2 = route(NT * 2).rearrange("p (t k) -> p t k", t=NT)
        esum = route(NT)
        erec = route(NT)
        pk = route(NT * 2).rearrange("p (t k) -> p t k", t=NT)
        psum2 = route(NT)
        prec = route(NT)
        gate = route(NT * 2).rearrange("p (t k) -> p t k", t=NT)
        alpha = route(NT)
        oma = route(NT)
        sgb = route(1)
        slotf = route(2 * NT).rearrange("p (k t) -> p k t", k=2)
        sloti = route(2 * NT, I32).rearrange("p (k t) -> p k t", k=2)
        slt_tmp = route(2 * NT * NE).rearrange("p (k t e) -> p k t e", k=2, t=NT)
        ecnt_i = route(2, I32)
        ech_b = route(2, BF16)
        estart = route(NE, BF16)
        eend = route(1)
        ecmp = route(NTM, BF16)
        etile = route(NTM)
        etile_i = route(NTM, I32)

        block = ctx.enter_context(nc.Block())
        tp, dv, sc, pl = nc.tensor, nc.vector, nc.scalar, nc.gpsimd
        rowsplit = [(0, T // 5 * 5 - 5), (T - 5, 5)]

        def rows_dma(q, to, frm, s):
            for a, n in rowsplit:
                q.dma_start(to[a:a + n], frm[a:a + n]).then_inc(s, 16)

        s_ws = sem("shared_weights_in")
        s_sgb = sem("sg_bias_in")
        s_xf = sem("xf_ready")
        s_lg = sem("logits_psum")
        s_lgsb = sem("logits_sb")
        s_picked = sem("picked")
        s_epre = sem("slot_psum")
        s_et = sem("tile_expert")
        s_sloti = sem("row_slots")
        s_rows = sem("rows_scattered")
        s_exin = sem("softmax_in")
        s_exout = sem("softmax_exp")
        s_gate = sem("gates_ready")
        s_sgp = sem("shared_gate_psum")
        s_sup = sem("shared_up_psum")
        s_ssil = sem("shared_silu")
        s_sh = sem("shared_h")
        s_shT = sem("shared_hT_psum")
        s_shTs = sem("shared_hT_sb")
        s_sdn = sem("shared_down_psum")
        s_sout = sem("shared_added")
        FT = O2.after(NT)
        s_ew = [[sem(f"expert_w{i}_in{b}") for i in range(3)] for b in range(2)]
        s_xg = [sem(f"slot_rows_in{b}") for b in range(2)]
        s_g = sem("gate_psum")
        s_up = sem("up_psum")
        s_xt = sem("slot_xT_psum")
        s_ht = sem("hT_psum")
        s_y = sem("y_psum")
        s_silu = sem("silu_ready")
        s_xTs = sem("slot_xT_sb")
        s_ya = sem("y_copied_act")
        s_h = sem("h_ready")
        s_hTs = sem("hT_sb")
        s_yd = sem("y_copied_dve")
        s_yout = [sem(f"y_out{b}") for b in range(2)]
        s_gath = [sem(f"gathered{b}") for b in range(NGB)]
        s_comb = sem("combined")
        s_fout = sem("out_written")

        def over_tiles(eng, tile):
            tile(0, 0)
            tile(1, 1)
            with eng.Fori(1, NTM // 2) as i:
                tile(2 * i, 0)
                tile(2 * i + 1, 1)
            tile(NTM - 1, 0)

        def first_two(j):
            return isinstance(j, int) and j < 2

        def use(j, b):
            return (j - b) // 2 + 1 if isinstance(j, int) else None

        def wait_use(eng, s, j, b, each, ago=0):
            if isinstance(j, int):
                eng.wait_ge(s, each * ((j - b) // 2 + 1 - ago))
            else:
                eng.wait_ge(s, (j - b) * (each // 2) + each * (1 - ago))

        def ffn_sync(sp):
            sp.wait_ge(s_hout, NT * (H1 + H2))
            sp.dma_start(rwx[:, :, 0:NE], router_w.rearrange("(k p) n -> p k n", p=P)).then_inc(s_ws, 16)
            sp.dma_start(rwx[:, :, NE:NE + 1], sg_w.rearrange("(k p) n -> p k n", p=P),
                         allow_slow_non_contiguous=True).then_inc(s_ws, 16)
            sp.dma_start(wsgu[:, :, 0:HS], ws_gate.rearrange("(k p) n -> p k n", p=P)).then_inc(s_ws, 16)
            sp.dma_start(wsgu[:, :, HS:2 * HS], ws_up.rearrange("(k p) n -> p k n", p=P)).then_inc(s_ws, 16)
            sp.dma_start(wsd[:, :, :], ws_down.rearrange("(k p) n -> p k n", p=P)).then_inc(s_ws, 16)
            sp.wait_ge(s_zero, 16 * NTM)
            sp.dma_start(sgb[0:T], sg_b.partition_broadcast(T)).then_inc(s_sgb, 16)
            sp.wait_ge(s_et, 1)
            sp.wait_ge(s_rows, 16 * 2 * NT)

            def tile(j, b):
                if not first_two(j):
                    sp.wait_ge(s_ya, j - 1)
                    sp.wait_ge(s_yd, j - 1)
                    sp.dma_start(yg_dram[bass.ds((j - 2) * P, P)], yb[:, b]).then_inc(s_yout[b], 16)
                elif j == 1:
                    sp.wait_ge(s_sdn, 2 * NT)
                sp.dma_start(xgb[:, b], xg_dram[bass.ds(j * P, P)]).then_inc(s_xg[b], 16)
                e = sp.value_load(etile_i[0:1, bass.ds(j, 1)], min_val=0, max_val=NE - 1)
                for i, w in enumerate((w_gate, w_up, w_down)):
                    sp.dma_start(ew[b][i], w[bass.ds(e, 1)].rearrange("a (k p) n -> p (a k) n", p=P)).then_inc(s_ew[b][i], 16)

            over_tiles(sp, tile)
            for j in (NTM - 2, NTM - 1):
                sp.wait_ge(s_ya, j + 1)
                sp.wait_ge(s_yd, j + 1)
                sp.dma_start(yg_dram[j * P:(j + 1) * P], yb[:, j % 2]).then_inc(s_yout[j % 2], 16)
            for t in range(NT):
                sp.wait_ge(s_comb, 2 * (t + 1))
                rows_dma(sp, out_rows[:, t], x2[0:T, t], s_fout)
            sp.wait_ge(s_fout, 32 * NT)

        def ffn_pool(pool):
            pool.wait_ge(s_sloti, 1)
            pool.wait_ge(s_zero, 16 * NTM)
            pool.wait_ge(s_xf, NT)
            for t in range(NT):
                for k in range(2):
                    pl.indirect_dma_start(xg_dram[:, :], bass.IndirectOffsetOnAxis(ap=sloti[0:T, k, t:t + 1], axis=0),
                                          xf[0:T, t], None).then_inc(s_rows, 16)
            pool.wait_ge(s_yout[0], 16 * (NTM // 2 + 1))
            pool.wait_ge(s_yout[1], 16 * (NTM // 2))
            for q in range(2 * NT):
                if q >= NGB:
                    pool.wait_ge(s_comb, q - NGB + 1)
                pl.indirect_dma_start(gath[0:T, q % NGB], None, yg_dram[:, :],
                                      bass.IndirectOffsetOnAxis(ap=sloti[0:T, q % 2, q // 2:q // 2 + 1], axis=0))\
                    .then_inc(s_gath[q % NGB], 16)

        def ffn_pe(pe):
            pe.wait_ge(s_fin_taken, 2 * NT)
            for t in range(NT):
                pe.wait_ge(s_xf, t + 1)
                for hf in range(2):
                    q = 2 * t + hf
                    FT.wait_free(pe, q)
                    for i in range(3):
                        k = 3 * hf + i
                        ins = tp.transpose(ps[q % 4][:, i * T:(i + 1) * T], xf[0:T, t, k * P:(k + 1) * P], ident[0:T, 0:T])
                    FT.filled(ins)
            FT.wait_all_taken(pe, 2 * NT)
            pe.wait_ge(s_ws, 80)
            for t in range(NT):
                for k in range(KD):
                    ins = tp.matmul(ps[4][0:T, 9 * t:9 * t + 9], xfT[:, k, t * T:(t + 1) * T], rwx[:, k, :],
                                    start=(k == 0), stop=(k == KD - 1))
            ins.then_inc(s_lg, 1)

            def shared_up(t):
                b = 2 * (t % 2)
                if t >= 2:
                    pe.wait_ge(s_ssil, t - 1)
                for k in range(KD):
                    ins = tp.matmul(ps[b][0:T, 0:HS], xfT[:, k, t * T:(t + 1) * T], wsgu[:, k, 0:HS],
                                    start=(k == 0), stop=(k == KD - 1))
                ins.then_inc(s_sgp, 1)
                if t >= 2:
                    pe.wait_ge(s_sh, t - 1)
                for k in range(KD):
                    ins = tp.matmul(ps[b + 1][0:T, 0:HS], xfT[:, k, t * T:(t + 1) * T], wsgu[:, k, HS:2 * HS],
                                    start=(k == 0), stop=(k == KD - 1))
                ins.then_inc(s_sup, 1)

            def shared_down(t):
                pe.wait_ge(s_sh, t + 1)
                if t >= 2:
                    pe.wait_ge(s_shTs, t - 1)
                for k in range(KS):
                    ins = tp.transpose(ps[4 + t % 2][:, k * T:(k + 1) * T], sg_h[0:T, t % 2, k * P:(k + 1) * P], ident[0:T, 0:T])
                ins.then_inc(s_shT, 1)
                pe.wait_ge(s_shTs, t + 1)
                for hf in range(2):
                    if t >= 1:
                        pe.wait_ge(s_sout, 2 * (t - 1) + hf + 1)
                    for k in range(KS):
                        ins = tp.matmul(ps[6 + hf][0:T, 0:384], sg_hT[:, t % 2, k, :], wsd[:, k, hf * 384:(hf + 1) * 384],
                                        start=(k == 0), stop=(k == KS - 1))
                    ins.then_inc(s_sdn, 1)

            shared_up(0)
            pe.wait_ge(s_picked, 1)
            for t in range(NT):
                ins = tp.matmul(ps[6][0:NE, 0:1], picked[0:T, t, :], ones_b[0:T, 0:1], start=(t == 0), stop=(t == NT - 1))
            ins.then_inc(s_cnt, 1)
            shared_up(1)
            pe.wait_ge(s_chunks, 2)
            tp.matmul(ps[6][0:1, 8:8 + NE], ech_b[0:NE, 0:1], tri[0:NE, 0:NE], start=True, stop=True)
            tp.matmul(ps[6][0:NE, 16:17], triinc[0:NE, 0:NE], ech_b[0:NE, 0:1], start=True, stop=True).then_inc(s_starts, 1)
            pe.wait_ge(s_startrow, 2)
            o = ps[5][0:T, 0:NT * NE].rearrange("p (t e) -> p t e", t=NT)
            tp.matmul(o, tri[0:T, 0:T], picked[0:T], start=True, stop=False)
            for t in range(NT - 1):
                n = NT - 1 - t
                tp.matmul(o[:, t + 1:NT], ones_b[0:T, 0:T], picked[0:T, t:t + 1].to_broadcast([T, n, NE]),
                          start=False, stop=False)
            tp.matmul(o, ones_b[0:1, 0:T], estart[0:1, 0:NE].unsqueeze(1).to_broadcast([1, NT, NE]),
                      start=False, stop=True).then_inc(s_epre, 1)
            pe.wait_ge(s_cmp, 2)
            tp.matmul(ps[7][0:1, 0:NTM], ones_b[0:NE, 0:1], ecmp[0:NE, 0:NTM], start=True, stop=True).then_inc(s_bk, 1)
            pe.wait_ge(s_et, 1)
            pe.wait_ge(s_sloti, 1)
            shared_down(0)
            for t in range(2, NT):
                shared_up(t)
                shared_down(t - 1)
            shared_down(NT - 1)
            pe.wait_ge(s_sout, 2 * NT)

            def x_transposes(j, b):
                wait_use(pe, s_xg[b], j, b, 16)
                for i in range(2):
                    if not first_two(j):
                        pe.wait_ge(s_hTs, 2 * j - 3 + i)
                    for k in range(3):
                        ins = tp.transpose(ps[6 + i][:, k * P:(k + 1) * P], xgb[:, b, (3 * i + k) * P:(3 * i + k + 1) * P], ident)
                    ins.then_inc(s_xt, 1)

            def tile(j, b):
                last = isinstance(j, int) and j == NTM - 1
                pe.wait_ge(s_xTs, 2 * j + 2)
                wait_use(pe, s_ew[b][0], j, b, 16)
                for i in range(2):
                    if not (isinstance(j, int) and j == 0):
                        pe.wait_ge(s_silu, 2 * j - 1 + i)
                    for k in range(KD):
                        ins = tp.matmul(ps[i][:, 0:384], xgT[:, b, k], ew[b][0][:, k, i * 384:(i + 1) * 384],
                                        start=(k == 0), stop=(k == KD - 1))
                    ins.then_inc(s_g, 1)
                wait_use(pe, s_ew[b][1], j, b, 16)
                for i in range(2):
                    if not (isinstance(j, int) and j == 0):
                        pe.wait_ge(s_h, 2 * j - 1 + i)
                    for k in range(KD):
                        ins = tp.matmul(ps[2 + i][:, 0:384], xgT[:, b, k], ew[b][1][:, k, i * 384:(i + 1) * 384],
                                        start=(k == 0), stop=(k == KD - 1))
                    ins.then_inc(s_up, 1)
                if not last:
                    x_transposes(j + 1, 1 - b)
                for i in range(2):
                    if last:
                        pe.wait_ge(s_hTs, 2 * j)
                    else:
                        pe.wait_ge(s_xTs, 2 * j + 3 + i)
                    pe.wait_ge(s_h, 2 * j + 1 + i)
                    for k in range(3):
                        ins = tp.transpose(ps[6 + i][:, k * P:(k + 1) * P], hh[:, b, (3 * i + k) * P:(3 * i + k + 1) * P], ident)
                    ins.then_inc(s_ht, 1)
                wait_use(pe, s_ew[b][2], j, b, 16)
                if not (isinstance(j, int) and j == 0):
                    pe.wait_ge(s_ya, j)
                    pe.wait_ge(s_yd, j)
                for i in range(2):
                    pe.wait_ge(s_hTs, 2 * j + 1 + i)
                    for k in range(3):
                        for o in range(2):
                            ins = tp.matmul(ps[4 + o][:, 0:384], hT[:, b, 3 * i + k], ew[b][2][:, 3 * i + k, o * 384:(o + 1) * 384],
                                            start=(i == 0 and k == 0), stop=(i == 1 and k == 2))
                ins.then_inc(s_y, 1)

            x_transposes(0, 0)
            over_tiles(pe, tile)

        def ffn_act(act):
            act.wait_ge(s_stats, 3)
            sc.activation(std[0:T], mv[0:T, :, 1], ACT.Sqrt, bias=epst[0:T]).then_inc(s_std, 1)
            for t in range(NT):
                q = 2 * t
                FT.wait_filled(act, q)
                FT.taken(sc.activation(xfT[:, 0:3, t * T:(t + 1) * T],
                                       ps[q % 4][:, 0:3 * T].rearrange("p (k n) -> p k n", k=3), ACT.Copy), q)
            act.wait_ge(s_exin, 1)
            sc.activation(ex[0:T], ex[0:T], ACT.Exp)
            sc.activation(ex2[0:T], ex2[0:T], ACT.Exp).then_inc(s_exout, 1)
            act.wait_ge(s_sgb, 16)
            sc.activation(alpha[0:T], lg[0:T, :, NE], ACT.Sigmoid, bias=sgb[0:T]).then_inc(s_exout, 1)

            def shared_silu(t):
                act.wait_ge(s_sgp, t + 1)
                if t >= 2:
                    act.wait_ge(s_sh, t - 1)
                sc.activation(sg_s[0:T, t % 2], ps[2 * (t % 2)][0:T, 0:HS], ACT.Silu).then_inc(s_ssil, 1)

            def shared_hT(t):
                act.wait_ge(s_shT, t + 1)
                if t >= 2:
                    act.wait_ge(s_sdn, 2 * (t - 1))
                sc.activation(sg_hT[:, t % 2].rearrange("p k n -> p (k n)"), ps[4 + t % 2][:, 0:KS * T], ACT.Copy).then_inc(s_shTs, 1)

            shared_silu(0)
            shared_silu(1)
            shared_hT(0)
            for t in range(2, NT):
                shared_silu(t)
                shared_hT(t - 1)
            shared_hT(NT - 1)

            def take_x(j, b):
                for i in range(2):
                    act.wait_ge(s_xt, 2 * j + 1 + i)
                    sc.activation(xgT[:, b, 3 * i:3 * i + 3].rearrange("p k n -> p (k n)"), ps[6 + i][:, 0:384],
                                  ACT.Copy).then_inc(s_xTs, 1)

            def tile(j, b):
                for i in range(2):
                    act.wait_ge(s_g, 2 * j + 1 + i)
                    sc.activation(gs[:, b, i * 384:(i + 1) * 384], ps[i][:, 0:384], ACT.Silu).then_inc(s_silu, 1)
                if not (isinstance(j, int) and j == NTM - 1):
                    take_x(j + 1, 1 - b)
                act.wait_ge(s_y, j + 1)
                if not first_two(j):
                    wait_use(act, s_yout[b], j, b, 16, ago=1)
                sc.activation(yb[:, b, 0:384], ps[4][:, 0:384], ACT.Copy).then_inc(s_ya, 1)

            take_x(0, 0)
            over_tiles(act, tile)

        def ffn_dve(dve, step, norm_stats):
            stt = dv.scalar_tensor_tensor
            dve.wait_ge(s_fin_taken, 2 * NT)
            norm_stats(x2).then_inc(s_stats, 1)
            dve.wait_ge(s_std, 3)
            step(dv.reciprocal(rstd[0:T], std[0:T]))
            step.wait()
            for t in range(NT):
                dv.tensor_scalar(xf[0:T, t], x2[0:T, t], mv[0:T, t, 0:1], rstd[0:T, t:t + 1], ALU.subtract, ALU.mult)\
                    .then_inc(s_xf, 1)
            for t in range(NT):
                q = 2 * t + 1
                FT.wait_filled(dve, q)
                FT.taken(dv.tensor_copy(xfT[:, 3:6, t * T:(t + 1) * T],
                                        ps[q % 4][:, 0:3 * T].rearrange("p (k n) -> p k n", k=3)), q)
            dve.wait_ge(s_lg, 1)
            dve.wait_ge(s_zero, 16 * NTM)
            step(dv.tensor_copy(lg[0:T], ps[4][0:T, 0:9 * NT].rearrange("p (t e) -> p t e", t=NT)))
            step.wait()
            for t in range(NT):
                step(dv.max(mx8[0:T, t], lg[0:T, t, 0:NE]))
            step.wait()
            for t in range(NT):
                step(dv.max_index(ix8[0:T, t], mx8[0:T, t], lg[0:T, t, 0:NE]))
            step.wait()
            step(dv.tensor_copy(ixf[0:T], ix8[0:T, :, 0:2].rearrange("p t k -> p k t")))
            step.wait()
            for k in range(2):
                step(dv.tensor_tensor(oh[0:T, k], iota[0:T, 0:NE].unsqueeze(1).to_broadcast([T, NT, NE]),
                                      ixf[0:T, k].unsqueeze(2).to_broadcast([T, NT, NE]), ALU.is_equal))
            step.wait()
            dv.tensor_tensor(picked[0:T], oh[0:T, 0], oh[0:T, 1], ALU.add).then_inc(s_picked, 1)
            m0 = mx8[0:T, :, 0:1]
            step(dv.tensor_tensor(ex[0:T], lg[0:T, :, 0:NE], m0.to_broadcast([T, NT, NE]), ALU.subtract))
            dv.tensor_tensor(ex2[0:T], mx8[0:T, :, 0:2], m0.to_broadcast([T, NT, 2]), ALU.subtract).then_inc(s_exin, 1)
            dve.wait_ge(s_cnt, 2)
            step(dv.tensor_scalar(ecnt_i[0:NE, 0:1], ps[6][0:NE, 0:1], float(P - 1), None, ALU.add))
            step.wait()
            step(dv.tensor_scalar(ecnt_i[0:NE, 1:2], ecnt_i[0:NE, 0:1], 7, None, ALU.arith_shift_right))
            step.wait()
            dv.tensor_copy(ech_b[0:NE, 0:1], ecnt_i[0:NE, 1:2]).then_inc(s_chunks, 1)
            dve.wait_ge(s_starts, 2)
            dv.tensor_scalar(estart[0:1], ps[6][0:1, 8:8 + NE], float(P), None, ALU.mult).then_inc(s_startrow, 1)
            step(dv.tensor_copy(eend[0:NE], ps[6][0:NE, 16:17]))
            step.wait()
            dv.tensor_scalar(ecmp[0:NE, 0:NTM], iota[0:NE, 0:NTM], eend[0:NE], None, ALU.is_ge).then_inc(s_cmp, 1)
            dve.wait_ge(s_epre, 1)
            slots = ps[5][0:T, 0:NT * NE].rearrange("p (t e) -> p t e", t=NT)
            for k in range(2):
                step(dv.tensor_tensor(slt_tmp[0:T, k], slots, oh[0:T, k], ALU.mult))
            step.wait()
            step(dv.tensor_reduce(slotf[0:T], slt_tmp[0:T], AX.X, ALU.add))
            step.wait()
            dv.tensor_copy(sloti[0:T], slotf[0:T]).then_inc(s_sloti, 1)
            dve.wait_ge(s_bk, 2)
            dv.tensor_scalar(etile_i[0:1], ps[7][0:1, 0:NTM], float(NE - 1), None, ALU.min).then_inc(s_et, 1)
            dve.wait_ge(s_exout, 2)
            step(dv.tensor_reduce(esum[0:T], ex[0:T], AX.X, ALU.add))
            step.wait()
            step(dv.reciprocal(erec[0:T], esum[0:T]))
            step.wait()
            step(dv.tensor_tensor(pk[0:T], ex2[0:T], erec[0:T].unsqueeze(2).to_broadcast([T, NT, 2]), ALU.mult))
            step.wait()
            step(dv.tensor_reduce(psum2[0:T], pk[0:T], AX.X, ALU.add))
            step.wait()
            step(dv.reciprocal(prec[0:T], psum2[0:T]))
            step(dv.tensor_scalar(oma[0:T], alpha[0:T], -1.0, 1.0, ALU.mult, ALU.add))
            step.wait()
            step(dv.tensor_tensor(prec[0:T], prec[0:T], oma[0:T], ALU.mult))
            step.wait()
            step(dv.tensor_tensor(gate[0:T], pk[0:T], prec[0:T].unsqueeze(2).to_broadcast([T, NT, 2]), ALU.mult))

            def shared_h(t):
                dve.wait_ge(s_ssil, t + 1)
                dve.wait_ge(s_sup, t + 1)
                if t >= 2:
                    dve.wait_ge(s_shT, t - 1)
                dv.tensor_tensor(sg_h[0:T, t % 2], ps[2 * (t % 2) + 1][0:T, 0:HS], sg_s[0:T, t % 2], ALU.mult).then_inc(s_sh, 1)

            def shared_out(t):
                for hf in range(2):
                    dve.wait_ge(s_sdn, 2 * t + hf + 1)
                    cols = x2[0:T, t, hf * 384:(hf + 1) * 384]
                    stt(out=cols, in0=ps[6 + hf][0:T, 0:384], scalar=alpha[0:T, t:t + 1], in1=cols,
                        op0=ALU.mult, op1=ALU.add).then_inc(s_sout, 1)

            shared_h(0)
            shared_h(1)
            shared_out(0)
            for t in range(2, NT):
                shared_h(t)
                shared_out(t - 1)
            shared_out(NT - 1)

            def tile(j, b):
                for i in range(2):
                    dve.wait_ge(s_silu, 2 * j + 1 + i)
                    dve.wait_ge(s_up, 2 * j + 1 + i)
                    dv.tensor_tensor(hh[:, b, i * 384:(i + 1) * 384], ps[2 + i][:, 0:384], gs[:, b, i * 384:(i + 1) * 384],
                                     ALU.mult).then_inc(s_h, 1)
                for i in range(2):
                    dve.wait_ge(s_ht, 2 * j + 1 + i)
                    dv.tensor_copy(hT[:, b, 3 * i:3 * i + 3].rearrange("p k n -> p (k n)"), ps[6 + i][:, 0:384]).then_inc(s_hTs, 1)
                dve.wait_ge(s_y, j + 1)
                if not first_two(j):
                    wait_use(dve, s_yout[b], j, b, 16, ago=1)
                dv.tensor_copy(yb[:, b, 384:768], ps[5][:, 0:384]).then_inc(s_yd, 1)

            over_tiles(dve, tile)
            step.wait()
            dve.wait_ge(s_sout, 2 * NT)
            for q in range(2 * NT):
                t, k = q // 2, q % 2
                dve.wait_ge(s_gath[q % NGB], 16 * (q // NGB + 1))
                if k:
                    dve.wait_ge(s_comb, q)
                stt(out=x2[0:T, t], in0=gath[0:T, q % NGB], scalar=gate[0:T, t, k:k + 1], in1=x2[0:T, t],
                    op0=ALU.mult, op1=ALU.add).then_inc(s_comb, 1)

        @block.sync
        def _(sp):
            sp.dma_start(src_i.bitcast(I32)[0:T], src.rearrange("(p c) -> p c", p=T)).then_inc(s_edges, 16)
            sp.dma_start(dst_i.bitcast(I32)[0:T], dst.rearrange("(p c) -> p c", p=T)).then_inc(s_edges, 16)
            for g in range(5):
                rows_dma(sp, xs[0:T, 2 * g:2 * g + 2], x_rows[:, 2 * g:2 * g + 2], s_x[g])
            sp.dma_start(avec[:, 0:D], a_src1.rearrange("h c -> (h c)").partition_broadcast(P)).then_inc(s_avec, 16)
            sp.dma_start(avec[:, D:2 * D], a_dst1.rearrange("h c -> (h c)").partition_broadcast(P)).then_inc(s_avec, 16)
            for hf in range(2):
                sp.dma_start(w1x[:, :, hf, 0:384], W1[:, hf * 384:(hf + 1) * 384].rearrange("(k p) n -> p k n", p=P)).then_inc(s_w1, 16)
            XT.wait_all_taken(sp, 4 * NT)
            sp.dma_start(wkv[:, :, :], w_qkv[:, D:3 * D].rearrange("(k p) n -> p k n", p=P)).then_inc(s_wkv, 16)
            sp.dma_start(wq[:, :, :], w_qkv[:, 0:D].rearrange("(k p) n -> p k n", p=P)).then_inc(s_wq, 16)
            sp.wait_ge(s_slot, 1)
            sp.wait_ge(s_bk, 1)
            sp.dma_start(biasb, bu.partition_broadcast(P)).then_inc(s_bias, 16)
            sp.dma_start(bias2, b_proj.partition_broadcast(P)).then_inc(s_bias, 16)
            sp.wait_ge(s_kready, 2 * NT)
            sp.wait_ge(s_vready, 2 * NT)
            sp.dma_start(wout[:, 0:KD], Wu[0:D].rearrange("(k p) n -> p k n", p=P)).then_inc(s_wout, 16)
            sp.dma_start(wout[:, KD:2 * KD], w_proj.rearrange("(k p) n -> p k n", p=P)).then_inc(s_wout, 16)
            for t in range(NT):
                sp.wait_ge(s_mixrow, 2 * t + 2)
                rows_dma(sp, mixed_dram.rearrange("(t p) d -> p t d", p=T)[:, t], mrow[0:T, t % 2], s_mixout[t % 2])
            sp.wait_ge(s_scat, 16 * EC)
            sp.wait_ge(s_mixps, 2 * NT)
            sp.dma_start(vtab, edge_table.rearrange("(p c) a -> p (c a)", p=P)).then_inc(s_tabin, 16)
            for i in range(2):
                sp.wait_ge(s_mixout[i], 32 * NT // 2)
            sp.dma_start(w2x[:, :, 0:192], W2.rearrange("(k p) n -> p k n", p=P)).then_inc(s_w2, 16)
            sp.dma_start(avec2[:, 0:192], a_src2.rearrange("h c -> (h c)").partition_broadcast(P)).then_inc(s_w2, 16)
            sp.dma_start(avec2[:, 192:384], a_dst2.rearrange("h c -> (h c)").partition_broadcast(P)).then_inc(s_w2, 16)
            OT.wait_all_taken(sp, 2 * NT)
            sp.dma_start(wub[0:C2], Wu[D:D + H2 * C2].rearrange("(h p) n -> p h n", p=C2)).then_inc(s_wub, 16)
            for i in range(2):
                sp.wait_ge(s_mixout[i], 32 * NT // 2)
            sp.wait_ge(s_ptused, NT * (H1 + H2))
            for t in range(NT):
                if t >= 2:
                    sp.wait_ge(s_resfree, t - 1)
                rows_dma(sp, mixin[0:T, t % 2], mixed_dram.rearrange("(t p) d -> p t d", p=T)[:, t], s_res[t % 2])
                rows_dma(sp, xin[0:T, t % 2], x_rows[:, t], s_res[t % 2])
            ffn_sync(sp)

        @block.gpsimd
        def _(pool):
            step = Chain(pool, s_pool)
            step(pl.memset(ident, 0.0))
            pl.memset(ones, 1.0).then_inc(s_const, 1)
            pl.memset(zeros, 0.0).then_inc(s_const, 1)
            pl.memset(ones_b, 1.0).then_inc(s_const, 1)
            pl.memset(epst, EPS).then_inc(s_const, 1)
            step(pl.memset(tri, 1.0))
            step(pl.memset(triinc, 1.0))
            step(pl.memset(later, 1.0))
            step(pl.iota(iota_i, pattern=[[1, G]], base=0, channel_multiplier=0))
            step.wait()
            pl.affine_select(out=ident, in_=ident, compare_op=ALU.not_equal, fill=1.0, base=0,
                             pattern=[[-1, P]], channel_multiplier=1).then_inc(s_const, 1)
            pl.affine_select(out=tri, in_=tri, compare_op=ALU.is_ge, fill=0.0, base=-1,
                             pattern=[[1, P]], channel_multiplier=-1).then_inc(s_const, 1)
            pl.affine_select(out=triinc, in_=triinc, compare_op=ALU.is_ge, fill=0.0, base=0,
                             pattern=[[1, P]], channel_multiplier=-1).then_inc(s_const, 1)
            pl.affine_select(out=later, in_=later, compare_op=ALU.is_ge, fill=0.0, base=-1,
                             pattern=[[1, EC]], channel_multiplier=-1).then_inc(s_const, 1)
            pl.tensor_copy(iota, iota_i).then_inc(s_const, 1)
            pl.tensor_copy(iota_h[:, 0:G], iota_i).then_inc(s_const, 1)
            pl.memset(invalid, P * SRS).then_inc(s_invmem, 1)
            pool.wait_ge(s_invmem, 1)
            pl.dma_start(edge_table.rearrange("(p c) a -> p (c a)", p=P), invalid).then_inc(s_inval, 16)
            pool.wait_ge(s_inval, 16)
            pool.wait_ge(s_slot, 1)
            for c in range(EC):
                pl.indirect_dma_start(edge_table[:, :], bass.IndirectOffsetOnAxis(ap=slot_i[0:T, c:c + 1], axis=0),
                                      edge_v[0:T, c:c + 1], None).then_inc(s_scat, 16)
            ffn_pool(pool)

        @block.tensor
        def _(pe):
            def transposes(which, srct):
                for t in range(NT):
                    pe.wait_ge(s_xn, which * NT + t + 1)
                    for hf in range(2):
                        q = (which * NT + t) * 2 + hf
                        XT.wait_free(pe, q)
                        for i in range(3):
                            k = 3 * hf + i
                            ins = tp.transpose(ps[q % 4][:, i * T:(i + 1) * T], srct[0:T, t, k * P:(k + 1) * P],
                                               ident[0:T, 0:T])
                        XT.filled(ins)

            pe.wait_ge(s_const, 10)
            pe.wait_ge(s_oh, 1)
            for b in range(NBK):
                tp.matmul(ps[4][:, b:b + 1], onehot[0:T, 0:P, b], ones_b[0:T, 0:1], start=True, stop=True)
            for b in range(NBK):
                ins = tp.matmul(ps[5][0:EC1, b:b + 1], onehot[0:T, P:EC, b], ones_b[0:T, 0:1], start=True, stop=True)
            ins.then_inc(s_tot, 1)
            pe.wait_ge(s_br, 1)
            tp.matmul(ps[4][0:NBK, 32:33], tot0[:, :], ones_b[:, 0:1], start=True, stop=False)
            tp.matmul(ps[4][0:NBK, 32:33], tot1[0:EC1, :], ones_b[0:EC1, 0:1], start=False, stop=True).then_inc(s_cnt, 1)
            pe.wait_ge(s_chunks, 1)
            tp.matmul(ps[5][0:1, 0:NBK], chb.bitcast(BF16)[0:NBK, 0:1], tri[0:NBK, 0:NBK], start=True, stop=True)
            tp.matmul(ps[5][0:NBK, 32:33], triinc[0:NBK, 0:NBK], chb.bitcast(BF16)[0:NBK, 0:1],
                      start=True, stop=True).then_inc(s_starts, 1)
            pe.wait_ge(s_startrow, 1)
            for j in range(RJ):
                if j >= 2:
                    pe.wait_ge(s_rankfree, j - 1)
                o = ps[6 + j % 2][0:T, 0:RC * NBK]
                cs = slice(RC * j, RC * j + RC)
                tp.matmul(o, tri[0:T, 0:T], onehot[0:T, cs, :], start=True, stop=False)
                tp.matmul(o, ones_b[:, 0:T], base0[:, cs, :], start=False, stop=False)
                if RC * j >= P:
                    c1 = slice(RC * j - P, RC * j - P + RC)
                    tp.matmul(o, ones_b[0:EC1, 0:T], base1[0:EC1, c1, :], start=False, stop=False)
                tp.matmul(o, ones_b[0:1, 0:T], startrow[0:1, 0:NBK].unsqueeze(1).to_broadcast([1, RC, NBK]),
                          start=False, stop=True).then_inc(s_rank, 1)
            pe.wait_ge(s_cmp, 1)
            tp.matmul(ps[4][0:1, 64:64 + NCH], ones_b[0:NBK, 0:1], cmpb[0:NBK, 0:NCH], start=True, stop=True).then_inc(s_bk, 1)

            transposes(0, xs)
            transposes(1, xm)
            XT.wait_all_taken(pe, 4 * NT)
            pe.wait_ge(s_wa, 1)
            pe.wait_ge(s_w1, 32)
            for t in range(NT):
                for hf in range(2):
                    q = 2 * t + hf
                    HH.wait_free(pe, q)
                    for k in range(KD):
                        ins = tp.matmul(ps[q % 4][0:T, 0:388], xmT[:, k, t * T:(t + 1) * T], w1x[:, k, hf, :],
                                        start=(k == 0), stop=(k == KD - 1))
                    HH.filled(ins)
            HH.wait_all_taken(pe, 2 * NT)
            pe.wait_ge(s_wkv, 16)

            def kv_accumulate(t):
                pe.wait_ge(s_kfeat, 2 * t + 2)
                pe.wait_ge(s_vsb, 2 * t + 2)
                for pr in range(KD):
                    ins = tp.matmul(ps[4 + pr // 3][:, (pr % 3) * 129:(pr % 3) * 129 + 129],
                                    kbuf[0:T, t % 2, pr * P:(pr + 1) * P], vbuf[0:T, t % 2, pr, :],
                                    start=(t == 0 and pr % 3 == 0), stop=(t == NT - 1 and pr % 3 == 2),
                                    skip_group_check=True)
                ins.then_inc(s_kvused, 1)

            for t in range(NT):
                for hf in range(2):
                    if t >= 1:
                        pe.wait_ge(s_kexp, 2 * (t - 1) + hf + 1)
                    for k in range(KD):
                        ins = tp.matmul(ps[hf][0:T, 0:384], xnT[:, k, t * T:(t + 1) * T],
                                        wkv[:, k, hf * 384:(hf + 1) * 384], start=(k == 0), stop=(k == KD - 1))
                    ins.then_inc(s_kready, 1)
                for hf in range(2):
                    if t >= 1:
                        pe.wait_ge(s_vsb, 2 * (t - 1) + hf + 1)
                    for k in range(KD):
                        ins = tp.matmul(ps[2 + hf][0:T, 0:384], xnT[:, k, t * T:(t + 1) * T],
                                        wkv[:, k, D + hf * 384:D + (hf + 1) * 384], start=(k == 0), stop=(k == KD - 1))
                    ins.then_inc(s_vready, 1)
                if t >= 1:
                    kv_accumulate(t - 1)
            kv_accumulate(NT - 1)
            pe.wait_ge(s_wq, 16)
            steps = [(mb, i) for mb in range(KD) for i in range(DG)]

            def attend(s):
                mb, i = steps[s]
                n0, n = NG[i]
                if s == 0:
                    pe.wait_ge(s_kvblk, 1)
                if s >= 2:
                    pe.wait_ge(s_mixT, s - 1)
                pe.wait_ge(s_qfeat, s + 1)
                tp.matmul(ps[6 + s % 2][:, 0:n], ksb[:, mb, :], qbuf[:, s % 2, 0:n], start=True, stop=True)
                tp.matmul(ps[2 + s % 2][:, 0:n], kvb[:, mb, :], qbuf[:, s % 2, 0:n], start=True, stop=True).then_inc(s_den, 1)

            pe.wait_ge(s_kexp, 2 * NT)
            pe.wait_ge(s_vsb, 2 * NT)
            for s, (mb, i) in enumerate(steps):
                n0, n = NG[i]
                if s >= 2:
                    pe.wait_ge(s_qexp, s - 1)
                for k in range(KD):
                    ins = tp.matmul(ps[s % 2][:, 0:n], wq[:, k, mb * P:(mb + 1) * P], xnT[:, k, n0:n0 + n],
                                    start=(k == 0), stop=(k == KD - 1))
                ins.then_inc(s_qpsum, 1)
                if s >= 1:
                    attend(s - 1)
            attend(len(steps) - 1)
            pe.wait_ge(s_wout, 32)
            pe.wait_ge(s_mixT, len(steps))
            for t in range(NT):
                for hf in range(2):
                    q = 2 * t + hf
                    if q >= 2:
                        pe.wait_ge(s_mixrow, q - 1)
                    for k in range(2 * KD):
                        lhs = (xnT if k < KD else mixT)[:, k % KD, t * T:(t + 1) * T]
                        ins = tp.matmul(ps[q % 2][0:T, 0:384], lhs, wout[:, k, hf * 384:(hf + 1) * 384],
                                        start=(k == 0), stop=(k == 2 * KD - 1))
                    ins.then_inc(s_mixps, 1)
            pe.wait_ge(s_mixrow, 2 * NT)

            def chunk(j, b):
                pe.wait_ge(s_ohb, j + 1)
                pe.wait_ge(s_acc, j + 1)
                tp.matmul(ps[b][0:T, 0:G], ohs[:, b, 0:T], ohd[:, b, 0:G], start=True, stop=True).then_inc(s_cps, 1)

            with pe.Fori(0, NCH // 2) as i:
                chunk(2 * i, 0)
                chunk(2 * i + 1, 1)
            pe.wait_ge(s_acc, NCH + 2)
            for dt in range(NT):
                if dt >= 2:
                    pe.wait_ge(s_mask, 3 * (dt - 1))
                for st in range(NT):
                    bank = ps[(dt % 2) * 4 + st // 4]
                    ins = tp.transpose(bank[0:T, (st % 4) * T:(st % 4 + 1) * T],
                                       counts[0:T, st, dt * T:(dt + 1) * T], ident[0:T, 0:T])
                ins.then_inc(s_mskT, 1)
            pe.wait_ge(s_mask, 3 * NT)
            def row_to_banks(n):
                pe.wait_ge(s_diag, n + 1)
                if n >= 1:
                    pe.wait_ge(s_row, n)
                for i in range(DG):
                    ins = tp.matmul(ps[i][:, 0:NG[i][1]], ones[0:T, :],
                                    ubuf.rearrange("p b n -> p (b n)")[0:T, NG[i][0]:NG[i][0] + NG[i][1]],
                                    start=True, stop=True)
                ins.then_inc(s_rowps, 1)

            def heads(layer, H, C, hsrc, first):
                for h in range(H):
                    n = first + h
                    for r in range(3):
                        row_to_banks(3 * n + r)
                    if n >= 1:
                        pe.wait_ge(s_hout, NT * n)
                    for st in range(NT):
                        j = n * NT + st
                        pe.wait_ge(s_pt, j + 1)
                        for dt in range(NT):
                            o = ps[3 + dt // 2][0:T, (dt % 2) * (C + 1):(dt % 2 + 1) * (C + 1)]
                            ins = tp.matmul(o, ptile[0:T, j % NPT, dt * T:(dt + 1) * T], hsrc[0:T, st, h, :],
                                            start=(st == 0 and dt % 2 == 0), stop=(st == NT - 1 and dt % 2 == 1),
                                            skip_group_check=True)
                        ins.then_inc(s_ptused, 1)
                        if st == NT - 1:
                            pass
                heads_done = first + H
                return heads_done

            heads(1, H1, C1, h1, 0)
            pe.wait_ge(s_hout, NT * H1)
            for t in range(NT):
                for hf in range(2):
                    q = 2 * t + hf
                    OT.wait_free(pe, q)
                    c0 = hf * 384
                    for i in range(3):
                        c = c0 + i * P
                        if c // C1 == (c + P - 1) // C1:
                            ins = tp.transpose(ps[q % 4][:, i * T:(i + 1) * T],
                                               out1[c // C1][0:T, t, c % C1:c % C1 + P], ident[0:T, 0:T])
                        else:
                            a, n = c // C1, C1 - c % C1
                            tp.matmul(ps[q % 4][0:n, i * T:(i + 1) * T], out1[a][0:T, t, c % C1:C1], ident[0:T, 0:T],
                                      start=True, stop=True)
                            ins = tp.matmul(ps[q % 4][n:P, i * T:(i + 1) * T], out1[a + 1][0:T, t, 0:P - n],
                                            ident[0:T, 0:T], start=True, stop=True)
                    OT.filled(ins)
            OT.wait_all_taken(pe, 2 * NT)
            pe.wait_ge(s_wa2, 1)
            for t in range(NT):
                H2H.wait_free(pe, t)
                for k in range(KD):
                    ins = tp.matmul(ps[t % 4][0:T, 0:196], out1T[:, k, t * T:(t + 1) * T], w2x[:, k, :],
                                    start=(k == 0), stop=(k == KD - 1))
                H2H.filled(ins)
            H2H.wait_all_taken(pe, NT)
            pe.wait_ge(s_h2ones, 1)
            heads(2, H2, C2, h2, H1)
            pe.wait_ge(s_hout, NT * (H1 + H2))
            for t in range(NT):
                O2.wait_free(pe, t)
                for h in range(H2):
                    ins = tp.transpose(ps[t % 4][0:C2, h * T:(h + 1) * T], out2[0:T, t, h, :], ident[0:T, 0:T])
                O2.filled(ins)
            O2.wait_all_taken(pe, NT)
            pe.wait_ge(s_wub, 16)
            for t in range(NT):
                for hf in range(2):
                    q = 2 * t + hf
                    if q >= 2:
                        pe.wait_ge(s_fin_taken, q - 1)
                    for h in range(H2):
                        ins = tp.matmul(ps[q % 2][0:T, 0:384], out2T[0:C2, h, t * T:(t + 1) * T],
                                        wub[0:C2, h, hf * 384:(hf + 1) * 384], start=(h == 0), stop=(h == H2 - 1))
                    ins.then_inc(s_fin, 1)
            ffn_pe(pe)

        @block.scalar
        def _(act):
            step = Chain(act, s_act)

            def take_xT(which):
                for t in range(NT):
                    q = (which * NT + t) * 2
                    XT.wait_filled(act, q)
                    if which == 0:
                        XT.taken(sc.activation(xnT[:, 0:3, t * T:(t + 1) * T],
                                               ps[q % 4][:, 0:3 * T].rearrange("p (k n) -> p k n", k=3), ACT.Copy), q)
                    else:
                        for i in range(3):
                            ins = sc.activation(xmT[:, i, t * T:(t + 1) * T], ps[q % 4][:, i * T:(i + 1) * T],
                                                ACT.Identity, scale=gcol[:, i:i + 1], bias=bcol[:, i:i + 1])
                        XT.taken(ins, q)

            act.dma_start(gcol, norm_g.rearrange("(k p) -> p k", p=P), allow_slow_non_contiguous=True).then_inc(s_gb, 16)
            act.dma_start(bcol, norm_b.rearrange("(k p) -> p k", p=P), allow_slow_non_contiguous=True).then_inc(s_gb, 16)
            act.dma_start(b1col, b1.rearrange("(k p) -> p k", p=P), allow_slow_non_contiguous=True).then_inc(s_gb, 16)
            act.dma_start(b2col[0:C2], b2.rearrange("(h p) -> p h", p=C2), allow_slow_non_contiguous=True).then_inc(s_b2, 16)
            act.wait_ge(s_const, 10)
            for j in range(NTM):
                act.dma_start(xg_dram[j * P:(j + 1) * P], zeros).then_inc(s_zero, 16)
            act.wait_ge(s_stats, 1)
            sc.activation(std[0:T], mv[0:T, :, 1], ACT.Sqrt, bias=epst[0:T]).then_inc(s_std, 1)
            take_xT(0)
            act.wait_ge(s_stats, 2)
            sc.activation(std[0:T], mv[0:T, :, 1], ACT.Sqrt, bias=epst[0:T]).then_inc(s_std, 1)
            act.wait_ge(s_gb, 48)
            take_xT(1)

            def take_h1(q):
                t = q // 2
                HH.wait_filled(act, q)
                sc.activation(h1[0:T, t, 0:2, 0:C1], ps[q % 4][0:T, 0:384].rearrange("p (h c) -> p h c", h=2), ACT.Copy)
                HH.taken(sc.activation(s1[0:T, t, 0].rearrange("p s a -> p (s a)"), ps[q % 4][0:T, 384:388], ACT.Copy), q)
            act.wait_ge(s_inval, 16)
            for t in range(NT):
                take_h1(2 * t)
            for t in range(NT):
                for hf in range(2):
                    act.wait_ge(s_kready, 2 * t + hf + 1)
                    if 2 * t + hf >= 2:
                        act.wait_ge(s_kfeat, 2 * t + hf - 1)
                    sc.activation(ebuf[0:T, hf, 0:384], ps[hf][0:T, 0:384], ACT.Exp)
                    sc.activation(rbuf[0:T, hf, 0:384], ps[hf][0:T, 0:384], ACT.Relu).then_inc(s_kexp, 1)
            for s in range(KD * DG):
                n = NG[s % DG][1]
                act.wait_ge(s_qpsum, s + 1)
                act.wait_ge(s_kfeat, 2 * NT)
                if s >= 2:
                    act.wait_ge(s_qfeat, s - 1)
                sc.activation(ebuf[:, s % 2, 0:n], ps[s % 2][:, 0:n], ACT.Exp)
                sc.activation(rbuf[:, s % 2, 0:n], ps[s % 2][:, 0:n], ACT.Relu).then_inc(s_qexp, 1)

            def heads(H, first, ssrc):
                for h in range(H):
                    n = first + h
                    for r in range(3):
                        act.wait_ge(s_rowps, 3 * n + r + 1)
                        if n >= 1 and r == 0:
                            act.wait_ge(s_t, NT * n)
                            act.wait_ge(s_u, NT * n)
                        for i in range(DG):
                            ins = sc.activation(rowbuf[:, r, NG[i][0]:NG[i][0] + NG[i][1]], ps[i][:, 0:NG[i][1]], ACT.Copy)
                        ins.then_inc(s_row, 1)
                    act.wait_ge(s_row, 3 * n + 3)
                    act.wait_ge(s_rowps, 3 * n + 3)

                    def lower(st):
                        j = n * NT + st
                        if j >= 2:
                            act.wait_ge(s_t, j - 1)
                        sc.activation(ubuf[0:T, j % 2], rowbuf[0:T, 2], ACT.Identity, bias=s02[0:T, st:st + 1]).then_inc(s_u, 1)

                    lower(0)
                    for st in range(NT):
                        j = n * NT + st
                        if st + 1 < NT:
                            lower(st + 1)
                        act.wait_ge(s_t, j + 1)
                        sc.activation(tbuf[0:T, j % 2], tbuf[0:T, j % 2], ACT.Exp).then_inc(s_e, 1)

            heads(H1, 0, None)
            for t in range(NT):
                q = 2 * t
                OT.wait_filled(act, q)
                for i in range(3):
                    ins = sc.activation(out1T[:, i, t * T:(t + 1) * T], ps[q % 4][:, i * T:(i + 1) * T],
                                        ACT.Identity, bias=b1col[:, i:i + 1])
                OT.taken(ins, q)
            for t in range(0, NT, 2):
                H2H.wait_filled(act, t)
                sc.activation(h2[0:T, t, :, 0:C2], ps[t % 4][0:T, 0:192].rearrange("p (h c) -> p h c", h=2), ACT.Copy)
                H2H.taken(sc.activation(s2[0:T, t].rearrange("p s a -> p (s a)"), ps[t % 4][0:T, 192:196], ACT.Copy), t)
            heads(H2, H1, None)
            for t in range(0, NT, 2):
                O2.wait_filled(act, t)
                act.wait_ge(s_b2, 16)
                for h in range(H2):
                    ins = sc.activation(out2T[0:C2, h, t * T:(t + 1) * T], ps[t % 4][0:C2, h * T:(h + 1) * T],
                                        ACT.Identity, bias=b2col[0:C2, h:h + 1])
                O2.taken(ins, t)
            ffn_act(act)

        @block.vector
        def _(dve):
            step = Chain(dve, s_dve)
            stt = dv.scalar_tensor_tensor

            dve.wait_ge(s_edges, 32)
            dve.wait_ge(s_const, 10)
            step(dv.tensor_copy(src_f[0:T], src_i.bitcast(I32)[0:T]))
            step(dv.tensor_copy(dst_f[0:T], dst_i.bitcast(I32)[0:T]))
            step.wait()
            step(dv.tensor_scalar(st_f[0:T], src_f[0:T], float(T), None, ALU.is_ge))
            step(dv.tensor_scalar(dg_f[0:T], dst_f[0:T], float(G), None, ALU.is_ge))
            for k in range(2, NT):
                step.wait()
                step(stt(out=st_f[0:T], in0=src_f[0:T], scalar=float(k * T), in1=st_f[0:T], op0=ALU.is_ge, op1=ALU.add))
            for k in range(2, DG):
                step.wait()
                step(stt(out=dg_f[0:T], in0=dst_f[0:T], scalar=float(k * G), in1=dg_f[0:T], op0=ALU.is_ge, op1=ALU.add))
            step.wait()
            step(stt(out=src_f[0:T], in0=st_f[0:T], scalar=-float(T), in1=src_f[0:T], op0=ALU.mult, op1=ALU.add))
            step(stt(out=dst_f[0:T], in0=dg_f[0:T], scalar=-float(G), in1=dst_f[0:T], op0=ALU.mult, op1=ALU.add))
            step(stt(out=st_f[0:T], in0=st_f[0:T], scalar=float(DG), in1=dg_f[0:T], op0=ALU.mult, op1=ALU.add))
            step.wait()
            step(stt(out=src_f[0:T], in0=src_f[0:T], scalar=float(SRS), in1=dst_f[0:T], op0=ALU.mult, op1=ALU.add))
            step.wait()
            dv.tensor_copy(edge_v[0:T], src_f[0:T])
            dv.tensor_tensor(onehot[0:T], iota[0:T, 0:NBK].unsqueeze(1).to_broadcast([T, EC, NBK]),
                             st_f[0:T].unsqueeze(2).to_broadcast([T, EC, NBK]), ALU.is_equal).then_inc(s_oh, 1)
            dve.wait_ge(s_avec, 32)
            dve.wait_ge(s_w1, 32)
            for k in range(KD):
                for h in range(H1):
                    for s in range(2):
                        step.wait(but=3)
                        ins = dv.tensor_tensor_reduce(ttr_junk[:, (2 * h + s) % 4], w1x[:, k, h // 2, (h % 2) * C1:(h % 2 + 1) * C1],
                                                      avec[:, s * D + h * C1:s * D + (h + 1) * C1], 1.0, 0.0,
                                                      ALU.mult, ALU.add, w1x[:, k, h // 2, 384 + 2 * s + h % 2:385 + 2 * s + h % 2])
                        step(ins)
            step.wait()
            dv.memset(junk8[:, 0:1], 0.0).then_inc(s_wa, 1)
            dve.wait_ge(s_tot, 1)
            step(dv.tensor_copy(tot0, ps[4][:, 0:NBK]))
            step(dv.tensor_copy(tot1[0:EC1], ps[5][0:EC1, 0:NBK]))
            step.wait()
            dv.tensor_tensor(base0, tot0.unsqueeze(1).to_broadcast([P, EC, NBK]),
                             later.unsqueeze(2).to_broadcast([P, EC, NBK]), ALU.mult)
            dv.tensor_tensor(base1[0:EC1], tot1[0:EC1].unsqueeze(1).to_broadcast([EC1, EC1, NBK]),
                             tri[0:EC1, 0:EC1].unsqueeze(2).to_broadcast([EC1, EC1, NBK]), ALU.mult).then_inc(s_br, 1)
            dve.wait_ge(s_cnt, 1)
            chi = chb.bitcast(I32)
            step(dv.tensor_scalar(chi[0:NBK, 1:2], ps[4][0:NBK, 32:33], float(P - 1), None, ALU.add))
            step.wait()
            step(dv.tensor_scalar(chi[0:NBK, 2:3], chi[0:NBK, 1:2], 7, None, ALU.arith_shift_right))
            step.wait()
            dv.tensor_copy(chb.bitcast(BF16)[0:NBK, 0:1], chi[0:NBK, 2:3]).then_inc(s_chunks, 1)
            dve.wait_ge(s_starts, 1)
            dv.tensor_scalar(startrow[0:1, 0:NBK], ps[5][0:1, 0:NBK], float(P), None, ALU.mult).then_inc(s_startrow, 1)
            step(dv.tensor_copy(junk8[0:NBK, 0:1], ps[5][0:NBK, 32:33]))
            step.wait()
            dv.tensor_scalar(cmpb[0:NBK, 0:NCH], iota[0:NBK, 0:NCH], junk8[0:NBK, 0:1], None, ALU.is_ge).then_inc(s_cmp, 1)
            for j in range(RJ):
                dve.wait_ge(s_rank, j + 1)
                cs = slice(RC * j, RC * j + RC)
                step.wait(but=1)
                ins = dv.tensor_tensor(rank_tmp[0:T, j % 2], ps[6 + j % 2][0:T, 0:RC * NBK].rearrange("p (c b) -> p c b", c=RC),
                                       onehot[0:T, cs, :], ALU.mult)
                ins.then_inc(s_rankfree, 1)
                dve.wait_ge(s_rankfree, j + 1)
                step(dv.tensor_reduce(rank[0:T, cs], rank_tmp[0:T, j % 2], AX.X, ALU.add))
            step.wait()
            step(dv.tensor_copy(slot_i[0:T], rank[0:T]))
            step.wait()
            step(dv.tensor_scalar(src_i.bitcast(I32)[0:T], slot_i[0:T], P - 1, None, ALU.bitwise_and))
            step(dv.tensor_scalar(dst_i.bitcast(I32)[0:T], slot_i[0:T], 7, None, ALU.arith_shift_right))
            step.wait()
            stt(out=slot_i[0:T], in0=src_i.bitcast(I32)[0:T], scalar=float(NCH), in1=dst_i.bitcast(I32)[0:T],
                op0=ALU.mult, op1=ALU.add).then_inc(s_slot, 1)
            dve.wait_ge(s_bk, 1)
            dv.tensor_scalar(offs_i[0:1], ps[4][0:1, 64:64 + NCH], float(NBK - 1), float(G), ALU.min, ALU.mult).then_inc(s_offs, 1)

            def norm_stats(xt, waits=None):
                for t in range(NT):
                    if waits and t % 2 == 0:
                        dve.wait_ge(waits[t // 2], 32)
                    for i in range(2):
                        ins = dv.bn_stats(stats[0:T, t, 6 * i:6 * i + 6], xt[0:T, t, i * 384:(i + 1) * 384])
                    step(ins)
                step.wait()
                for t in range(NT):
                    ins = dv.bn_aggr(mv[0:T, t, :], stats[0:T, t, :])
                return ins

            norm_stats(xs, s_x).then_inc(s_stats, 1)
            dve.wait_ge(s_std, 1)
            step(dv.reciprocal(rstd[0:T], std[0:T]))
            step.wait()
            for t in range(NT):
                dv.tensor_scalar(xs[0:T, t], xs[0:T, t], mv[0:T, t, 0:1], rstd[0:T, t:t + 1], ALU.subtract, ALU.mult)\
                    .then_inc(s_xn, 1)
            for t in range(NT):
                q = 2 * t + 1
                XT.wait_filled(dve, q)
                XT.taken(dv.tensor_copy(xnT[:, 3:6, t * T:(t + 1) * T],
                                        ps[q % 4][:, 0:3 * T].rearrange("p (k n) -> p k n", k=3)), q)
            dve.wait_ge(s_xn, NT)
            norm_stats(xs).then_inc(s_stats, 1)
            dve.wait_ge(s_std, 2)
            step(dv.reciprocal(rstd[0:T], std[0:T]))
            step.wait()
            for t in range(NT):
                dv.tensor_scalar(xm[0:T, t], xs[0:T, t], mv[0:T, t, 0:1], rstd[0:T, t:t + 1], ALU.subtract, ALU.mult)\
                    .then_inc(s_xn, 1)
            dve.wait_ge(s_gb, 48)
            for t in range(NT):
                q = (NT + t) * 2 + 1
                XT.wait_filled(dve, q)
                for i in range(3):
                    ins = dv.tensor_scalar(xmT[:, 3 + i, t * T:(t + 1) * T], ps[q % 4][:, i * T:(i + 1) * T],
                                           gcol[:, 3 + i:4 + i], bcol[:, 3 + i:4 + i], ALU.mult, ALU.add)
                XT.taken(ins, q)
            dve.wait_ge(s_wa, 1)
            dve.wait_ge(s_inval, 16)
            dv.memset(h1[0:T, :, :, C1:C1 + 1], 1.0).then_inc(s_h1ones, 1)
            for t in range(NT):
                q = 2 * t + 1
                HH.wait_filled(dve, q)
                dv.tensor_copy(h1[0:T, t, 2:4, 0:C1], ps[q % 4][0:T, 0:384].rearrange("p (h c) -> p h c", h=2))
                HH.taken(dv.tensor_copy(s1[0:T, t, 1].rearrange("p s a -> p (s a)"), ps[q % 4][0:T, 384:388]), q)
            HH.wait_all_taken(dve, 2 * NT)
            step(dv.memset(vbuf[0:T, :, :, P:P + 1], 1.0))
            step.wait()
            for t in range(NT):
                for hf in range(2):
                    dve.wait_ge(s_kexp, 2 * t + hf + 1)
                    if t >= 2:
                        dve.wait_ge(s_kvused, t - 1)
                    stt(out=kbuf[0:T, t % 2, hf * 384:(hf + 1) * 384], in0=ebuf[0:T, hf, 0:384], scalar=1.0,
                        in1=rbuf[0:T, hf, 0:384], op0=ALU.min, op1=ALU.add).then_inc(s_kfeat, 1)
                for hf in range(2):
                    dve.wait_ge(s_vready, 2 * t + hf + 1)
                    dv.tensor_copy(vbuf[0:T, t % 2, 3 * hf:3 * hf + 3, 0:P],
                                   ps[2 + hf][0:T, 0:384].rearrange("p (k n) -> p k n", k=3)).then_inc(s_vsb, 1)
            dve.wait_ge(s_bias, 32)
            step(dv.tensor_tensor(biasb, biasb, bias2, ALU.add))
            step.wait()
            step(dv.memset(kvb, 0.0))
            step(dv.memset(ksb, 0.0))
            step.wait()
            dve.wait_ge(s_kvused, NT)
            for b in range(2):
                acc = ps[4 + b][:, 0:387].rearrange("p (k n) -> p k n", k=3)
                for hd in range(2):
                    r = slice(64 * hd, 64 * hd + 64)
                    dv.tensor_copy(kvb[r, 3 * b:3 * b + 3, 64 * hd:64 * hd + 64], acc[r, :, 64 * hd:64 * hd + 64])
                    ins = dv.tensor_copy(ksb[r, 3 * b:3 * b + 3, 64 * hd:64 * hd + 64],
                                         acc[r, :, 128:129].to_broadcast([64, 3, 64]))
            ins.then_inc(s_kvblk, 1)

            def mix_out(s):
                mb, i = s // DG, s % DG
                n0, n = NG[i]
                dve.wait_ge(s_den, s + 1)
                if s:
                    dve.wait_ge(s_mixT, s)
                step(dv.reciprocal(dbuf[:, 0:n], ps[6 + s % 2][:, 0:n]))
                step.wait()
                dv.tensor_tensor(mixT[:, mb, n0:n0 + n], ps[2 + s % 2][:, 0:n], dbuf[:, 0:n], ALU.mult).then_inc(s_mixT, 1)

            for s in range(KD * DG):
                n = NG[s % DG][1]
                dve.wait_ge(s_qexp, s + 1)
                if s >= 2:
                    dve.wait_ge(s_den, s - 1)
                stt(out=qbuf[:, s % 2, 0:n], in0=ebuf[:, s % 2, 0:n], scalar=1.0, in1=rbuf[:, s % 2, 0:n],
                    op0=ALU.min, op1=ALU.add).then_inc(s_qfeat, 1)
                if s >= 1:
                    mix_out(s - 1)
            mix_out(KD * DG - 1)
            for q in range(2 * NT):
                t, hf = q // 2, q % 2
                dve.wait_ge(s_mixps, q + 1)
                if t >= 2:
                    dve.wait_ge(s_mixout[t % 2], 32 * (t // 2))
                dv.tensor_tensor(mrow[0:T, t % 2, hf * 384:(hf + 1) * 384], ps[q % 2][0:T, 0:384],
                                 biasb[0:T, hf * 384:(hf + 1) * 384], ALU.add).then_inc(s_mixrow, 1)
            dve.wait_ge(s_mixps, 2 * NT)
            for i in range(2):
                dve.wait_ge(s_mixout[i], 32 * NT // 2)
            step(dv.memset(counts_flat[0:T], 0.0))
            dve.wait_ge(s_tabin, 16)
            step(dv.tensor_scalar(vtmp, vtab, 9, None, ALU.arith_shift_right))
            step.wait()
            step(dv.tensor_copy(srow[:, 0:NCH], vtmp))
            step.wait()
            step(dv.tensor_scalar(vtmp, vtab, SRS - 1, None, ALU.bitwise_and))
            step.wait()
            step(dv.tensor_copy(dcol[:, 0:NCH], vtmp))
            step(dv.memset(srow[:, NCH:NCH + 1], -1.0))
            step(dv.memset(dcol[:, NCH:NCH + 1], -1.0))
            for t in range(NT):
                step(dv.tensor_copy(counts[0:T, t, t * T:(t + 1) * T], ident[0:T, 0:T]))
            step.wait()
            for i in range(2):
                dv.memset(junk8[:, 1 + i:2 + i], 0.0).then_inc(s_acc, 1)

            def onehots(j, b, first=False):
                if not first:
                    dve.wait_ge(s_cps, j - 1)
                dv.tensor_scalar(ohs[:, b, 0:T], iota_h[:, 0:T], srow[:, bass.ds(j, 1)], None, ALU.is_equal)
                dv.tensor_scalar(ohd[:, b, 0:G], iota_h[:, 0:G], dcol[:, bass.ds(j, 1)], None, ALU.is_equal)\
                    .then_inc(s_ohb, 1)

            def count(j, b):
                dve.wait_ge(s_cps, j + 1)
                dve.wait_ge(s_acc, j + 2)
                off = dve.value_load(offs_i[0:1, bass.ds(j, 1)], min_val=0, max_val=(NBK - 1) * G)
                o = counts_flat[0:T, bass.ds(off, G)]
                dv.tensor_tensor(o, o, ps[b][0:T, 0:G], ALU.add).then_inc(s_acc, 1)

            dve.wait_ge(s_offs, 1)
            onehots(0, 0, True)
            onehots(1, 1, True)
            count(0, 0)
            onehots(2, 0)
            count(1, 1)
            with dve.Fori(1, NCH // 2) as i:
                onehots(2 * i + 1, 1)
                count(2 * i, 0)
                onehots(2 * i + 2, 0)
                count(2 * i + 1, 1)
            dve.wait_ge(s_acc, NCH + 2)
            for dt in range(NT):
                dve.wait_ge(s_mskT, dt + 1)
                for i, (a, n) in enumerate([(0, 500), (500, 500), (1000, 250)]):
                    dv.tensor_scalar(mask[0:T, dt, a:a + n], ps[(dt % 2) * 4 + i][0:T, 0:n], 0.0, MASKED,
                                     ALU.is_equal, ALU.mult).then_inc(s_mask, 1)
            dve.wait_ge(s_mask, 3 * NT)
            dve.wait_ge(s_w2, 48)
            for k in range(KD):
                for h in range(H2):
                    for s in range(2):
                        step.wait(but=3)
                        ins = dv.tensor_tensor_reduce(tbuf[:, s, h * C2:(h + 1) * C2], w2x[:, k, h * C2:(h + 1) * C2],
                                                      avec2[:, s * 192 + h * C2:s * 192 + (h + 1) * C2], 1.0, 0.0,
                                                      ALU.mult, ALU.add, w2x[:, k, 192 + 2 * s + h:193 + 2 * s + h])
                        step(ins)
            step.wait()
            dv.memset(junk8[:, 3:4], 0.0).then_inc(s_wa2, 1)
            dve.wait_ge(s_wa2, 1)

            def heads(H, C, first, score, dest):
                for h in range(H):
                    n = first + h
                    ssrc, sdst = score(h)
                    diag = ubuf.rearrange("p b n -> p (b n)")[0:T, 0:N].rearrange("p (t m) -> p t m", t=NT)

                    def row(r, col):
                        if r or n:
                            dve.wait_ge(s_rowps, 3 * n + r)
                        dv.tensor_tensor(diag, ident[0:T, 0:T].unsqueeze(1).to_broadcast([T, NT, T]),
                                         col.unsqueeze(2).to_broadcast([T, NT, T]), ALU.mult).then_inc(s_diag, 1)

                    if n:
                        dve.wait_ge(s_t, NT * n)
                    row(0, ssrc)
                    dve.wait_ge(s_row, 3 * n + 1)
                    for dt in range(NT):
                        if dt == 0 and n:
                            dve.wait_ge(s_pt, NT * n)
                        step.wait(but=1)
                        ins = dv.tensor_tensor_reduce(tbuf[0:T, dt % 2], mask[0:T, dt], rowbuf[0:T, 0], 1.0, -3.0e38,
                                                      ALU.add, ALU.max, smax[0:T, dt:dt + 1])
                        step(ins)
                    step.wait()
                    step(dv.tensor_tensor(zt[0:T], smax[0:T], sdst, ALU.add))
                    step.wait()
                    step(stt(out=mt[0:T], in0=zt[0:T], scalar=SLOPE, in1=zt[0:T], op0=ALU.mult, op1=ALU.max))
                    step.wait()
                    dve.wait_ge(s_diag, 3 * n + 1)
                    step(dv.tensor_tensor(arow[0:T], sdst, mt[0:T], ALU.subtract))
                    step(stt(out=brow[0:T], in0=sdst, scalar=SLOPE, in1=mt[0:T], op0=ALU.mult, op1=ALU.subtract))
                    step(dv.tensor_scalar(s02[0:T], ssrc, SLOPE, None, ALU.mult))
                    step.wait()
                    row(1, arow[0:T])
                    row(2, brow[0:T])

                    def weigh(st):
                        j = n * NT + st
                        dve.wait_ge(s_e, j + 1)
                        if j >= NPT:
                            dve.wait_ge(s_ptused, j - NPT + 1)
                        stt(out=ptile[0:T, j % NPT], in0=tbuf[0:T, j % 2], scalar=1.0, in1=counts[0:T, st, 0:N],
                            op0=ALU.min, op1=ALU.mult).then_inc(s_pt, 1)

                    for st in range(NT):
                        j = n * NT + st
                        dve.wait_ge(s_u, j + 1)
                        if st == 0:
                            dve.wait_ge(s_row, 3 * n + 3)
                        if st >= 2:
                            dve.wait_ge(s_pt, j - 1)
                        stt(out=tbuf[0:T, j % 2], in0=rowbuf[0:T, 1], scalar=ssrc[:, st:st + 1], in1=ubuf[0:T, j % 2],
                            op0=ALU.add, op1=ALU.max).then_inc(s_t, 1)
                        if st >= 1:
                            weigh(st - 1)
                    weigh(NT - 1)
                    dve.wait_ge(s_ptused, NT * (n + 1))
                    if n:
                        dve.wait_ge(s_hout, NT * n)
                    for b in range(NT // 2):
                        step(dv.reciprocal(rec[0:T, 2 * b:2 * b + 2],
                                           ps[3 + b][0:T, 0:2 * (C + 1)].rearrange("p (d c) -> p d c", d=2)[:, :, C]))
                    step.wait()
                    for dt in range(NT):
                        dv.tensor_scalar(dest(h, dt), ps[3 + dt // 2][0:T, (dt % 2) * (C + 1):(dt % 2) * (C + 1) + C],
                                         rec[0:T, dt:dt + 1], None, ALU.mult).then_inc(s_hout, 1)

            heads(H1, C1, 0, lambda h: (s1[0:T, :, h // 2, 0, h % 2], s1[0:T, :, h // 2, 1, h % 2]),
                  lambda h, dt: out1[h][0:T, dt])
            for t in range(NT):
                q = 2 * t + 1
                OT.wait_filled(dve, q)
                for i in range(3):
                    ins = dv.tensor_scalar(out1T[:, 3 + i, t * T:(t + 1) * T], ps[q % 4][:, i * T:(i + 1) * T],
                                           b1col[:, 3 + i:4 + i], None, ALU.add)
                OT.taken(ins, q)
            dv.memset(h2[0:T, :, :, C2:C2 + 1], 1.0).then_inc(s_h2ones, 1)
            for t in range(1, NT, 2):
                H2H.wait_filled(dve, t)
                dv.tensor_copy(h2[0:T, t, :, 0:C2], ps[t % 4][0:T, 0:192].rearrange("p (h c) -> p h c", h=2))
                H2H.taken(dv.tensor_copy(s2[0:T, t].rearrange("p s a -> p (s a)"), ps[t % 4][0:T, 192:196]), t)
            H2H.wait_all_taken(dve, NT)
            heads(H2, C2, H1, lambda h: (s2[0:T, :, 0, h], s2[0:T, :, 1, h]), lambda h, dt: out2[0:T, dt, h])
            dve.wait_ge(s_b2, 16)
            for t in range(1, NT, 2):
                O2.wait_filled(dve, t)
                for h in range(H2):
                    ins = dv.tensor_scalar(out2T[0:C2, h, t * T:(t + 1) * T], ps[t % 4][0:C2, h * T:(h + 1) * T],
                                           b2col[0:C2, h:h + 1], None, ALU.add)
                O2.taken(ins, t)
            for t in range(NT):
                dve.wait_ge(s_res[t % 2], 64 * (t // 2 + 1))
                step(dv.tensor_tensor(mixin[0:T, t % 2], mixin[0:T, t % 2], xin[0:T, t % 2], ALU.add))
                step.wait()
                for hf in range(2):
                    q = 2 * t + hf
                    dve.wait_ge(s_fin, q + 1)
                    ins = dv.tensor_tensor(x2[0:T, t, hf * 384:(hf + 1) * 384], ps[q % 2][0:T, 0:384],
                                           mixin[0:T, t % 2, hf * 384:(hf + 1) * 384], ALU.add)
                    ins.then_inc(s_fin_taken, 1)
                    if hf:
                        dve.wait_ge(s_fin_taken, q + 1)
                dv.memset(junk8[:, 2:3], 0.0).then_inc(s_resfree, 1)
            ffn_dve(dve, step, norm_stats)


_INS = ['x', 'src', 'dst', 'L0_gnn_norm_g', 'L0_gnn_norm_b', 'L0_gnn_W1', 'L0_gnn_a_src1', 'L0_gnn_a_dst1', 'L0_gnn_b1',
        'L0_gnn_W2', 'L0_gnn_a_src2', 'L0_gnn_a_dst2', 'L0_gnn_b2', 'L0_gnn_Wu', 'L0_gnn_bu', 'L0_mix_w_qkv',
        'L0_mix_w_proj', 'L0_mix_b_proj', 'L0_ffn_router_w', 'L0_ffn_w_gate', 'L0_ffn_w_up', 'L0_ffn_w_down',
        'L0_ffn_ws_gate', 'L0_ffn_ws_up', 'L0_ffn_ws_down', 'L0_ffn_sg_w', 'L0_ffn_sg_b']
_OUTS = [((1250, 768), 'float32')]


def kernel(**inputs):
    import numpy as _np
    import concourse.bacc as _bacc
    from concourse import mybir as _mybir
    from concourse.bass_utils import run_bass_kernel_spmd as _run

    nc = _bacc.Bacc("TRN2", target_bir_lowering=False, num_devices=1)
    arrays, args = {}, []
    for name in _INS:
        a = _np.ascontiguousarray(inputs[name])
        arrays[f"in_{name}_dram"] = a
        args.append(nc.dram_tensor(f"in_{name}_dram", a.shape, _mybir.dt.from_np(a.dtype), kind="ExternalInput").ap())
    for i, (shape, dtype) in enumerate(_OUTS):
        dt = _mybir.dt.from_np(_np.dtype(dtype))
        args.append(nc.dram_tensor(f"out_{i}_dram", shape, dt, kind="ExternalOutput").ap())
    gps_layer(nc, *args)
    r = _run(nc, [arrays], core_ids=[0])
    got = tuple(r.results[0][f"out_{i}_dram"] for i in range(len(_OUTS)))
    return got[0]
```

```python
from contextlib import ExitStack

import concourse.bass as bass
from concourse import mybir

F32 = mybir.dt.float32
BF16 = mybir.dt.bfloat16
F16 = mybir.dt.float16
I32 = mybir.dt.int32
U32 = mybir.dt.uint32
U16 = mybir.dt.uint16
ALU = mybir.AluOpType
ACT = mybir.ActivationFunctionType
AX = mybir.AxisListType

P = 128
EPS = 1e-5
SLOPE = 0.2
MASKED = -1.0e30
ARENA = 52900
SMALL = 3420


class Handoff:

    def __init__(self, ready, freed, slots, first=0):
        self.ready, self.freed, self.slots, self.first = ready, freed, slots, first

    def after(self, jobs):
        assert jobs % 2 == 0
        return Handoff(self.ready, self.freed, self.slots, self.first + jobs)

    def wait_free(self, pe, q):
        if q >= self.slots:
            p = self.first + q - self.slots
            pe.wait_ge(self.freed[p % 2], p // 2 + 1)

    def filled(self, ins):
        ins.then_inc(self.ready, 1)

    def wait_filled(self, eng, q):
        eng.wait_ge(self.ready, self.first + q + 1)

    def taken(self, ins, q):
        ins.then_inc(self.freed[q % 2], 1)

    def wait_all_taken(self, eng, n):
        eng.wait_ge(self.freed[0], (self.first + n) // 2)
        eng.wait_ge(self.freed[1], (self.first + n) // 2)


class Chain:

    def __init__(self, eng, sem):
        self.eng, self.sem, self.n = eng, sem, 0

    def __call__(self, ins):
        ins.then_inc(self.sem, 1)
        self.n += 1
        return ins

    def wait(self, but=0):
        if self.n > but:
            self.eng.wait_ge(self.sem, self.n - but)


def gps_layer(nc, x, src, dst, norm_g, norm_b, W1, a_src1, a_dst1, b1, W2, a_src2, a_dst2, b2, Wu, bu,
              w_qkv, w_proj, b_proj, router_w, w_gate, w_up, w_down, ws_gate, ws_up, ws_down, sg_w, sg_b,
              out):
    N, D = x.shape
    KD = D // P
    NT = 10
    T = N // NT
    E = src.shape[0]
    EC = E // T
    H1, C1 = a_src1.shape
    H2, C2 = a_src2.shape
    DG = 3
    G = -(-N // DG)
    NBK = NT * DG
    CW = DG * G
    NCH = (E + NBK * (P - 1)) // P
    NCH += NCH % 2
    NPQ = max(0, NCH // 2 - 4 * 2 * NT)
    SRS = 512
    NE = router_w.shape[1]
    HS = ws_gate.shape[1]
    NTM = (2 * N + NE * (P - 1)) // P
    assert T * NT == N and T * EC == E and T <= P and G <= 512 and NTM % 2 == 1
    NG = [(i * G, min(G, N - i * G)) for i in range(DG)]

    with ExitStack() as ctx:
        def sem(name):
            return ctx.enter_context(nc.semaphore(name))

        arena = ctx.enter_context(nc.sbuf_tensor("arena", [P, ARENA], F32))
        ps = [ctx.enter_context(nc.psum_tensor(f"bank{i}", [P, 512], F32)) for i in range(8)]

        def words(off, n, dt=F32):
            v = arena[:, off:off + n]
            return v if dt == F32 else v.bitcast(dt)

        small_at = [0]

        def small(n, dt=F32):
            w = n if dt in (F32, I32, U32) else (n + 1) // 2
            v = words(small_at[0], w, dt)
            small_at[0] += w
            assert small_at[0] <= SMALL, small_at
            return v

        ident = small(P)
        ones = small(P)
        route0 = small_at[0]
        zeros = small(D)
        iota_i = small(G, I32)
        route1 = small_at[0]
        ones_b = small(P, BF16)
        tri = small(P, BF16)
        triinc = small(P, BF16)
        later = small(EC, BF16)
        iota = small(G)
        iota_h = small(G + 1, F16)
        epst = small(1)
        stats = small(NT * 12).rearrange("p (t s) -> p t s", t=NT)
        mv = small(NT * 2).rearrange("p (t s) -> p t s", t=NT)
        std = small(NT)
        rstd = small(NT)
        gcol = small(KD)
        bcol = small(KD)
        b1col = small(KD)
        b2col = small(2)
        s1 = small(NT * 8).rearrange("p (t h s a) -> p t h s a", t=NT, h=2, s=2)
        s2 = small(NT * 4).rearrange("p (t s a) -> p t s a", t=NT, s=2)
        smax = small(NT)
        zt = small(NT)
        mt = small(NT)
        arow = small(NT)
        brow = small(NT)
        s02 = small(2 * NT).rearrange("p (b t) -> p b t", b=2)
        rec = small(NT)
        slot_i = small(EC, I32)
        edge_v = small(EC, I32)
        offs_i = small(NCH, I32)
        junk8 = small(8)

        A0 = SMALL
        B0 = A0 + NT * D
        F0 = B0 + NT * D
        C0 = F0 + 4 * 193 * NT
        D0 = C0 + KD * N
        E0 = D0 + KD * N
        G0 = E0 + 776 * KD
        assert G0 + 6700 <= ARENA

        x_rows = x.rearrange("(t p) d -> p t d", p=T)
        out_rows = out.rearrange("(t p) d -> p t d", p=T)

        def scratch(name, shape, dt):
            return nc.dram_tensor(name, shape, dt, kind="Internal").ap()

        edge_table = scratch("edge_table", [P * NCH, 1], I32)
        mixed_dram = scratch("mixed_rows", [N, D], F32)
        xg_dram = scratch("expert_in", [NTM * P, D], F32)
        yg_dram = scratch("expert_out", [NTM * P, D], F32)

        s_const = sem("const_ready")
        s_edges = sem("edges_in")
        s_gb = sem("gain_bias_in")
        s_x = [sem(f"x_in{g}") for g in range(5)]
        s_avec = sem("avec_in")
        s_w1 = sem("w1_in")
        s_stats = sem("ln_stats")
        s_std = sem("ln_std")
        s_xn = sem("xn_ready")
        s_oh = sem("edge_onehot")
        s_tot = sem("edge_totals")
        s_br = sem("edge_base_ready")
        s_cnt = sem("bucket_counts")
        s_chunks = sem("bucket_chunks")
        s_starts = sem("bucket_starts")
        s_startrow = sem("start_row")
        s_cmp = sem("chunk_cmp")
        s_bk = sem("chunk_bucket")
        s_rank = sem("rank_ready")
        s_rankfree = sem("rank_taken")
        s_slot = sem("slots_ready")
        s_inval = sem("table_invalid")
        s_invmem = sem("invalid_words")
        s_scat = sem("edges_scattered")
        s_tabin = sem("table_in")
        s_wa = sem("wa_ready")
        s_h1ones = sem("h1_ones")
        s_dve = sem("dve_step")
        s_pool = sem("pool_step")
        s_offs = sem("chunk_offsets")
        s_fin_taken = sem("gnn_taken")
        s_zero = sem("slots_zeroed")
        XT = Handoff(sem("banks_filled"), [sem("banks_taken_act"), sem("banks_taken_dve")], 4)
        HH = XT.after(4 * NT)

        xs = words(A0, NT * D).rearrange("p (t d) -> p t d", t=NT)
        rescale = words(B0, N).rearrange("p (t m) -> p t m", t=NT)
        var2 = words(B0 + N, NT)
        std2 = words(B0 + N + NT, NT)
        rstd2 = words(B0 + N + 2 * NT, NT)
        avec = words(F0 + 4 * C1, 2 * D)
        xnT = words(C0, KD * N).rearrange("p (k n) -> p k n", k=KD)
        xmT = words(D0, KD * N).rearrange("p (k n) -> p k n", k=KD)
        w1x = words(E0, 776 * KD).rearrange("p (k h n) -> p k h n", k=KD, h=2)
        h1 = words(F0, 772 * NT).rearrange("p (t h c) -> p t h c", t=NT, h=H1)
        ttr_junk = words(F0, 4 * C1).rearrange("p (b c) -> p b c", b=4)

        g = G0
        onehot = words(g, EC * NBK // 2, BF16).rearrange("p (c b) -> p c b", c=EC)
        g += EC * NBK // 2
        base0 = words(g, EC * NBK // 2, BF16).rearrange("p (c b) -> p c b", c=EC)
        g += EC * NBK // 2
        EC1 = EC - P
        base1 = words(g, EC1 * NBK // 2, BF16).rearrange("p (c b) -> p c b", c=EC1)
        g += EC1 * NBK // 2
        ef = words(g, 6 * EC).rearrange("p (i c) -> p i c", i=6)
        src_i, dst_i, src_f, dst_f, st_f, dg_f = [ef[:, i, :] for i in range(6)]
        g += 6 * EC
        tot0 = words(g, NBK // 2, BF16)
        g += NBK // 2
        tot1 = words(g, NBK // 2, BF16)
        g += NBK // 2
        chb = words(g, 4)
        g += 4
        startrow = words(g, NBK // 2, BF16)
        g += NBK // 2
        cmpb = words(g, NCH // 2, BF16)
        g += NCH // 2
        assert g <= ARENA, g
        invalid = words(g, NCH, I32)
        g += NCH
        assert g <= ARENA, g
        rank_tmp = words(F0 - 1120, 960).rearrange("p (i c b) -> p i c b", i=2, c=16)
        rank = words(F0 - 160, EC)
        RC = 16
        RJ = EC // RC

        wkv = words(A0, 2 * D * KD).rearrange("p (k n) -> p k n", k=KD)
        m = A0 + 2 * D * KD
        kbuf = words(m, 2 * D).rearrange("p (b n) -> p b n", b=2)
        m += 2 * D
        vbuf = words(m, 2 * KD * 129).rearrange("p (b k n) -> p b k n", b=2, k=KD)
        m += 2 * KD * 129
        ohs = words(m, 4 * 64, BF16).rearrange("p (b n) -> p b n", b=4)
        m += 4 * 64
        ohd = words(m, 4 * 210, BF16).rearrange("p (b n) -> p b n", b=4)
        m += 4 * 210
        vtab = words(m, NCH, I32)
        m += NCH
        vtmp = words(m, NCH, I32)
        m += NCH
        srow = words(m, NCH)
        m += NCH
        dcol = words(m, NCH)
        m += NCH
        assert m <= F0 - 1120, (m, F0)
        wq = words(E0, D * KD).rearrange("p (k n) -> p k n", k=KD)
        mixT = words(D0, KD * N).rearrange("p (k n) -> p k n", k=KD)
        CW16 = NT * CW // 2 + 1
        counts_flat = words(A0, CW16, U16)[:, 0:NT * CW]
        counts = counts_flat.rearrange("p (t n) -> p t n", t=NT)
        m = A0 + CW16
        wout = [words(w, 384 * 2 * KD).rearrange("p (k n) -> p k n", k=2 * KD) for w in (m, E0)]
        m += 384 * 2 * KD
        mrow = words(m, 2 * 384).rearrange("p (b n) -> p b n", b=2)
        m += 2 * 384
        assert m <= A0 + 2 * D * KD + 2 * D + 2 * KD * 129
        m = G0
        qbuf = words(m, 2 * G).rearrange("p (b n) -> p b n", b=2)
        m += 2 * G
        ebuf = words(m, 2 * G).rearrange("p (b n) -> p b n", b=2)
        m += 2 * G
        rbuf = words(m, 2 * G).rearrange("p (b n) -> p b n", b=2)
        m += 2 * G
        dbuf = words(m, G)
        m += G
        kvb = words(m, D).rearrange("p (k n) -> p k n", k=KD)
        m += D
        ksb = words(m, D).rearrange("p (k n) -> p k n", k=KD)
        m += D
        biasb = words(m, D)
        m += D
        assert m <= ARENA, m
        bias2 = kvb.rearrange("p k n -> p (k n)")

        s_wkv = sem("wkv_in")
        s_wq = sem("wq_in")
        s_wout = [sem(f"wout_in{i}") for i in range(2)]
        s_bias = sem("bias_in")
        s_kready = sem("k_psum")
        s_kexp = sem("k_exp")
        s_kfeat = sem("k_feature")
        s_vready = sem("v_psum")
        s_vsb = sem("v_sb")
        s_kvused = sem("kv_used")
        s_kvblk = sem("kv_blocks")
        s_qpsum = sem("q_psum")
        s_qexp = sem("q_exp")
        s_qfeat = sem("q_feature")
        s_den = sem("attn_psum")
        s_mixT = sem("mixT_ready")
        s_mixps = sem("mix_psum")
        s_mixrow = sem("mix_row")
        s_mixout = [sem(f"mix_out{i}") for i in range(2)]

        m = A0 + CW16
        out1 = [words(m + h * NT * C1, NT * C1).rearrange("p (t c) -> p t c", t=NT) for h in range(H1)]
        m += H1 * NT * C1
        assert m <= F0
        m = C0
        mask = words(m, NT * N // 2, BF16).rearrange("p (t n) -> p t n", t=NT)
        m += NT * N // 2
        NPT = 3
        out1T_at = m
        ptile = words(m, NPT * N).rearrange("p (b n) -> p b n", b=NPT)
        m += NPT * N
        ubuf = words(m, 2 * N).rearrange("p (b n) -> p b n", b=2)
        m += 2 * N
        tbuf = words(m, 2 * N).rearrange("p (b n) -> p b n", b=2)
        m += 2 * N
        rowbuf = words(m, 3 * N).rearrange("p (b n) -> p b n", b=3)
        m += 3 * N
        diags = words(m, 2 * N).rearrange("p (b n) -> p b n", b=2)
        m += 2 * N
        junk = words(m, N, BF16).rearrange("p (b n) -> p b n", b=2)
        m += N
        w2x = words(m, KD * 196).rearrange("p (k n) -> p k n", k=KD)
        m += KD * 196
        avec2 = words(m, 2 * H2 * C2)
        m += 2 * H2 * C2
        xin = words(m, 2 * D).rearrange("p (b n) -> p b n", b=2)
        m += 2 * D
        assert m <= ARENA, m
        out1T = words(out1T_at, KD * N).rearrange("p (k n) -> p k n", k=KD)
        assert KD * N <= 9 * N
        h2 = words(F0, NT * H2 * (C2 + 1)).rearrange("p (t h c) -> p t h c", t=NT, h=H2)
        m = F0 + NT * H2 * (C2 + 1)
        out2 = words(m, NT * H2 * C2).rearrange("p (t h c) -> p t h c", t=NT, h=H2)
        m += NT * H2 * C2
        out2T = words(m, H2 * N).rearrange("p (h n) -> p h n", h=H2)
        m += H2 * N
        wub = [words(A0 + CW16 + NT * D, D), words(m, D)]
        assert m + D <= C0 and A0 + CW16 + NT * D + D <= F0
        x2 = words(A0, NT * D).rearrange("p (t d) -> p t d", t=NT)
        mixin = words(A0 + CW16, NT * D).rearrange("p (t n) -> p t n", t=NT)

        s_ohb = sem("chunk_onehots")
        s_cps = sem("chunk_psum")
        s_acc = sem("chunk_counted")
        s_mskT = sem("mask_psum")
        s_mask = sem("mask_ready")
        s_w2 = sem("w2_in")
        s_wa2 = sem("wa2_ready")
        s_diag = sem("row_diag")
        s_rowps = sem("row_psum")
        s_row = sem("row_copied")
        s_u = sem("head_u")
        s_t = sem("head_t")
        s_e = sem("head_exp")
        s_pt = sem("head_p")
        s_ptused = sem("head_p_used")
        s_hout = sem("head_out")
        s_h2ones = sem("h2_ones")
        OT = HH.after(2 * NT)
        H2H = OT.after(2 * NT)
        O2 = H2H.after(NT)
        s_wub = sem("wub_in")
        s_cf = sem("counts_as_float")

        row_order = []
        for first, H in ((0, H1), (H1, H2)):
            row_order.append(("s", first))
            for n in range(first, first + H):
                row_order += [("a", n), ("b", n)] + [("s", n + 1)] * (n + 1 < first + H)

        def row_no(kind, n):
            return row_order.index((kind, n))

        s_b2 = sem("b2_in")
        s_res = [sem(f"residual_in{i}") for i in range(2)]
        s_fin = sem("gnn_psum")
        s_resadd = sem("residual_added")

        xf = words(B0, NT * D).rearrange("p (t d) -> p t d", t=NT)
        xfT = words(F0, KD * N).rearrange("p (k n) -> p k n", k=KD)
        wsgu = words(F0 + KD * N, KD * 2 * HS).rearrange("p (k n) -> p k n", k=KD)
        m = F0 + KD * N + KD * 2 * HS
        KS = HS // P
        wsd = words(m, KS * D).rearrange("p (k n) -> p k n", k=KS)
        m += KS * D
        rwx = words(m, KD * 9).rearrange("p (k n) -> p k n", k=KD)
        m += KD * 9
        sg_s = words(m, 2 * HS).rearrange("p (b n) -> p b n", b=2)
        m += 2 * HS
        sg_h = words(m, 2 * HS).rearrange("p (b n) -> p b n", b=2)
        m += 2 * HS
        sg_hT = words(m, 2 * KS * T).rearrange("p (b k n) -> p b k n", b=2, k=KS)
        m += 2 * KS * T
        assert m <= 36004, m
        m = 36004
        xgb = words(m, 2 * D).rearrange("p (b n) -> p b n", b=2)
        m += 2 * D
        xgT = words(m, 2 * D).rearrange("p (b k n) -> p b k n", b=2, k=KD)
        m += 2 * D
        WB = [ARENA - 3 * KD * D, B0]
        assert m <= WB[0], (m, WB)
        ew = [[words(w + i * KD * D, KD * D).rearrange("p (k n) -> p k n", k=KD) for i in range(3)] for w in WB]

        def expert_cols(i, at, k, c, n):
            return arena[:, bass.ds(at + ((i * KD + k) * D + c), n)]

        m = WB[1] + 3 * KD * D
        gs = words(m, 2 * D).rearrange("p (b n) -> p b n", b=2)
        m += 2 * D
        hh = words(m, 2 * D).rearrange("p (b n) -> p b n", b=2)
        m += 2 * D
        hT = words(m, 2 * D).rearrange("p (b k n) -> p b k n", b=2, k=KD)
        m += 2 * D
        yb = words(m, 2 * D).rearrange("p (b n) -> p b n", b=2)
        m += 2 * D
        assert m <= 36004, m
        NGB = 6
        gath = words(B0, NGB * D).rearrange("p (b n) -> p b n", b=NGB)
        route_at = [route0]

        def route(n, dt=F32):
            w = n if dt in (F32, I32, U32) else (n + 1) // 2
            v = words(route_at[0], w, dt)
            route_at[0] += w
            assert route_at[0] <= route1, (route_at, route1)
            return v

        lg = route(NT * 9).rearrange("p (t e) -> p t e", t=NT)
        mx8 = route(NT * 8).rearrange("p (t e) -> p t e", t=NT)
        ix8 = route(NT * 8, U32).rearrange("p (t e) -> p t e", t=NT)
        ixf = route(2 * NT).rearrange("p (k t) -> p k t", k=2)
        oh = route(2 * NT * NE).rearrange("p (k t e) -> p k t e", k=2, t=NT)
        picked = route(NT * NE, BF16).rearrange("p (t e) -> p t e", t=NT)
        ex = route(NT * NE).rearrange("p (t e) -> p t e", t=NT)
        ex2 = route(NT * 2).rearrange("p (t k) -> p t k", t=NT)
        esum = route(NT)
        erec = route(NT)
        pk = route(NT * 2).rearrange("p (t k) -> p t k", t=NT)
        psum2 = route(NT)
        prec = route(NT)
        gate = route(NT * 2).rearrange("p (t k) -> p t k", t=NT)
        alpha = route(NT)
        oma = route(NT)
        sgb = route(1)
        slotf = route(2 * NT).rearrange("p (k t) -> p k t", k=2)
        sloti = route(2 * NT, I32).rearrange("p (k t) -> p k t", k=2)
        slt_tmp = route(2 * NT * NE).rearrange("p (k t e) -> p k t e", k=2, t=NT)
        ecnt_i = route(2, I32)
        ech_b = route(2, BF16)
        estart = route(NE, BF16)
        eend = route(1)
        ecmp = route(NTM, BF16)
        etile_i = route(NTM, I32)
        eused_i = route(NE, I32)

        block = ctx.enter_context(nc.Block())
        tp, dv, sc, pl = nc.tensor, nc.vector, nc.scalar, nc.gpsimd
        rowsplit = [(0, T // 5 * 5 - 5), (T - 5, 5)]

        def rows_dma(q, to, frm, s):
            for a, n in rowsplit:
                q.dma_start(to[a:a + n], frm[a:a + n]).then_inc(s, 16)

        s_ws = sem("shared_weights_in")
        s_sgb = sem("sg_bias_in")
        s_xf = sem("xf_ready")
        s_lg = sem("logits_psum")
        s_picked = sem("picked")
        s_epre = sem("slot_psum")
        s_et = sem("tile_expert")
        s_sloti = sem("row_slots")
        s_rows = sem("rows_scattered")
        s_exin = sem("softmax_in")
        s_exout = sem("softmax_exp")
        s_sgp = sem("shared_gate_psum")
        s_sup = sem("shared_up_psum")
        s_ssil = sem("shared_silu")
        s_sh = sem("shared_h")
        s_shT = sem("shared_hT_psum")
        s_shTs = sem("shared_hT_sb")
        s_sdn = sem("shared_down_psum")
        s_sout = sem("shared_added")
        FT = O2.after(NT)
        s_ew = [[sem(f"expert_w{i}_in{b}") for i in range(3)] for b in range(2)]
        s_ewready = [sem(f"expert_w{i}_ready") for i in range(3)]
        s_xg = [sem(f"slot_rows_in{b}") for b in range(2)]
        s_g = sem("gate_psum")
        s_up = sem("up_psum")
        s_xt = sem("slot_xT_psum")
        s_ht = sem("hT_psum")
        s_y = sem("y_psum")
        s_silu = sem("silu_ready")
        s_xTs = sem("slot_xT_sb")
        s_ya = sem("y_copied_act")
        s_h = sem("h_ready")
        s_hTs = sem("hT_sb")
        s_yd = sem("y_copied_dve")
        s_yout = [sem(f"y_out{b}") for b in range(2)]
        s_gath = [sem(f"gathered{b}") for b in range(NGB)]
        s_comb = sem("combined")
        s_fout = sem("out_written")

        def over_tiles(eng, tile):
            tile(0, 0)
            tile(1, 1)
            with eng.Fori(1, NTM // 2 - 1) as i:
                tile(2 * i, 0)
                tile(2 * i + 1, 1)
            for j in range(NTM - 3, NTM):
                tile(j, j % 2)

        def first_two(j):
            return isinstance(j, int) and j < 2

        def use(j, b):
            return (j - b) // 2 + 1 if isinstance(j, int) else None

        def wait_use(eng, s, j, b, each, ago=0):
            if isinstance(j, int):
                eng.wait_ge(s, each * ((j - b) // 2 + 1 - ago))
            else:
                eng.wait_ge(s, (j - b) * (each // 2) + each * (1 - ago))

        def ffn_sync(sp):
            sp.wait_ge(s_hout, NT * (H1 + H2))
            sp.dma_start(rwx[:, :, 0:NE], router_w.rearrange("(k p) n -> p k n", p=P)).then_inc(s_ws, 16)
            sp.dma_start(rwx[:, :, NE:NE + 1], sg_w.rearrange("(k p) n -> p k n", p=P),
                         allow_slow_non_contiguous=True).then_inc(s_ws, 16)
            sp.dma_start(wsgu[:, :, 0:HS], ws_gate.rearrange("(k p) n -> p k n", p=P)).then_inc(s_ws, 16)
            sp.dma_start(wsgu[:, :, HS:2 * HS], ws_up.rearrange("(k p) n -> p k n", p=P)).then_inc(s_ws, 16)
            sp.dma_start(wsd[:, :, :], ws_down.rearrange("(k p) n -> p k n", p=P)).then_inc(s_ws, 16)
            sp.wait_ge(s_zero, 16 * NTM)
            sp.dma_start(sgb[0:T], sg_b.partition_broadcast(T)).then_inc(s_sgb, 16)

            def load_expert(e):
                for i, w in enumerate((w_gate, w_up, w_down)):
                    sp.dma_start(ew[e % 2][i], w[e].rearrange("(k p) n -> p k n", p=P)).then_inc(s_ew[e % 2][i], 16)

            sp.wait_ge(s_fin_taken, 2 * NT)
            load_expert(0)
            sp.wait_ge(s_rows, 16 * 2 * NT)
            sp.wait_ge(s_sdn, 2 * NT)
            sp.wait_ge(s_et, 1)
            load_expert(1)
            for e in range(2, NE):
                through = sp.value_load(eused_i[0:1, e - 1:e], min_val=1, max_val=NTM + 1)
                sp.wait_ge(s_y, through)
                load_expert(e)
            for t in range(NT):
                sp.wait_ge(s_comb, 2 * (t + 1))
                rows_dma(sp, out_rows[:, t], x2[0:T, t], s_fout)
            sp.wait_ge(s_fout, 32 * NT)

        def ffn_pool(pool):
            def expert_ready(e):
                for i in range(3):
                    pool.wait_ge(s_ew[e % 2][i], 16 * (e // 2 + 1))
                    if e:
                        pool.wait_ge(s_ewready[i], e)
                    pl.memset(junk8[0:1, 4 + i:5 + i], 0.0).then_inc(s_ewready[i], 1)

            pool.wait_ge(s_sloti, 1)
            pool.wait_ge(s_zero, 16 * NTM)
            pool.wait_ge(s_xf, NT)
            for t in range(NT):
                for k in range(2):
                    pl.indirect_dma_start(xg_dram[:, :], bass.IndirectOffsetOnAxis(ap=sloti[0:T, k, t:t + 1], axis=0),
                                          xf[0:T, t], None).then_inc(s_rows, 16)
            for e in range(NE):
                expert_ready(e)
            pool.wait_ge(s_yout[0], 16 * (NTM // 2 + 1))
            pool.wait_ge(s_yout[1], 16 * (NTM // 2))
            for q in range(2 * NT):
                if q >= NGB:
                    pool.wait_ge(s_comb, q - NGB + 1)
                pl.indirect_dma_start(gath[0:T, q % NGB], None, yg_dram[:, :],
                                      bass.IndirectOffsetOnAxis(ap=sloti[0:T, q % 2, q // 2:q // 2 + 1], axis=0))\
                    .then_inc(s_gath[q % NGB], 16)

        def ffn_pe(pe):
            pe.wait_ge(s_fin_taken, 2 * NT)
            for t in range(NT):
                pe.wait_ge(s_xf, t + 1)
                for hf in range(2):
                    q = 2 * t + hf
                    FT.wait_free(pe, q)
                    for i in range(3):
                        k = 3 * hf + i
                        ins = tp.transpose(ps[q % 4][:, i * T:(i + 1) * T], xf[0:T, t, k * P:(k + 1) * P], ident[0:T, 0:T])
                    FT.filled(ins)
            FT.wait_all_taken(pe, 2 * NT)
            pe.wait_ge(s_ws, 80)
            for t in range(NT):
                for k in range(KD):
                    ins = tp.matmul(ps[4][0:T, 9 * t:9 * t + 9], xfT[:, k, t * T:(t + 1) * T], rwx[:, k, :],
                                    start=(k == 0), stop=(k == KD - 1))
            ins.then_inc(s_lg, 1)

            def shared_up(t):
                b = 2 * (t % 2)
                if t >= 2:
                    pe.wait_ge(s_ssil, t - 1)
                for k in range(KD):
                    ins = tp.matmul(ps[b][0:T, 0:HS], xfT[:, k, t * T:(t + 1) * T], wsgu[:, k, 0:HS],
                                    start=(k == 0), stop=(k == KD - 1))
                ins.then_inc(s_sgp, 1)
                if t >= 2:
                    pe.wait_ge(s_sh, t - 1)
                for k in range(KD):
                    ins = tp.matmul(ps[b + 1][0:T, 0:HS], xfT[:, k, t * T:(t + 1) * T], wsgu[:, k, HS:2 * HS],
                                    start=(k == 0), stop=(k == KD - 1))
                ins.then_inc(s_sup, 1)

            def shared_down(t):
                pe.wait_ge(s_sh, t + 1)
                if t >= 2:
                    pe.wait_ge(s_shTs, t - 1)
                for k in range(KS):
                    ins = tp.transpose(ps[4 + t % 2][:, k * T:(k + 1) * T], sg_h[0:T, t % 2, k * P:(k + 1) * P], ident[0:T, 0:T])
                ins.then_inc(s_shT, 1)
                pe.wait_ge(s_shTs, t + 1)
                for hf in range(2):
                    if t >= 1:
                        pe.wait_ge(s_sout, 2 * (t - 1) + hf + 1)
                    for k in range(KS):
                        ins = tp.matmul(ps[6 + hf][0:T, 0:384], sg_hT[:, t % 2, k, :], wsd[:, k, hf * 384:(hf + 1) * 384],
                                        start=(k == 0), stop=(k == KS - 1))
                    ins.then_inc(s_sdn, 1)

            shared_up(0)
            pe.wait_ge(s_picked, 1)
            for t in range(NT):
                ins = tp.matmul(ps[6][0:NE, 0:1], picked[0:T, t, :], ones_b[0:T, 0:1], start=(t == 0), stop=(t == NT - 1))
            ins.then_inc(s_cnt, 1)
            shared_up(1)
            pe.wait_ge(s_chunks, 2)
            tp.matmul(ps[6][0:1, 8:8 + NE], ech_b[0:NE, 0:1], tri[0:NE, 0:NE], start=True, stop=True)
            tp.matmul(ps[6][0:NE, 16:17], triinc[0:NE, 0:NE], ech_b[0:NE, 0:1], start=True, stop=True).then_inc(s_starts, 1)
            pe.wait_ge(s_startrow, 2)
            o = ps[5][0:T, 0:NT * NE].rearrange("p (t e) -> p t e", t=NT)
            tp.matmul(o, tri[0:T, 0:T], picked[0:T], start=True, stop=False)
            for t in range(NT - 1):
                n = NT - 1 - t
                tp.matmul(o[:, t + 1:NT], ones_b[0:T, 0:T], picked[0:T, t:t + 1].to_broadcast([T, n, NE]),
                          start=False, stop=False)
            tp.matmul(o, ones_b[0:1, 0:T], estart[0:1, 0:NE].unsqueeze(1).to_broadcast([1, NT, NE]),
                      start=False, stop=True).then_inc(s_epre, 1)
            pe.wait_ge(s_cmp, 2)
            tp.matmul(ps[7][0:1, 0:NTM], ones_b[0:NE, 0:1], ecmp[0:NE, 0:NTM], start=True, stop=True).then_inc(s_bk, 1)
            pe.wait_ge(s_et, 1)
            pe.wait_ge(s_sloti, 1)
            shared_down(0)
            for t in range(2, NT):
                shared_up(t)
                shared_down(t - 1)
            shared_down(NT - 1)
            pe.wait_ge(s_sout, 2 * NT)

            def x_transposes(j, b):
                wait_use(pe, s_xg[b], j, b, 16)
                for i in range(2):
                    if not first_two(j):
                        pe.wait_ge(s_hTs, 2 * j - 3 + i)
                    for k in range(3):
                        ins = tp.transpose(ps[6 + i][:, k * P:(k + 1) * P], xgb[:, b, (3 * i + k) * P:(3 * i + k + 1) * P], ident)
                        if isinstance(j, int) and j == 0 and i == 0 and k == 0:
                            ins.then_inc(s_y, 1)
                    ins.then_inc(s_xt, 1)

            def tile(j, b):
                last = isinstance(j, int) and j == NTM - 1
                e = pe.value_load(etile_i[0:1, bass.ds(j, 1)], min_val=0, max_val=NE - 1)
                at = (1 - (e & 1)) * (WB[0] - WB[1]) + WB[1]
                pe.wait_ge(s_xTs, 2 * j + 2)
                pe.wait_ge(s_ewready[0], e + 1)
                for i in range(2):
                    if not (isinstance(j, int) and j == 0):
                        pe.wait_ge(s_silu, 2 * j - 1 + i)
                    for k in range(KD):
                        ins = tp.matmul(ps[i][:, 0:384], xgT[:, b, k], expert_cols(0, at, k, i * 384, 384),
                                        start=(k == 0), stop=(k == KD - 1))
                    ins.then_inc(s_g, 1)
                if not last:
                    x_transposes(j + 1, 1 - b)

                def up(i, ks):
                    for k in ks:
                        ins = tp.matmul(ps[2 + i][:, 0:384], xgT[:, b, k], expert_cols(1, at, k, i * 384, 384),
                                        start=(k == 0), stop=(k == KD - 1))
                    if k == KD - 1:
                        ins.then_inc(s_up, 1)

                def h_transposes(i):
                    if last:
                        pe.wait_ge(s_hTs, 2 * j)
                    else:
                        pe.wait_ge(s_xTs, 2 * j + 3 + i)
                    pe.wait_ge(s_h, 2 * j + 1 + i)
                    for k in range(3):
                        ins = tp.transpose(ps[6 + i][:, k * P:(k + 1) * P], hh[:, b, (3 * i + k) * P:(3 * i + k + 1) * P], ident)
                    ins.then_inc(s_ht, 1)

                def down(blocks):
                    for k in blocks:
                        for o in range(2):
                            ins = tp.matmul(ps[4 + o][:, 0:384], hT[:, b, k], expert_cols(2, at, k, o * 384, 384),
                                            start=(k == 0), stop=(k == KD - 1))
                    return ins

                pe.wait_ge(s_ewready[1], e + 1)
                if not (isinstance(j, int) and j == 0):
                    pe.wait_ge(s_h, 2 * j)
                up(0, range(KD))
                up(1, range(KD - 2))
                h_transposes(0)
                up(1, range(KD - 2, KD))
                pe.wait_ge(s_ewready[2], e + 1)
                if not (isinstance(j, int) and j == 0):
                    pe.wait_ge(s_ya, j)
                    pe.wait_ge(s_yd, j)
                pe.wait_ge(s_hTs, 2 * j + 1)
                down(range(2))
                h_transposes(1)
                down(range(2, 3))
                pe.wait_ge(s_hTs, 2 * j + 2)
                ins = down(range(3, KD))
                ins.then_inc(s_y, 1)

            x_transposes(0, 0)
            over_tiles(pe, tile)

        def ffn_act(act):
            act.wait_ge(s_stats, 3)
            sc.activation(std[0:T], mv[0:T, :, 1], ACT.Sqrt, bias=epst[0:T]).then_inc(s_std, 1)
            for t in range(NT):
                q = 2 * t
                FT.wait_filled(act, q)
                FT.taken(sc.activation(xfT[:, 0:3, t * T:(t + 1) * T],
                                       ps[q % 4][:, 0:3 * T].rearrange("p (k n) -> p k n", k=3), ACT.Copy), q)
            act.wait_ge(s_exin, 1)
            sc.activation(ex[0:T], ex[0:T], ACT.Exp)
            sc.activation(ex2[0:T], ex2[0:T], ACT.Exp).then_inc(s_exout, 1)
            act.wait_ge(s_sgb, 16)
            sc.activation(alpha[0:T], lg[0:T, :, NE], ACT.Sigmoid, bias=sgb[0:T]).then_inc(s_exout, 1)

            def shared_silu(t):
                act.wait_ge(s_sgp, t + 1)
                if t >= 2:
                    act.wait_ge(s_sh, t - 1)
                sc.activation(sg_s[0:T, t % 2], ps[2 * (t % 2)][0:T, 0:HS], ACT.Silu).then_inc(s_ssil, 1)

            def shared_hT(t):
                act.wait_ge(s_shT, t + 1)
                if t >= 2:
                    act.wait_ge(s_sdn, 2 * (t - 1))
                sc.activation(sg_hT[:, t % 2].rearrange("p k n -> p (k n)"), ps[4 + t % 2][:, 0:KS * T], ACT.Copy).then_inc(s_shTs, 1)

            shared_silu(0)
            shared_silu(1)
            shared_hT(0)
            for t in range(2, NT):
                shared_silu(t)
                shared_hT(t - 1)
            shared_hT(NT - 1)

            def load_x(j, b):
                act.dma_start(xgb[:, b], xg_dram[bass.ds(j * P, P)]).then_inc(s_xg[b], 16)

            def take_x(j, b):
                for i in range(2):
                    act.wait_ge(s_xt, 2 * j + 1 + i)
                    sc.activation(xgT[:, b, 3 * i:3 * i + 3].rearrange("p k n -> p (k n)"), ps[6 + i][:, 0:384],
                                  ACT.Copy).then_inc(s_xTs, 1)

            def tile(j, b):
                last = isinstance(j, int) and j == NTM - 1
                if not (isinstance(j, int) and j + 2 >= NTM):
                    load_x(j + 2, b)
                for i in range(2):
                    act.wait_ge(s_g, 2 * j + 1 + i)
                    sc.activation(gs[:, b, i * 384:(i + 1) * 384], ps[i][:, 0:384], ACT.Silu).then_inc(s_silu, 1)
                if not last:
                    take_x(j + 1, 1 - b)
                act.wait_ge(s_y, j + 2)
                if not first_two(j):
                    wait_use(act, s_yout[b], j, b, 16, ago=1)
                sc.activation(yb[:, b, 0:384], ps[4][:, 0:384], ACT.Copy).then_inc(s_ya, 1)
                act.wait_ge(s_ya, j + 1)
                act.wait_ge(s_yd, j + 1)
                act.dma_start(yg_dram[bass.ds(j * P, P)], yb[:, b]).then_inc(s_yout[b], 16)

            act.wait_ge(s_rows, 16 * 2 * NT)
            load_x(0, 0)
            load_x(1, 1)
            take_x(0, 0)
            over_tiles(act, tile)

        def ffn_dve(dve, step, mean_var):
            stt = dv.scalar_tensor_tensor
            mean_var().then_inc(s_stats, 1)
            dve.wait_ge(s_std, 3)
            step(dv.reciprocal(rstd[0:T], std[0:T]))
            step.wait()
            for t in range(NT):
                dv.tensor_scalar(xf[0:T, t], x2[0:T, t], mv[0:T, t, 0:1], rstd[0:T, t:t + 1], ALU.subtract, ALU.mult)\
                    .then_inc(s_xf, 1)
            for t in range(NT):
                q = 2 * t + 1
                FT.wait_filled(dve, q)
                FT.taken(dv.tensor_copy(xfT[:, 3:6, t * T:(t + 1) * T],
                                        ps[q % 4][:, 0:3 * T].rearrange("p (k n) -> p k n", k=3)), q)
            dve.wait_ge(s_lg, 1)
            dve.wait_ge(s_zero, 16 * NTM)
            step(dv.tensor_copy(lg[0:T], ps[4][0:T, 0:9 * NT].rearrange("p (t e) -> p t e", t=NT)))
            step.wait()
            for t in range(NT):
                step(dv.max(mx8[0:T, t], lg[0:T, t, 0:NE]))
            step.wait()
            for t in range(NT):
                step(dv.max_index(ix8[0:T, t], mx8[0:T, t], lg[0:T, t, 0:NE]))
            step.wait()
            step(dv.tensor_copy(ixf[0:T], ix8[0:T, :, 0:2].rearrange("p t k -> p k t")))
            step.wait()
            for k in range(2):
                step(dv.tensor_tensor(oh[0:T, k], iota[0:T, 0:NE].unsqueeze(1).to_broadcast([T, NT, NE]),
                                      ixf[0:T, k].unsqueeze(2).to_broadcast([T, NT, NE]), ALU.is_equal))
            step.wait()
            dv.tensor_tensor(picked[0:T], oh[0:T, 0], oh[0:T, 1], ALU.add).then_inc(s_picked, 1)
            m0 = mx8[0:T, :, 0:1]
            step(dv.tensor_tensor(ex[0:T], lg[0:T, :, 0:NE], m0.to_broadcast([T, NT, NE]), ALU.subtract))
            dv.tensor_tensor(ex2[0:T], mx8[0:T, :, 0:2], m0.to_broadcast([T, NT, 2]), ALU.subtract).then_inc(s_exin, 1)
            dve.wait_ge(s_cnt, 2)
            step(dv.tensor_scalar(ecnt_i[0:NE, 0:1], ps[6][0:NE, 0:1], float(P - 1), None, ALU.add))
            step.wait()
            step(dv.tensor_scalar(ecnt_i[0:NE, 1:2], ecnt_i[0:NE, 0:1], 7, None, ALU.arith_shift_right))
            step.wait()
            dv.tensor_copy(ech_b[0:NE, 0:1], ecnt_i[0:NE, 1:2]).then_inc(s_chunks, 1)
            dve.wait_ge(s_starts, 2)
            dv.tensor_scalar(estart[0:1], ps[6][0:1, 8:8 + NE], float(P), None, ALU.mult).then_inc(s_startrow, 1)
            step(dv.tensor_copy(eend[0:NE], ps[6][0:NE, 16:17]))
            step.wait()
            dv.tensor_scalar(ecmp[0:NE, 0:NTM], iota[0:NE, 0:NTM], eend[0:NE], None, ALU.is_ge).then_inc(s_cmp, 1)
            dve.wait_ge(s_epre, 1)
            slots = ps[5][0:T, 0:NT * NE].rearrange("p (t e) -> p t e", t=NT)
            for k in range(2):
                step(dv.tensor_tensor(slt_tmp[0:T, k], slots, oh[0:T, k], ALU.mult))
            step.wait()
            step(dv.tensor_reduce(slotf[0:T], slt_tmp[0:T], AX.X, ALU.add))
            step.wait()
            dv.tensor_copy(sloti[0:T], slotf[0:T]).then_inc(s_sloti, 1)
            dve.wait_ge(s_bk, 2)
            step(dv.tensor_scalar(eused_i[0:1], ps[6][0:1, 8:8 + NE], 1.0, None, ALU.add))
            step.wait()
            dv.tensor_scalar(etile_i[0:1], ps[7][0:1, 0:NTM], float(NE - 1), None, ALU.min).then_inc(s_et, 1)
            dve.wait_ge(s_exout, 2)
            step(dv.tensor_reduce(esum[0:T], ex[0:T], AX.X, ALU.add))
            step.wait()
            step(dv.reciprocal(erec[0:T], esum[0:T]))
            step.wait()
            step(dv.tensor_tensor(pk[0:T], ex2[0:T], erec[0:T].unsqueeze(2).to_broadcast([T, NT, 2]), ALU.mult))
            step.wait()
            step(dv.tensor_reduce(psum2[0:T], pk[0:T], AX.X, ALU.add))
            step.wait()
            step(dv.reciprocal(prec[0:T], psum2[0:T]))
            step(dv.tensor_scalar(oma[0:T], alpha[0:T], -1.0, 1.0, ALU.mult, ALU.add))
            step.wait()
            step(dv.tensor_tensor(prec[0:T], prec[0:T], oma[0:T], ALU.mult))
            step.wait()
            step(dv.tensor_tensor(gate[0:T], pk[0:T], prec[0:T].unsqueeze(2).to_broadcast([T, NT, 2]), ALU.mult))

            def shared_h(t):
                dve.wait_ge(s_ssil, t + 1)
                dve.wait_ge(s_sup, t + 1)
                if t >= 2:
                    dve.wait_ge(s_shT, t - 1)
                dv.tensor_tensor(sg_h[0:T, t % 2], ps[2 * (t % 2) + 1][0:T, 0:HS], sg_s[0:T, t % 2], ALU.mult).then_inc(s_sh, 1)

            def shared_out(t):
                for hf in range(2):
                    dve.wait_ge(s_sdn, 2 * t + hf + 1)
                    cols = x2[0:T, t, hf * 384:(hf + 1) * 384]
                    stt(out=cols, in0=ps[6 + hf][0:T, 0:384], scalar=alpha[0:T, t:t + 1], in1=cols,
                        op0=ALU.mult, op1=ALU.add).then_inc(s_sout, 1)

            shared_h(0)
            shared_h(1)
            shared_out(0)
            for t in range(2, NT):
                shared_h(t)
                shared_out(t - 1)
            shared_out(NT - 1)

            def tile(j, b):
                for i in range(2):
                    dve.wait_ge(s_silu, 2 * j + 1 + i)
                    dve.wait_ge(s_up, 2 * j + 1 + i)
                    dv.tensor_tensor(hh[:, b, i * 384:(i + 1) * 384], ps[2 + i][:, 0:384], gs[:, b, i * 384:(i + 1) * 384],
                                     ALU.mult).then_inc(s_h, 1)
                    dve.wait_ge(s_ht, 2 * j + 1 + i)
                    dv.tensor_copy(hT[:, b, 3 * i:3 * i + 3].rearrange("p k n -> p (k n)"), ps[6 + i][:, 0:384]).then_inc(s_hTs, 1)
                dve.wait_ge(s_y, j + 2)
                if not first_two(j):
                    wait_use(dve, s_yout[b], j, b, 16, ago=1)
                dv.tensor_copy(yb[:, b, 384:768], ps[5][:, 0:384]).then_inc(s_yd, 1)

            over_tiles(dve, tile)
            step.wait()
            dve.wait_ge(s_sout, 2 * NT)
            for q in range(2 * NT):
                t, k = q // 2, q % 2
                dve.wait_ge(s_gath[q % NGB], 16 * (q // NGB + 1))
                if k:
                    dve.wait_ge(s_comb, q)
                stt(out=x2[0:T, t], in0=gath[0:T, q % NGB], scalar=gate[0:T, t, k:k + 1], in1=x2[0:T, t],
                    op0=ALU.mult, op1=ALU.add).then_inc(s_comb, 1)

        @block.sync
        def _(sp):
            sp.dma_start(src_i.bitcast(I32)[0:T], src.rearrange("(p c) -> p c", p=T)).then_inc(s_edges, 16)
            sp.dma_start(dst_i.bitcast(I32)[0:T], dst.rearrange("(p c) -> p c", p=T)).then_inc(s_edges, 16)
            for g in range(5):
                rows_dma(sp, xs[0:T, 2 * g:2 * g + 2], x_rows[:, 2 * g:2 * g + 2], s_x[g])
            sp.dma_start(avec[:, 0:D], a_src1.rearrange("h c -> (h c)").partition_broadcast(P)).then_inc(s_avec, 16)
            sp.dma_start(avec[:, D:2 * D], a_dst1.rearrange("h c -> (h c)").partition_broadcast(P)).then_inc(s_avec, 16)
            for hf in range(2):
                sp.dma_start(w1x[:, :, hf, 0:384], W1[:, hf * 384:(hf + 1) * 384].rearrange("(k p) n -> p k n", p=P)).then_inc(s_w1, 16)
            XT.wait_all_taken(sp, 4 * NT)
            sp.dma_start(wkv[:, :, :], w_qkv[:, D:3 * D].rearrange("(k p) n -> p k n", p=P)).then_inc(s_wkv, 16)
            HH.wait_all_taken(sp, 2 * NT)
            sp.dma_start(wq[:, :, :], w_qkv[:, 0:D].rearrange("(k p) n -> p k n", p=P)).then_inc(s_wq, 16)
            sp.wait_ge(s_slot, 1)
            sp.wait_ge(s_bk, 1)
            sp.dma_start(biasb, bu.partition_broadcast(P)).then_inc(s_bias, 16)
            sp.dma_start(bias2, b_proj.partition_broadcast(P)).then_inc(s_bias, 16)
            sp.wait_ge(s_scat, 16 * EC)
            sp.dma_start(vtab, edge_table.rearrange("(p c) a -> p (c a)", p=P)).then_inc(s_tabin, 16)

            def load_wout(hf):
                for i, w in enumerate((Wu[0:D], w_proj)):
                    sp.dma_start(wout[hf][:, i * KD:(i + 1) * KD],
                                 w[:, hf * 384:(hf + 1) * 384].rearrange("(k p) n -> p k n", p=P)).then_inc(s_wout[hf], 16)

            sp.wait_ge(s_kready, 2 * NT)
            sp.wait_ge(s_vready, 2 * NT)
            sp.wait_ge(s_kvused, NT)
            load_wout(0)
            sp.wait_ge(s_den, KD * DG)
            load_wout(1)
            sp.wait_ge(s_mixT, KD * DG)
            sp.dma_start(w2x[:, :, 0:192], W2.rearrange("(k p) n -> p k n", p=P)).then_inc(s_w2, 16)
            sp.dma_start(avec2[:, 0:192], a_src2.rearrange("h c -> (h c)").partition_broadcast(P)).then_inc(s_w2, 16)
            sp.dma_start(avec2[:, 192:384], a_dst2.rearrange("h c -> (h c)").partition_broadcast(P)).then_inc(s_w2, 16)
            for q in range(2 * NT):
                hf, t = q // NT, q % NT
                sp.wait_ge(s_mixrow, q + 1)
                rows_dma(sp, mixed_dram.rearrange("(t p) d -> p t d", p=T)[:, t, hf * 384:(hf + 1) * 384],
                         mrow[0:T, q % 2], s_mixout[q % 2])
            OT.wait_all_taken(sp, 2 * NT)
            for h in range(H2):
                sp.dma_start(wub[h][0:C2], Wu[D + h * C2:D + (h + 1) * C2]).then_inc(s_wub, 16)
            for i in range(2):
                sp.wait_ge(s_mixout[i], 32 * NT)
            for t in range(NT):
                if t >= 2:
                    sp.wait_ge(s_resadd, t - 1)
                rows_dma(sp, mixin[0:T, t], mixed_dram.rearrange("(t p) d -> p t d", p=T)[:, t], s_res[t % 2])
                rows_dma(sp, xin[0:T, t % 2], x_rows[:, t], s_res[t % 2])
            ffn_sync(sp)

        @block.gpsimd
        def _(pool):
            step = Chain(pool, s_pool)
            step(pl.memset(ident, 0.0))
            pl.memset(ones, 1.0).then_inc(s_const, 1)
            pl.memset(zeros, 0.0).then_inc(s_const, 1)
            pl.memset(ones_b, 1.0).then_inc(s_const, 1)
            pl.memset(epst, EPS).then_inc(s_const, 1)
            step(pl.memset(tri, 1.0))
            step(pl.memset(triinc, 1.0))
            step(pl.memset(later, 1.0))
            step(pl.iota(iota_i, pattern=[[1, G]], base=0, channel_multiplier=0))
            step.wait()
            pl.affine_select(out=ident, in_=ident, compare_op=ALU.not_equal, fill=1.0, base=0,
                             pattern=[[-1, P]], channel_multiplier=1).then_inc(s_const, 1)
            pl.affine_select(out=tri, in_=tri, compare_op=ALU.is_ge, fill=0.0, base=-1,
                             pattern=[[1, P]], channel_multiplier=-1).then_inc(s_const, 1)
            pl.affine_select(out=triinc, in_=triinc, compare_op=ALU.is_ge, fill=0.0, base=0,
                             pattern=[[1, P]], channel_multiplier=-1).then_inc(s_const, 1)
            pl.affine_select(out=later, in_=later, compare_op=ALU.is_ge, fill=0.0, base=-1,
                             pattern=[[1, EC]], channel_multiplier=-1).then_inc(s_const, 1)
            pl.tensor_copy(iota, iota_i).then_inc(s_const, 1)
            pl.tensor_copy(iota_h[:, 0:G], iota_i).then_inc(s_const, 1)
            pl.memset(invalid, P * SRS).then_inc(s_invmem, 1)
            pool.wait_ge(s_invmem, 1)
            pl.dma_start(edge_table.rearrange("(p c) a -> p (c a)", p=P), invalid).then_inc(s_inval, 16)
            pool.wait_ge(s_inval, 16)
            pool.wait_ge(s_slot, 1)
            for c in range(EC):
                pl.indirect_dma_start(edge_table[:, :], bass.IndirectOffsetOnAxis(ap=slot_i[0:T, c:c + 1], axis=0),
                                      edge_v[0:T, c:c + 1], None).then_inc(s_scat, 16)
            for t in range(NT):
                pool.wait_ge(s_res[t % 2], 64 * (t // 2 + 1))
                pl.tensor_tensor(mixin[0:T, t], mixin[0:T, t], xin[0:T, t % 2], ALU.add).then_inc(s_resadd, 1)
            ffn_pool(pool)

        @block.tensor
        def _(pe):
            def transposes(which):
                for t in range(NT):
                    pe.wait_ge(s_xn, NT + 1 if which else t + 1)
                    for hf in range(2):
                        q = (which * NT + t) * 2 + hf
                        XT.wait_free(pe, q)
                        for i in range(3):
                            k = 3 * hf + i
                            ins = tp.matmul(ps[q % 4][:, i * T:(i + 1) * T], xs[0:T, t, k * P:(k + 1) * P],
                                            rescale[0:T, t] if which else ident[0:T, 0:T], start=True, stop=True)
                        XT.filled(ins)

            def edge_counts():
                pe.wait_ge(s_br, 1)
                tp.matmul(ps[4][0:NBK, 32:33], tot0[:, :], ones_b[:, 0:1], start=True, stop=False)
                tp.matmul(ps[4][0:NBK, 32:33], tot1[0:EC1, :], ones_b[0:EC1, 0:1], start=False, stop=True).then_inc(s_cnt, 1)

            def edge_starts():
                pe.wait_ge(s_chunks, 1)
                tp.matmul(ps[5][0:1, 0:NBK], chb.bitcast(BF16)[0:NBK, 0:1], tri[0:NBK, 0:NBK], start=True, stop=True)
                tp.matmul(ps[5][0:NBK, 32:33], triinc[0:NBK, 0:NBK], chb.bitcast(BF16)[0:NBK, 0:1],
                          start=True, stop=True).then_inc(s_starts, 1)

            def edge_rank(j):
                if j == 0:
                    pe.wait_ge(s_startrow, 1)
                if j >= 2:
                    pe.wait_ge(s_rankfree, j - 1)
                o = ps[6 + j % 2][0:T, 0:RC * NBK]
                cs = slice(RC * j, RC * j + RC)
                tp.matmul(o, tri[0:T, 0:T], onehot[0:T, cs, :], start=True, stop=False)
                tp.matmul(o, ones_b[:, 0:T], base0[:, cs, :], start=False, stop=False)
                if RC * j >= P:
                    c1 = slice(RC * j - P, RC * j - P + RC)
                    tp.matmul(o, ones_b[0:EC1, 0:T], base1[0:EC1, c1, :], start=False, stop=False)
                tp.matmul(o, ones_b[0:1, 0:T], startrow[0:1, 0:NBK].unsqueeze(1).to_broadcast([1, RC, NBK]),
                          start=False, stop=True).then_inc(s_rank, 1)

            def chunk_buckets():
                pe.wait_ge(s_cmp, 1)
                tp.matmul(ps[4][0:1, 64:64 + NCH], ones_b[0:NBK, 0:1], cmpb[0:NBK, 0:NCH], start=True, stop=True).then_inc(s_bk, 1)

            pe.wait_ge(s_const, 10)
            transposes(0)
            transposes(1)
            pe.wait_ge(s_oh, 1)
            for b in range(NBK):
                tp.matmul(ps[4][:, b:b + 1], onehot[0:T, 0:P, b], ones_b[0:T, 0:1], start=True, stop=True)
            for b in range(NBK):
                ins = tp.matmul(ps[5][0:EC1, b:b + 1], onehot[0:T, P:EC, b], ones_b[0:T, 0:1], start=True, stop=True)
            ins.then_inc(s_tot, 1)
            XT.wait_all_taken(pe, 4 * NT)
            pe.wait_ge(s_wa, 1)
            pe.wait_ge(s_w1, 32)
            for t in range(NT):
                for hf in range(2):
                    q = 2 * t + hf
                    HH.wait_free(pe, q)
                    for k in range(KD):
                        ins = tp.matmul(ps[q % 4][0:T, 0:388], xmT[:, k, t * T:(t + 1) * T], w1x[:, k, hf, :],
                                        start=(k == 0), stop=(k == KD - 1))
                    HH.filled(ins)
                if t == 0:
                    edge_counts()
                elif t == 1:
                    edge_starts()
                elif 2 * t - 3 <= RJ:
                    edge_rank(2 * t - 4)
                    edge_rank(2 * t - 3)
                if 2 * t - 2 == RJ:
                    chunk_buckets()
            HH.wait_all_taken(pe, 2 * NT)
            pe.wait_ge(s_wkv, 16)

            def kv_accumulate(t):
                pe.wait_ge(s_kfeat, 2 * t + 2)
                pe.wait_ge(s_vsb, 2 * t + 2)
                for pr in range(KD):
                    ins = tp.matmul(ps[4 + pr // 3][:, (pr % 3) * 129:(pr % 3) * 129 + 129],
                                    kbuf[0:T, t % 2, pr * P:(pr + 1) * P], vbuf[0:T, t % 2, pr, :],
                                    start=(t == 0 and pr % 3 == 0), stop=(t == NT - 1 and pr % 3 == 2),
                                    skip_group_check=True)
                ins.then_inc(s_kvused, 1)

            for t in range(NT):
                for hf in range(2):
                    if t >= 1:
                        pe.wait_ge(s_kexp, 2 * (t - 1) + hf + 1)
                    for k in range(KD):
                        ins = tp.matmul(ps[hf][0:T, 0:384], xnT[:, k, t * T:(t + 1) * T],
                                        wkv[:, k, hf * 384:(hf + 1) * 384], start=(k == 0), stop=(k == KD - 1))
                    ins.then_inc(s_kready, 1)
                for hf in range(2):
                    if t >= 1:
                        pe.wait_ge(s_vsb, 2 * (t - 1) + hf + 1)
                    for k in range(KD):
                        ins = tp.matmul(ps[2 + hf][0:T, 0:384], xnT[:, k, t * T:(t + 1) * T],
                                        wkv[:, k, D + hf * 384:D + (hf + 1) * 384], start=(k == 0), stop=(k == KD - 1))
                    ins.then_inc(s_vready, 1)
                if t >= 1:
                    kv_accumulate(t - 1)
            kv_accumulate(NT - 1)
            pe.wait_ge(s_wq, 16)
            steps = [(mb, i) for mb in range(KD) for i in range(DG)]

            def attend(s):
                mb, i = steps[s]
                n0, n = NG[i]
                if s >= 2:
                    pe.wait_ge(s_mixT, s - 1)
                pe.wait_ge(s_qfeat, s + 1)
                tp.matmul(ps[6 + s % 2][:, 0:n], ksb[:, mb, :], qbuf[:, s % 2, 0:n], start=True, stop=True)
                tp.matmul(ps[2 + s % 2][:, 0:n], kvb[:, mb, :], qbuf[:, s % 2, 0:n], start=True, stop=True).then_inc(s_den, 1)

            def chunk_products(i):
                for j in range(2 * i, min(2 * i + 2, NCH)):
                    pe.wait_ge(s_ohb, j + 1)
                    if j >= 2:
                        pe.wait_ge(s_acc, j - 1)
                    tp.matmul(ps[4 + j % 2][0:T, 0:G], ohs[:, j % 4, 0:T], ohd[:, j % 4, 0:G],
                              start=True, stop=True).then_inc(s_cps, 1)

            pe.wait_ge(s_kexp, 2 * NT)
            pe.wait_ge(s_vsb, 2 * NT)
            pair = 0
            for s, (mb, i) in enumerate(steps):
                n0, n = NG[i]
                if s >= 2:
                    pe.wait_ge(s_qexp, s - 1)
                for k in range(KD):
                    ins = tp.matmul(ps[s % 2][:, 0:n], wq[:, k, mb * P:(mb + 1) * P], xnT[:, k, n0:n0 + n],
                                    start=(k == 0), stop=(k == KD - 1))
                ins.then_inc(s_qpsum, 1)
                if s == 0:
                    pe.wait_ge(s_kvblk, 1)
                if s >= len(steps) - NPQ:
                    chunk_products(pair)
                    pair += 1
                if s >= 1:
                    attend(s - 1)
            attend(len(steps) - 1)
            pe.wait_ge(s_mixT, len(steps))
            for q in range(2 * NT):
                hf, t = q // NT, q % NT
                if t == 0:
                    pe.wait_ge(s_wout[hf], 32)
                if q >= 2:
                    pe.wait_ge(s_mixrow, q - 1)
                for k in range(2 * KD):
                    lhs = (xnT if k < KD else mixT)[:, k % KD, t * T:(t + 1) * T]
                    ins = tp.matmul(ps[q % 2][0:T, 0:384], lhs, wout[hf][:, k, :], start=(k == 0), stop=(k == 2 * KD - 1))
                    if k == 2 * KD - 1:
                        ins.then_inc(s_mixps, 1)
                    if k % 3 == 2:
                        chunk_products(pair)
                        pair += 1
            assert 2 * pair >= NCH
            pe.wait_ge(s_mixrow, 2 * NT)
            pe.wait_ge(s_acc, NCH)
            for st in range(NT):
                pe.wait_ge(s_cf, st + 1)
                if st >= 2:
                    pe.wait_ge(s_mask, 3 * (st - 1))
                for dt in range(NT):
                    bank = ps[(st % 2) * 4 + dt // 4]
                    ins = tp.transpose(bank[0:T, (dt % 4) * T:(dt % 4 + 1) * T],
                                       tbuf[0:T, st % 2, dt * T:(dt + 1) * T], ident[0:T, 0:T])
                ins.then_inc(s_mskT, 1)
            pe.wait_ge(s_mask, 3 * NT)

            def row_to_banks(r):
                pe.wait_ge(s_diag, r + 1)
                for i in range(DG):
                    if r:
                        pe.wait_ge(s_row, 3 * (r - 1) + i + 1)
                    tp.matmul(ps[i][:, 0:NG[i][1]], ones[0:T, :], diags[0:T, r % 2, NG[i][0]:NG[i][0] + NG[i][1]],
                              start=True, stop=True).then_inc(s_rowps, 1)

            def heads(layer, H, C, hsrc, first):
                row_to_banks(row_no("s", first))
                for n in range(first, first + H):
                    row_to_banks(row_no("a", n))
                    row_to_banks(row_no("b", n))
                    if n + 1 < first + H:
                        row_to_banks(row_no("s", n + 1))
                    if n:
                        pe.wait_ge(s_hout, NT * n)
                    for st in range(NT):
                        j = n * NT + st
                        pe.wait_ge(s_pt, j + 1)
                        for dt in range(NT):
                            o = ps[3 + dt // 2][0:T, (dt % 2) * (C + 1):(dt % 2 + 1) * (C + 1)]
                            ins = tp.matmul(o, ptile[0:T, j % NPT, dt * T:(dt + 1) * T], hsrc[0:T, st, n - first, :],
                                            start=(st == 0 and dt % 2 == 0), stop=(st == NT - 1 and dt % 2 == 1),
                                            skip_group_check=True)
                        ins.then_inc(s_ptused, 1)

            heads(1, H1, C1, h1, 0)
            pe.wait_ge(s_hout, NT * H1)
            for t in range(NT):
                for hf in range(2):
                    q = 2 * t + hf
                    OT.wait_free(pe, q)
                    c0 = hf * 384
                    for i in range(3):
                        c = c0 + i * P
                        if c // C1 == (c + P - 1) // C1:
                            ins = tp.transpose(ps[q % 4][:, i * T:(i + 1) * T],
                                               out1[c // C1][0:T, t, c % C1:c % C1 + P], ident[0:T, 0:T])
                        else:
                            a, n = c // C1, C1 - c % C1
                            tp.matmul(ps[q % 4][0:n, i * T:(i + 1) * T], out1[a][0:T, t, c % C1:C1], ident[0:T, 0:T],
                                      start=True, stop=True)
                            ins = tp.matmul(ps[q % 4][n:P, i * T:(i + 1) * T], out1[a + 1][0:T, t, 0:P - n],
                                            ident[0:T, 0:T], start=True, stop=True)
                    OT.filled(ins)
            OT.wait_all_taken(pe, 2 * NT)
            pe.wait_ge(s_wa2, 1)
            for t in range(NT):
                H2H.wait_free(pe, t)
                for k in range(KD):
                    ins = tp.matmul(ps[t % 4][0:T, 0:196], out1T[:, k, t * T:(t + 1) * T], w2x[:, k, :],
                                    start=(k == 0), stop=(k == KD - 1))
                H2H.filled(ins)
            H2H.wait_all_taken(pe, NT)
            pe.wait_ge(s_h2ones, 1)
            heads(2, H2, C2, h2, H1)
            pe.wait_ge(s_hout, NT * (H1 + H2))
            for t in range(NT):
                O2.wait_free(pe, t)
                for h in range(H2):
                    ins = tp.transpose(ps[t % 4][0:C2, h * T:(h + 1) * T], out2[0:T, t, h, :], ident[0:T, 0:T])
                O2.filled(ins)
            O2.wait_all_taken(pe, NT)
            pe.wait_ge(s_wub, 32)
            for t in range(NT):
                for hf in range(2):
                    q = 2 * t + hf
                    if q >= 2:
                        pe.wait_ge(s_fin_taken, q - 1)
                    for h in range(H2):
                        ins = tp.matmul(ps[q % 2][0:T, 0:384], out2T[0:C2, h, t * T:(t + 1) * T],
                                        wub[h][0:C2, hf * 384:(hf + 1) * 384], start=(h == 0), stop=(h == H2 - 1))
                    ins.then_inc(s_fin, 1)
            ffn_pe(pe)

        @block.scalar
        def _(act):
            def take_xT(which):
                for t in range(NT):
                    q = (which * NT + t) * 2
                    XT.wait_filled(act, q)
                    if which == 0:
                        XT.taken(sc.activation(xnT[:, 0:3, t * T:(t + 1) * T],
                                               ps[q % 4][:, 0:3 * T].rearrange("p (k n) -> p k n", k=3), ACT.Copy), q)
                    else:
                        for i in range(3):
                            ins = sc.activation(xmT[:, i, t * T:(t + 1) * T], ps[q % 4][:, i * T:(i + 1) * T],
                                                ACT.Identity, scale=gcol[:, i:i + 1], bias=bcol[:, i:i + 1])
                        XT.taken(ins, q)

            act.dma_start(gcol, norm_g.rearrange("(k p) -> p k", p=P), allow_slow_non_contiguous=True).then_inc(s_gb, 16)
            act.dma_start(bcol, norm_b.rearrange("(k p) -> p k", p=P), allow_slow_non_contiguous=True).then_inc(s_gb, 16)
            act.dma_start(b1col, b1.rearrange("(k p) -> p k", p=P), allow_slow_non_contiguous=True).then_inc(s_gb, 16)
            act.dma_start(b2col[0:C2], b2.rearrange("(h p) -> p h", p=C2), allow_slow_non_contiguous=True).then_inc(s_b2, 16)
            act.wait_ge(s_const, 10)
            for j in range(NTM):
                act.dma_start(xg_dram[j * P:(j + 1) * P], zeros).then_inc(s_zero, 16)
            act.wait_ge(s_stats, 1)
            sc.activation(std[0:T], mv[0:T, :, 1], ACT.Sqrt, bias=epst[0:T]).then_inc(s_std, 1)
            act.wait_ge(s_stats, 2)
            sc.activation(std2[0:T], var2[0:T], ACT.Sqrt, bias=epst[0:T]).then_inc(s_std, 1)
            take_xT(0)
            act.wait_ge(s_gb, 48)
            take_xT(1)

            def take_h1(q):
                t = q // 2
                HH.wait_filled(act, q)
                sc.activation(h1[0:T, t, 0:2, 0:C1], ps[q % 4][0:T, 0:384].rearrange("p (h c) -> p h c", h=2), ACT.Copy)
                HH.taken(sc.activation(s1[0:T, t, 0].rearrange("p s a -> p (s a)"), ps[q % 4][0:T, 384:388], ACT.Copy), q)
            act.wait_ge(s_inval, 16)
            for t in range(NT):
                take_h1(2 * t)
            for t in range(NT):
                for hf in range(2):
                    act.wait_ge(s_kready, 2 * t + hf + 1)
                    if 2 * t + hf >= 2:
                        act.wait_ge(s_kfeat, 2 * t + hf - 1)
                    sc.activation(ebuf[0:T, hf, 0:384], ps[hf][0:T, 0:384], ACT.Exp)
                    sc.activation(rbuf[0:T, hf, 0:384], ps[hf][0:T, 0:384], ACT.Relu).then_inc(s_kexp, 1)
            for s in range(KD * DG):
                n = NG[s % DG][1]
                act.wait_ge(s_qpsum, s + 1)
                act.wait_ge(s_kfeat, 2 * NT)
                if s >= 2:
                    act.wait_ge(s_qfeat, s - 1)
                sc.activation(ebuf[:, s % 2, 0:n], ps[s % 2][:, 0:n], ACT.Exp)
                sc.activation(rbuf[:, s % 2, 0:n], ps[s % 2][:, 0:n], ACT.Relu).then_inc(s_qexp, 1)

            for st in range(NT):
                if st >= 2:
                    act.wait_ge(s_mskT, st - 1)
                elif st == 0:
                    act.wait_ge(s_mixrow, 2 * NT)
                    act.wait_ge(s_acc, NCH)
                sc.activation(tbuf[0:T, st % 2], counts[0:T, st, 0:N], ACT.Copy).then_inc(s_cf, 1)

            def copy_row(kind, n):
                r = row_no(kind, n)
                for i in range(DG):
                    act.wait_ge(s_rowps, 3 * r + i + 1)
                    sc.activation(rowbuf[:, "sab".index(kind), NG[i][0]:NG[i][0] + NG[i][1]], ps[i][:, 0:NG[i][1]],
                                  ACT.Copy).then_inc(s_row, 1)

            def heads(H, first):
                copy_row("s", first)
                for n in range(first, first + H):
                    if n:
                        act.wait_ge(s_t, NT * n)
                    copy_row("a", n)
                    copy_row("b", n)
                    act.wait_ge(s_row, 3 * row_no("b", n) + 3)

                    def lower(st):
                        j = n * NT + st
                        if j >= 2:
                            act.wait_ge(s_t, j - 1)
                        sc.activation(ubuf[0:T, j % 2], rowbuf[0:T, 2], ACT.Identity, bias=s02[0:T, n % 2, st:st + 1]).then_inc(s_u, 1)

                    lower(0)
                    if n + 1 < first + H:
                        copy_row("s", n + 1)
                    for st in range(NT):
                        j = n * NT + st
                        if st + 1 < NT:
                            lower(st + 1)
                        act.wait_ge(s_t, j + 1)
                        sc.activation(tbuf[0:T, j % 2], tbuf[0:T, j % 2], ACT.Exp).then_inc(s_e, 1)

            heads(H1, 0)
            for t in range(NT):
                q = 2 * t
                OT.wait_filled(act, q)
                for i in range(3):
                    ins = sc.activation(out1T[:, i, t * T:(t + 1) * T], ps[q % 4][:, i * T:(i + 1) * T],
                                        ACT.Identity, bias=b1col[:, i:i + 1])
                OT.taken(ins, q)
            for t in range(0, NT, 2):
                H2H.wait_filled(act, t)
                sc.activation(h2[0:T, t, :, 0:C2], ps[t % 4][0:T, 0:192].rearrange("p (h c) -> p h c", h=2), ACT.Copy)
                H2H.taken(sc.activation(s2[0:T, t].rearrange("p s a -> p (s a)"), ps[t % 4][0:T, 192:196], ACT.Copy), t)
            heads(H2, H1)
            for t in range(0, NT, 2):
                O2.wait_filled(act, t)
                act.wait_ge(s_b2, 16)
                for h in range(H2):
                    ins = sc.activation(out2T[0:C2, h, t * T:(t + 1) * T], ps[t % 4][0:C2, h * T:(h + 1) * T],
                                        ACT.Identity, bias=b2col[0:C2, h:h + 1])
                O2.taken(ins, t)
            ffn_act(act)

        @block.vector
        def _(dve):
            step = Chain(dve, s_dve)
            stt = dv.scalar_tensor_tensor

            dve.wait_ge(s_edges, 32)
            dve.wait_ge(s_const, 10)
            step(dv.tensor_copy(src_f[0:T], src_i.bitcast(I32)[0:T]))
            step(dv.tensor_copy(dst_f[0:T], dst_i.bitcast(I32)[0:T]))
            step.wait()
            step(dv.tensor_scalar(st_f[0:T], src_f[0:T], float(T), None, ALU.is_ge))
            step(dv.tensor_scalar(dg_f[0:T], dst_f[0:T], float(G), None, ALU.is_ge))
            for k in range(2, NT):
                step.wait()
                step(stt(out=st_f[0:T], in0=src_f[0:T], scalar=float(k * T), in1=st_f[0:T], op0=ALU.is_ge, op1=ALU.add))
            for k in range(2, DG):
                step.wait()
                step(stt(out=dg_f[0:T], in0=dst_f[0:T], scalar=float(k * G), in1=dg_f[0:T], op0=ALU.is_ge, op1=ALU.add))
            step.wait()
            step(stt(out=src_f[0:T], in0=st_f[0:T], scalar=-float(T), in1=src_f[0:T], op0=ALU.mult, op1=ALU.add))
            step(stt(out=dst_f[0:T], in0=dg_f[0:T], scalar=-float(G), in1=dst_f[0:T], op0=ALU.mult, op1=ALU.add))
            step(stt(out=st_f[0:T], in0=st_f[0:T], scalar=float(DG), in1=dg_f[0:T], op0=ALU.mult, op1=ALU.add))
            step.wait()
            step(stt(out=src_f[0:T], in0=src_f[0:T], scalar=float(SRS), in1=dst_f[0:T], op0=ALU.mult, op1=ALU.add))
            step.wait()
            dv.tensor_copy(edge_v[0:T], src_f[0:T])
            dv.tensor_tensor(onehot[0:T], iota[0:T, 0:NBK].unsqueeze(1).to_broadcast([T, EC, NBK]),
                             st_f[0:T].unsqueeze(2).to_broadcast([T, EC, NBK]), ALU.is_equal).then_inc(s_oh, 1)
            def row_stats(xt, t):
                for i in range(2):
                    ins = dv.bn_stats(stats[0:T, t, 6 * i:6 * i + 6], xt[0:T, t, i * 384:(i + 1) * 384])
                step(ins)

            def mean_var():
                step.wait()
                for t in range(NT):
                    ins = dv.bn_aggr(mv[0:T, t, :], stats[0:T, t, :])
                return ins

            for t in range(NT):
                if t % 2 == 0:
                    dve.wait_ge(s_x[t // 2], 32)
                row_stats(xs, t)
            mean_var().then_inc(s_stats, 1)
            dve.wait_ge(s_std, 1)
            step(dv.reciprocal(rstd[0:T], std[0:T]))
            step.wait()
            step(dv.tensor_tensor(var2[0:T], mv[0:T, :, 1], rstd[0:T], ALU.mult))
            step.wait()
            dv.tensor_tensor(var2[0:T], var2[0:T], rstd[0:T], ALU.mult).then_inc(s_stats, 1)
            for t in range(NT):
                dv.tensor_scalar(xs[0:T, t], xs[0:T, t], mv[0:T, t, 0:1], rstd[0:T, t:t + 1], ALU.subtract, ALU.mult)\
                    .then_inc(s_xn, 1)
            dve.wait_ge(s_std, 2)
            step(dv.reciprocal(rstd2[0:T], std2[0:T]))
            step.wait()
            dv.tensor_tensor(rescale[0:T], ident[0:T, 0:T].unsqueeze(1).to_broadcast([T, NT, T]),
                             rstd2[0:T].unsqueeze(2).to_broadcast([T, NT, T]), ALU.mult).then_inc(s_xn, 1)
            for t in range(NT):
                q = 2 * t + 1
                XT.wait_filled(dve, q)
                XT.taken(dv.tensor_copy(xnT[:, 3:6, t * T:(t + 1) * T],
                                        ps[q % 4][:, 0:3 * T].rearrange("p (k n) -> p k n", k=3)), q)
            dve.wait_ge(s_gb, 48)
            for t in range(NT):
                q = (NT + t) * 2 + 1
                XT.wait_filled(dve, q)
                for i in range(3):
                    ins = dv.tensor_scalar(xmT[:, 3 + i, t * T:(t + 1) * T], ps[q % 4][:, i * T:(i + 1) * T],
                                           gcol[:, 3 + i:4 + i], bcol[:, 3 + i:4 + i], ALU.mult, ALU.add)
                XT.taken(ins, q)
            dve.wait_ge(s_avec, 32)
            dve.wait_ge(s_w1, 32)
            for k in range(KD):
                for h in range(H1):
                    for s in range(2):
                        step.wait(but=3)
                        ins = dv.tensor_tensor_reduce(ttr_junk[:, (2 * h + s) % 4], w1x[:, k, h // 2, (h % 2) * C1:(h % 2 + 1) * C1],
                                                      avec[:, s * D + h * C1:s * D + (h + 1) * C1], 1.0, 0.0,
                                                      ALU.mult, ALU.add, w1x[:, k, h // 2, 384 + 2 * s + h % 2:385 + 2 * s + h % 2])
                        step(ins)
            step.wait()
            dv.memset(junk8[:, 0:1], 0.0).then_inc(s_wa, 1)
            def edge_totals():
                dve.wait_ge(s_tot, 1)
                step(dv.tensor_copy(tot0, ps[4][:, 0:NBK]))
                step(dv.tensor_copy(tot1[0:EC1], ps[5][0:EC1, 0:NBK]))
                step.wait()
                dv.tensor_tensor(base0, tot0.unsqueeze(1).to_broadcast([P, EC, NBK]),
                                 later.unsqueeze(2).to_broadcast([P, EC, NBK]), ALU.mult)
                dv.tensor_tensor(base1[0:EC1], tot1[0:EC1].unsqueeze(1).to_broadcast([EC1, EC1, NBK]),
                                 tri[0:EC1, 0:EC1].unsqueeze(2).to_broadcast([EC1, EC1, NBK]), ALU.mult).then_inc(s_br, 1)

            def bucket_chunks():
                dve.wait_ge(s_cnt, 1)
                chi = chb.bitcast(I32)
                step(dv.tensor_scalar(chi[0:NBK, 1:2], ps[4][0:NBK, 32:33], float(P - 1), None, ALU.add))
                step.wait()
                step(dv.tensor_scalar(chi[0:NBK, 2:3], chi[0:NBK, 1:2], 7, None, ALU.arith_shift_right))
                step.wait()
                dv.tensor_copy(chb.bitcast(BF16)[0:NBK, 0:1], chi[0:NBK, 2:3]).then_inc(s_chunks, 1)

            def bucket_starts():
                dve.wait_ge(s_starts, 1)
                dv.tensor_scalar(startrow[0:1, 0:NBK], ps[5][0:1, 0:NBK], float(P), None, ALU.mult).then_inc(s_startrow, 1)
                step(dv.tensor_copy(junk8[0:NBK, 0:1], ps[5][0:NBK, 32:33]))
                step.wait()
                dv.tensor_scalar(cmpb[0:NBK, 0:NCH], iota[0:NBK, 0:NCH], junk8[0:NBK, 0:1], None, ALU.is_ge).then_inc(s_cmp, 1)

            def edge_rank(j):
                dve.wait_ge(s_rank, j + 1)
                cs = slice(RC * j, RC * j + RC)
                step.wait(but=1)
                ins = dv.tensor_tensor(rank_tmp[0:T, j % 2], ps[6 + j % 2][0:T, 0:RC * NBK].rearrange("p (c b) -> p c b", c=RC),
                                       onehot[0:T, cs, :], ALU.mult)
                ins.then_inc(s_rankfree, 1)
                dve.wait_ge(s_rankfree, j + 1)
                step(dv.tensor_reduce(rank[0:T, cs], rank_tmp[0:T, j % 2], AX.X, ALU.add))

            def edge_slots():
                step.wait()
                step(dv.tensor_copy(slot_i[0:T], rank[0:T]))
                step.wait()
                step(dv.tensor_scalar(src_i.bitcast(I32)[0:T], slot_i[0:T], P - 1, None, ALU.bitwise_and))
                step(dv.tensor_scalar(dst_i.bitcast(I32)[0:T], slot_i[0:T], 7, None, ALU.arith_shift_right))
                step.wait()
                stt(out=slot_i[0:T], in0=src_i.bitcast(I32)[0:T], scalar=float(NCH), in1=dst_i.bitcast(I32)[0:T],
                    op0=ALU.mult, op1=ALU.add).then_inc(s_slot, 1)
                dve.wait_ge(s_bk, 1)
                dv.tensor_scalar(offs_i[0:1], ps[4][0:1, 64:64 + NCH], float(NBK - 1), float(G), ALU.min, ALU.mult).then_inc(s_offs, 1)

            dve.wait_ge(s_wa, 1)
            dve.wait_ge(s_inval, 16)
            dv.memset(h1[0:T, :, :, C1:C1 + 1], 1.0).then_inc(s_h1ones, 1)

            def take_h1(t):
                q = 2 * t + 1
                HH.wait_filled(dve, q)
                dv.tensor_copy(h1[0:T, t, 2:4, 0:C1], ps[q % 4][0:T, 0:384].rearrange("p (h c) -> p h c", h=2))
                HH.taken(dv.tensor_copy(s1[0:T, t, 1].rearrange("p s a -> p (s a)"), ps[q % 4][0:T, 384:388]), q)

            edge_totals()
            for t in range(NT):
                take_h1(t)
                if t == 0:
                    bucket_chunks()
                elif t == 1:
                    bucket_starts()
                elif 2 * t - 3 <= RJ:
                    edge_rank(2 * t - 4)
                    edge_rank(2 * t - 3)
                if 2 * t - 2 == RJ:
                    edge_slots()
            HH.wait_all_taken(dve, 2 * NT)
            step(dv.memset(vbuf[0:T, :, :, P:P + 1], 1.0))
            step.wait()
            for t in range(NT):
                for hf in range(2):
                    dve.wait_ge(s_kexp, 2 * t + hf + 1)
                    if t >= 2:
                        dve.wait_ge(s_kvused, t - 1)
                    stt(out=kbuf[0:T, t % 2, hf * 384:(hf + 1) * 384], in0=ebuf[0:T, hf, 0:384], scalar=1.0,
                        in1=rbuf[0:T, hf, 0:384], op0=ALU.min, op1=ALU.add).then_inc(s_kfeat, 1)
                for hf in range(2):
                    dve.wait_ge(s_vready, 2 * t + hf + 1)
                    dv.tensor_copy(vbuf[0:T, t % 2, 3 * hf:3 * hf + 3, 0:P],
                                   ps[2 + hf][0:T, 0:384].rearrange("p (k n) -> p k n", k=3)).then_inc(s_vsb, 1)
            dve.wait_ge(s_bias, 32)
            step(dv.tensor_tensor(biasb, biasb, bias2, ALU.add))
            step.wait()
            step(dv.memset(kvb, 0.0))
            step(dv.memset(ksb, 0.0))
            step.wait()
            dve.wait_ge(s_kvused, NT)
            for b in range(2):
                acc = ps[4 + b][:, 0:387].rearrange("p (k n) -> p k n", k=3)
                for hd in range(2):
                    r = slice(64 * hd, 64 * hd + 64)
                    dv.tensor_copy(kvb[r, 3 * b:3 * b + 3, 64 * hd:64 * hd + 64], acc[r, :, 64 * hd:64 * hd + 64])
                    ins = dv.tensor_copy(ksb[r, 3 * b:3 * b + 3, 64 * hd:64 * hd + 64],
                                         acc[r, :, 128:129].to_broadcast([64, 3, 64]))
            ins.then_inc(s_kvblk, 1)

            def mix_out(s):
                mb, i = s // DG, s % DG
                n0, n = NG[i]
                dve.wait_ge(s_den, s + 1)
                if s:
                    dve.wait_ge(s_mixT, s)
                step(dv.reciprocal(dbuf[:, 0:n], ps[6 + s % 2][:, 0:n]))
                step.wait()
                dv.tensor_tensor(mixT[:, mb, n0:n0 + n], ps[2 + s % 2][:, 0:n], dbuf[:, 0:n], ALU.mult).then_inc(s_mixT, 1)

            dve.wait_ge(s_kready, 2 * NT)
            dve.wait_ge(s_vready, 2 * NT)
            step(dv.memset(counts_flat[0:T], 0))
            dve.wait_ge(s_tabin, 16)
            step(dv.tensor_scalar(vtmp, vtab, 9, None, ALU.arith_shift_right))
            step(dv.tensor_scalar(vtab, vtab, SRS - 1, None, ALU.bitwise_and))
            step.wait()
            step(dv.tensor_copy(srow, vtmp))
            step(dv.tensor_copy(dcol, vtab))
            for t in range(NT):
                step(dv.tensor_copy(counts[0:T, t, t * T:(t + 1) * T], ident[0:T, 0:T]))
            step.wait()

            def onehots(j):
                if j >= NCH:
                    return
                if j >= 4:
                    dve.wait_ge(s_cps, j - 3)
                dv.tensor_scalar(ohs[:, j % 4, 0:T], iota_h[:, 0:T], srow[:, j:j + 1], None, ALU.is_equal)
                dv.tensor_scalar(ohd[:, j % 4, 0:G], iota_h[:, 0:G], dcol[:, j:j + 1], None, ALU.is_equal)\
                    .then_inc(s_ohb, 1)

            def count_pair(i):
                for j in range(2 * i, min(2 * i + 2, NCH)):
                    off = dve.value_load(offs_i[0:1, j:j + 1], min_val=0, max_val=(NBK - 1) * G)
                    o = counts_flat[0:T, bass.ds(off, G)]
                    dve.wait_ge(s_cps, j + 1)
                    if j:
                        dve.wait_ge(s_acc, j)
                    dv.tensor_tensor(o, o, ps[4 + j % 2][0:T, 0:G], ALU.add).then_inc(s_acc, 1)
                    onehots(j + 2)

            dve.wait_ge(s_offs, 1)
            onehots(0)
            onehots(1)
            pair = 0
            for s in range(KD * DG):
                n = NG[s % DG][1]
                dve.wait_ge(s_qexp, s + 1)
                if s >= 2:
                    dve.wait_ge(s_den, s - 1)
                stt(out=qbuf[:, s % 2, 0:n], in0=ebuf[:, s % 2, 0:n], scalar=1.0, in1=rbuf[:, s % 2, 0:n],
                    op0=ALU.min, op1=ALU.add).then_inc(s_qfeat, 1)
                if s >= KD * DG - NPQ:
                    count_pair(pair)
                    pair += 1
                if s >= 1:
                    mix_out(s - 1)
            mix_out(KD * DG - 1)
            for q in range(2 * NT):
                hf = q // NT
                for i in range(3):
                    count_pair(pair)
                    pair += 1
                dve.wait_ge(s_mixps, q + 1)
                if q >= 2:
                    dve.wait_ge(s_mixout[q % 2], 32 * (q // 2))
                dv.tensor_tensor(mrow[0:T, q % 2], ps[q % 2][0:T, 0:384],
                                 biasb[0:T, hf * 384:(hf + 1) * 384], ALU.add).then_inc(s_mixrow, 1)
                count_pair(pair)
                pair += 1
            dve.wait_ge(s_acc, NCH)
            for st in range(NT):
                dve.wait_ge(s_mskT, st + 1)
                for i, (a, n) in enumerate([(0, 4), (4, 4), (8, 2)]):
                    dv.tensor_scalar(mask[0:T, a:a + n, st * T:(st + 1) * T],
                                     ps[(st % 2) * 4 + i][0:T, 0:n * T].rearrange("p (d m) -> p d m", d=n), 0.0, MASKED,
                                     ALU.is_equal, ALU.mult).then_inc(s_mask, 1)
            dve.wait_ge(s_mask, 3 * NT)
            dve.wait_ge(s_w2, 48)
            for k in range(KD):
                for h in range(H2):
                    for s in range(2):
                        step.wait(but=3)
                        ins = dv.tensor_tensor_reduce(junk[:, s, h * C2:(h + 1) * C2], w2x[:, k, h * C2:(h + 1) * C2],
                                                      avec2[:, s * 192 + h * C2:s * 192 + (h + 1) * C2], 1.0, 0.0,
                                                      ALU.mult, ALU.add, w2x[:, k, 192 + 2 * s + h:193 + 2 * s + h])
                        step(ins)
            step.wait()
            dv.memset(junk8[:, 3:4], 0.0).then_inc(s_wa2, 1)
            dve.wait_ge(s_wa2, 1)

            def heads(H, C, first, score, dest):

                def diag(kind, n, col):
                    r = row_no(kind, n)
                    if r >= 2:
                        dve.wait_ge(s_rowps, 3 * (r - 1))
                    dv.tensor_tensor(diags[0:T, r % 2].rearrange("p (t m) -> p t m", t=NT),
                                     ident[0:T, 0:T].unsqueeze(1).to_broadcast([T, NT, T]),
                                     col.unsqueeze(2).to_broadcast([T, NT, T]), ALU.mult).then_inc(s_diag, 1)

                def largest(n, dt):
                    if dt == 0:
                        dve.wait_ge(s_row, 3 * row_no("s", n) + 3)
                    step.wait(but=1)
                    step(dv.tensor_tensor_reduce(junk[0:T, dt % 2], mask[0:T, dt], rowbuf[0:T, 0], 1.0, -3.0e38,
                                                 ALU.add, ALU.max, smax[0:T, dt:dt + 1]))

                def dst_rows(n):
                    ssrc, sdst = score(n - first)
                    step.wait()
                    step(dv.tensor_tensor(zt[0:T], smax[0:T], sdst, ALU.add))
                    step(dv.tensor_scalar(s02[0:T, n % 2], ssrc, SLOPE, None, ALU.mult))
                    step.wait()
                    step(stt(out=mt[0:T], in0=zt[0:T], scalar=SLOPE, in1=zt[0:T], op0=ALU.mult, op1=ALU.max))
                    step.wait()
                    dve.wait_ge(s_diag, row_no("a", n))
                    step(dv.tensor_tensor(arow[0:T], sdst, mt[0:T], ALU.subtract))
                    step(stt(out=brow[0:T], in0=sdst, scalar=SLOPE, in1=mt[0:T], op0=ALU.mult, op1=ALU.subtract))
                    step.wait()
                    diag("a", n, arow[0:T])
                    diag("b", n, brow[0:T])

                def rows_out(n):
                    dve.wait_ge(s_ptused, NT * (n + 1))
                    if n == 0:
                        for i in range(2):
                            dve.wait_ge(s_mixout[i], 32 * NT)
                    else:
                        dve.wait_ge(s_hout, NT * n)
                    for b in range(NT // 2):
                        step(dv.reciprocal(rec[0:T, 2 * b:2 * b + 2],
                                           ps[3 + b][0:T, 0:2 * (C + 1)].rearrange("p (d c) -> p d c", d=2)[:, :, C]))
                    step.wait()
                    for dt in range(NT):
                        dv.tensor_scalar(dest(n - first, dt), ps[3 + dt // 2][0:T, (dt % 2) * (C + 1):(dt % 2) * (C + 1) + C],
                                         rec[0:T, dt:dt + 1], None, ALU.mult).then_inc(s_hout, 1)

                def weigh(n, st):
                    j = n * NT + st
                    dve.wait_ge(s_e, j + 1)
                    if j >= NPT:
                        dve.wait_ge(s_ptused, j - NPT + 1)
                    stt(out=ptile[0:T, j % NPT], in0=tbuf[0:T, j % 2], scalar=1.0, in1=counts[0:T, st, 0:N],
                        op0=ALU.min, op1=ALU.mult).then_inc(s_pt, 1)

                diag("s", first, score(0)[0])
                for dt in range(NT):
                    largest(first, dt)
                for n in range(first, first + H):
                    more = n + 1 < first + H
                    dst_rows(n)
                    if more:
                        diag("s", n + 1, score(n + 1 - first)[0])
                    if n > first:
                        rows_out(n - 1)
                    ssrc = score(n - first)[0]
                    for st in range(NT):
                        j = n * NT + st
                        dve.wait_ge(s_u, j + 1)
                        if st == 0:
                            dve.wait_ge(s_row, 3 * row_no("b", n) + 3)
                        if j >= 2:
                            dve.wait_ge(s_pt, j - 1)
                        stt(out=tbuf[0:T, j % 2], in0=rowbuf[0:T, 1], scalar=ssrc[:, st:st + 1], in1=ubuf[0:T, j % 2],
                            op0=ALU.add, op1=ALU.max).then_inc(s_t, 1)
                        if st >= 1:
                            weigh(n, st - 1)
                        if more:
                            largest(n + 1, st)
                    weigh(n, NT - 1)
                rows_out(first + H - 1)

            heads(H1, C1, 0, lambda h: (s1[0:T, :, h // 2, 0, h % 2], s1[0:T, :, h // 2, 1, h % 2]),
                  lambda h, dt: out1[h][0:T, dt])
            for t in range(NT):
                q = 2 * t + 1
                OT.wait_filled(dve, q)
                for i in range(3):
                    ins = dv.tensor_scalar(out1T[:, 3 + i, t * T:(t + 1) * T], ps[q % 4][:, i * T:(i + 1) * T],
                                           b1col[:, 3 + i:4 + i], None, ALU.add)
                OT.taken(ins, q)
            dv.memset(h2[0:T, :, :, C2:C2 + 1], 1.0).then_inc(s_h2ones, 1)
            for t in range(1, NT, 2):
                H2H.wait_filled(dve, t)
                dv.tensor_copy(h2[0:T, t, :, 0:C2], ps[t % 4][0:T, 0:192].rearrange("p (h c) -> p h c", h=2))
                H2H.taken(dv.tensor_copy(s2[0:T, t].rearrange("p s a -> p (s a)"), ps[t % 4][0:T, 192:196]), t)
            H2H.wait_all_taken(dve, NT)
            heads(H2, C2, H1, lambda h: (s2[0:T, :, 0, h], s2[0:T, :, 1, h]), lambda h, dt: out2[0:T, dt, h])
            dve.wait_ge(s_b2, 16)
            for t in range(1, NT, 2):
                O2.wait_filled(dve, t)
                for h in range(H2):
                    ins = dv.tensor_scalar(out2T[0:C2, h, t * T:(t + 1) * T], ps[t % 4][0:C2, h * T:(h + 1) * T],
                                           b2col[0:C2, h:h + 1], None, ALU.add)
                O2.taken(ins, t)
            for t in range(NT):
                dve.wait_ge(s_resadd, t + 1)
                if t * D + D > CW16:
                    dve.wait_ge(s_fin_taken, 4)
                for hf in range(2):
                    q = 2 * t + hf
                    dve.wait_ge(s_fin, q + 1)
                    dv.tensor_tensor(x2[0:T, t, hf * 384:(hf + 1) * 384], ps[q % 2][0:T, 0:384],
                                     mixin[0:T, t, hf * 384:(hf + 1) * 384], ALU.add).then_inc(s_fin_taken, 1)
                dve.wait_ge(s_fin_taken, 2 * t + 2)
                row_stats(x2, t)
            ffn_dve(dve, step, mean_var)


_INS = ['x', 'src', 'dst', 'L0_gnn_norm_g', 'L0_gnn_norm_b', 'L0_gnn_W1', 'L0_gnn_a_src1', 'L0_gnn_a_dst1', 'L0_gnn_b1',
        'L0_gnn_W2', 'L0_gnn_a_src2', 'L0_gnn_a_dst2', 'L0_gnn_b2', 'L0_gnn_Wu', 'L0_gnn_bu', 'L0_mix_w_qkv',
        'L0_mix_w_proj', 'L0_mix_b_proj', 'L0_ffn_router_w', 'L0_ffn_w_gate', 'L0_ffn_w_up', 'L0_ffn_w_down',
        'L0_ffn_ws_gate', 'L0_ffn_ws_up', 'L0_ffn_ws_down', 'L0_ffn_sg_w', 'L0_ffn_sg_b']
_OUTS = [((1250, 768), 'float32')]


def kernel(**inputs):
    import numpy as _np
    import concourse.bacc as _bacc
    from concourse import mybir as _mybir
    from concourse.bass_utils import run_bass_kernel_spmd as _run

    nc = _bacc.Bacc("TRN2", target_bir_lowering=False, num_devices=1)
    arrays, args = {}, []
    for name in _INS:
        a = _np.ascontiguousarray(inputs[name])
        arrays[f"in_{name}_dram"] = a
        args.append(nc.dram_tensor(f"in_{name}_dram", a.shape, _mybir.dt.from_np(a.dtype), kind="ExternalInput").ap())
    for i, (shape, dtype) in enumerate(_OUTS):
        dt = _mybir.dt.from_np(_np.dtype(dtype))
        args.append(nc.dram_tensor(f"out_{i}_dram", shape, dt, kind="ExternalOutput").ap())
    gps_layer(nc, *args)
    r = _run(nc, [arrays], core_ids=[0])
    got = tuple(r.results[0][f"out_{i}_dram"] for i in range(len(_OUTS)))
    return got[0]
```
